# Optimizing a Trainium2 kernel written in Bass

```python
import numpy as np
import jax
import jax.numpy as jnp

def _softmax(x, axis=-1):
    return jax.nn.softmax(x, axis=axis)

def _gelu(x):
    return jax.nn.gelu(x, approximate=True)

def _silu(x):
    return jax.nn.silu(x)

def _sigmoid(x):
    return jax.nn.sigmoid(x)

def _layernorm(x, axis=-1, eps=1e-05):
    m = jnp.mean(x, axis=axis, keepdims=True)
    v = jnp.var(x, axis=axis, keepdims=True)
    return (x - m) / jnp.sqrt(v + eps)

def _scatter_add(tgt, idx, src, axis=0):
    return tgt.at[idx].add(src)

def _segment_sum(src, seg, n):
    return jax.ops.segment_sum(src, seg, n)
kernel_name = 'mk_macaron_d1_jaxref_r8_a25a58'

def setup_inputs(seed: int=0):
    np.random.seed(seed)
    _w = jnp.asarray

    def _L0_attn_setup():
        import jax, jax.numpy as jnp
        import numpy as np
        HIDDEN = 128
        N_HEADS = 16
        HEAD_DIM = HIDDEN // N_HEADS
        WINDOW = 32
        HALF_W = WINDOW // 2
        GLOBAL_TOKENS = (0,)

        def _longformer_mask(seq_len: int) -> jnp.ndarray:
            idx = jnp.arange(seq_len)
            mask = jnp.abs(idx[:, None] - idx[None, :]) <= HALF_W
            for g in GLOBAL_TOKENS:
                if 0 <= g < seq_len:
                    mask = mask.at[g, :].set(True)
                    mask = mask.at[:, g].set(True)
            return mask
        key = jax.random.key(seed)
        ks = jax.random.split(key, 5)
        B, S = (1, 512)
        scale = 0.02
        return {'x': jax.random.normal(ks[0], (B, S, HIDDEN), dtype=jnp.float32), 'Wq': jax.random.normal(ks[1], (HIDDEN, HIDDEN), dtype=jnp.float32) * scale, 'Wk': jax.random.normal(ks[2], (HIDDEN, HIDDEN), dtype=jnp.float32) * scale, 'Wv': jax.random.normal(ks[3], (HIDDEN, HIDDEN), dtype=jnp.float32) * scale, 'Wo': jax.random.normal(ks[4], (HIDDEN, HIDDEN), dtype=jnp.float32) * scale}
    _L0_attn_in = _L0_attn_setup()

    def _L0_ffn_setup():
        import jax, jax.numpy as jnp
        import numpy as np
        TOP_K = 2

        def _moe(x, Wr, br, W1, b1, W2, b2):
            B, S, D = x.shape
            E = Wr.shape[1]
            xt = x.reshape(-1, D)
            logits = xt @ Wr + br
            top_vals, top_idx = jax.lax.top_k(logits, TOP_K)
            mask = jnp.zeros_like(logits, dtype=bool).at[jnp.arange(xt.shape[0])[:, None], top_idx].set(True)
            sparse_logits = jnp.where(mask, logits, -jnp.inf)
            gate = jax.nn.softmax(sparse_logits, axis=-1)
            h = jax.nn.relu(jnp.einsum('td,edh->teh', xt, W1) + b1)
            y = jnp.einsum('teh,ehd->ted', h, W2) + b2
            out = jnp.einsum('ted,te->td', y, gate)
            return out.reshape(B, S, D)
        key = jax.random.key(seed)
        ks = jax.random.split(key, 5)
        B, S, D, E, H = (2, 256, 128, 8, 512)
        scale = 1.0 / np.sqrt(D)
        return {'x': jax.random.normal(ks[0], (B, S, D), dtype=jnp.float32), 'Wr': jax.random.normal(ks[1], (D, E), dtype=jnp.float32) * scale, 'br': jnp.zeros((E,), dtype=jnp.float32), 'W1': jax.random.normal(ks[2], (E, D, H), dtype=jnp.float32) * scale, 'b1': jnp.zeros((E, H), dtype=jnp.float32), 'W2': jax.random.normal(ks[3], (E, H, D), dtype=jnp.float32) * (1.0 / np.sqrt(H)), 'b2': jnp.zeros((E, D), dtype=jnp.float32)}
    _L0_ffn_in = _L0_ffn_setup()
    _d = {'L0_attn_x': _L0_attn_in['x'], 'L0_attn_Wq': _L0_attn_in['Wq'], 'L0_attn_Wk': _L0_attn_in['Wk'], 'L0_attn_Wv': _L0_attn_in['Wv'], 'L0_attn_Wo': _L0_attn_in['Wo'], 'L0_ffn_Wr': _L0_ffn_in['Wr'], 'L0_ffn_br': _L0_ffn_in['br'], 'L0_ffn_W1': _L0_ffn_in['W1'], 'L0_ffn_b1': _L0_ffn_in['b1'], 'L0_ffn_W2': _L0_ffn_in['W2'], 'L0_ffn_b2': _L0_ffn_in['b2']}
    _x0 = _d['L0_attn_x']
    _d['L0_attn_x'] = jax.random.normal(jax.random.fold_in(jax.random.key(seed), 1), (16, 256, 128), dtype=_x0.dtype)
    del _x0
    return _d

def reference(L0_attn_x, L0_attn_Wq, L0_attn_Wk, L0_attn_Wv, L0_attn_Wo, L0_ffn_Wr, L0_ffn_br, L0_ffn_W1, L0_ffn_b1, L0_ffn_W2, L0_ffn_b2):

    def _L0_attn_ref(x, Wq, Wk, Wv, Wo):
        import jax, jax.numpy as jnp
        import numpy as np
        HIDDEN = 128
        N_HEADS = 16
        HEAD_DIM = HIDDEN // N_HEADS
        WINDOW = 32
        HALF_W = WINDOW // 2
        GLOBAL_TOKENS = (0,)

        def _longformer_mask(seq_len: int) -> jnp.ndarray:
            idx = jnp.arange(seq_len)
            mask = jnp.abs(idx[:, None] - idx[None, :]) <= HALF_W
            for g in GLOBAL_TOKENS:
                if 0 <= g < seq_len:
                    mask = mask.at[g, :].set(True)
                    mask = mask.at[:, g].set(True)
            return mask
        B, S, H = x.shape
        scale = HEAD_DIM ** (-0.5)

        def proj(W):
            return jnp.einsum('bsh,oh->bso', x, W).reshape(B, S, N_HEADS, HEAD_DIM).transpose(0, 2, 1, 3)
        q, k, v = (proj(Wq), proj(Wk), proj(Wv))
        scores = jnp.einsum('bnsd,bntd->bnst', q, k) * scale
        mask = _longformer_mask(S)
        scores = jnp.where(mask[None, None], scores, jnp.float32(-jnp.inf))
        attn = jax.nn.softmax(scores, axis=-1)
        out = jnp.einsum('bnst,bntd->bnsd', attn, v)
        out = out.transpose(0, 2, 1, 3).reshape(B, S, H)
        return jnp.einsum('bsh,oh->bso', out, Wo)

    def _L0_ffn_ref(x, Wr, br, W1, b1, W2, b2):
        import jax, jax.numpy as jnp
        import numpy as np
        TOP_K = 2

        def _moe(x, Wr, br, W1, b1, W2, b2):
            B, S, D = x.shape
            E = Wr.shape[1]
            xt = x.reshape(-1, D)
            logits = xt @ Wr + br
            top_vals, top_idx = jax.lax.top_k(logits, TOP_K)
            mask = jnp.zeros_like(logits, dtype=bool).at[jnp.arange(xt.shape[0])[:, None], top_idx].set(True)
            sparse_logits = jnp.where(mask, logits, -jnp.inf)
            gate = jax.nn.softmax(sparse_logits, axis=-1)
            h = jax.nn.relu(jnp.einsum('td,edh->teh', xt, W1) + b1)
            y = jnp.einsum('teh,ehd->ted', h, W2) + b2
            out = jnp.einsum('ted,te->td', y, gate)
            return out.reshape(B, S, D)
        return _moe(x, Wr, br, W1, b1, W2, b2)
    x = L0_attn_x
    x = x + 0.5 * _L0_ffn_ref(_layernorm(x, axis=-1), L0_ffn_Wr, L0_ffn_br, L0_ffn_W1, L0_ffn_b1, L0_ffn_W2, L0_ffn_b2)
    x = x + _L0_attn_ref(_layernorm(x, axis=-1), L0_attn_Wq, L0_attn_Wk, L0_attn_Wv, L0_attn_Wo)
    x = x + 0.5 * _L0_ffn_ref(_layernorm(x, axis=-1), L0_ffn_Wr, L0_ffn_br, L0_ffn_W1, L0_ffn_b1, L0_ffn_W2, L0_ffn_b2)
    return x

_drawn_inputs = setup_inputs


def setup_inputs(seed=0):
    import zlib

    import numpy as np

    out = dict(_drawn_inputs(seed))
    spreads = {'L0_ffn_br': (0.0, 0.1), 'L0_ffn_b1': (0.0, 0.1), 'L0_ffn_b2': (0.0, 0.1)}
    factors = {'L0_attn_Wq': 8.0, 'L0_attn_Wk': 8.0, 'L0_attn_Wv': 3.402, 'L0_attn_Wo': 3.518}
    for name, (base, spread) in spreads.items():
        noise = np.random.default_rng([zlib.crc32(name.encode()), seed]).standard_normal(out[name].shape)
        drawn = base * np.exp(spread * noise) if base else spread * noise
        out[name] = jnp.asarray(drawn.astype(out[name].dtype))
    for name, factor in factors.items():
        out[name] = (out[name] * factor).astype(out[name].dtype)
    return out
```

```python
from contextlib import ExitStack

import concourse.bass as bass
from concourse import mybir

ALU = mybir.AluOpType
ACT = mybir.ActivationFunctionType
AX = mybir.AxisListType
F32 = mybir.dt.float32
F16 = mybir.dt.float16
BF16 = mybir.dt.bfloat16
I32 = mybir.dt.int32

P = 128
TOK = 512
WSCALE = 64.0
EPS = 1e-5
BIG = 3.0e38
NOT_SEEN = -1.0e30


def macaron_kernel(nc, x, Wq, Wk, Wv, Wo, Wr, br, W1, b1, W2, b2, out):
    B, S, D = x.shape
    E, _, H = W1.shape
    NT = B * S // P
    TT = TOK // P
    NC = NT // TT
    HC = H // P
    STEPS = NC * E
    HD, NH, WIN = 8, 16, 16
    HP, HG = 4, 4
    QB = 32
    NQ = S // QB
    NT_B = S // P
    NM = NT_B * NH
    PADS = S + 2 * WIN
    SLOTS = 9
    x_v = x.rearrange("b s d -> (b s) d").rearrange("(n p) d -> p n d", p=P)
    out_v = out.rearrange("b s d -> (b s) d").rearrange("(n p) d -> p n d", p=P)

    with ExitStack() as ctx:
        def sb(name, shape, dt=F32):
            return ctx.enter_context(nc.sbuf_tensor(name, shape, dt))

        def sem(name):
            return ctx.enter_context(nc.semaphore(name))

        xres = sb("xres", [P, NT, D])
        w1f = sb("w1f", [P, E, H])
        w1h, w1l = sb("w1h", [P, E, H], F16), sb("w1l", [P, E, H], F16)
        w2f = sb("w2f", [P, E, HC, D])
        w2h, w2l = sb("w2h", [P, E, HC, D], F16), sb("w2l", [P, E, HC, D], F16)
        b1n = sb("b1n", [E * HC, P])
        b1T = sb("b1T", [P, E, HC])
        wr = sb("wr", [P, E])
        br_bc = sb("br_bc", [P, E])
        b2s = sb("b2s", [E, D])
        ident = sb("ident", [P, P])
        tie = sb("tie", [P, E])
        xn = sb("xn", [P, TT, D])
        xT = sb("xT", [P, TOK])
        xh, xl = sb("xh", [P, NT * P], F16), sb("xl", [P, NT * P], F16)
        gates = sb("gates", [P, NT, E])
        gnew = sb("gnew", [P, TT, E])
        gT = sb("gT", [E, TOK])
        stats = sb("stats", [P, TT, 6])
        mean, dif = sb("mean", [P, TT]), sb("dif", [P, TT])
        rstd = sb("rstd", [P, TT])
        var, half, newton = (sb(n, [P, TT]) for n in ("var", "half", "newton"))
        guess = sb("guess", [P, TT], I32)
        lg, lg2, eq, one1, one2 = (sb(n, [P, TT, E]) for n in ("lg", "lg2", "eq", "one1", "one2"))
        m1, m2, pick, e2, g1, g2, den = (sb(n, [P, TT]) for n in ("m1", "m2", "pick", "e2", "g1", "g2", "den"))
        r = sb("r", [P, 2, HC, TOK])
        rh, rl = sb("rh", [P, 2, HC, TOK], F16), sb("rl", [P, 2, HC, TOK], F16)

        psum = ctx.enter_context(nc.psum_tensor("psum", [P, 8, 512], F32))
        banks = [psum[:, i, :] for i in range(8)]
        z = banks[0:4]
        y = banks[4:6]
        pT = banks[6]
        misc = banks[7]

        wnat = sb("wnat", [P, 4, D])
        wqr, wkr = sb("wqr", [P, HG, P]), sb("wkr", [P, HG, P])
        wvT, woT = sb("wvT", [P, D]), sb("woT", [P, D])
        identb = sb("identb", [P, P], BF16)
        maskb = sb("maskb", [P, NQ, 2 * QB], BF16)
        strip = sb("strip", [P, HP])
        strip16 = sb("strip16", [P, HG, NH])
        headrow = sb("headrow", [NH, D])
        fold = sb("fold", [P, QB])
        row_no = sb("row_no", [P, 1], I32)
        row_bit = sb("row_bit", [P, 2], I32)
        neg_q, neg_k = sb("neg_q", [P, 1]), sb("neg_k", [P, 1])
        ones = sb("ones", [P, 1])
        axn = sb("axn", [P, 2, D])
        aT = sb("aT", [P, PADS])
        aTr = sb("aTr", [P, NQ + 1, HP, QB])
        hi = sb("hi", [P, 2, 512], F16)
        qrow = sb("qrow", [P, 2, HG, S], F16)
        krow = sb("krow", [P, 2, HG, PADS], F16)
        k0 = sb("k0", [P, 2, HG, HP], F16)
        q0 = sb("q0", [P, 2, HG, NH], F16)
        vbd = sb("vbd", [P, 2, NQ + 1, HG, HP, HD + 1])
        vp = sb("vp", [P, 2, 3, D])
        mx = sb("mx", [P, HG, NQ])
        mxd = sb("mxd", [P, NQ, HG, HP])
        prob = sb("prob", [P, HG * NQ, 2 * QB])
        probT = sb("probT", [P, HG * NQ, 2, QB])
        mt_sb = sb("mt_sb", [P, NM])
        mg = sb("mg", [P, NM])
        dd = sb("dd", [P, 2, NM])
        ee = sb("ee", [P, 2, NM])
        al, mden, mrec = sb("al", [P, NM]), sb("mden", [P, NM]), sb("mrec", [P, NM])
        ar, cr = sb("ar", [P, NM]), sb("cr", [P, NM])
        t2 = sb("t2", [P, 2, D])
        att = sb("att", [P, 2, D])
        atT = sb("atT", [P, S])
        g_neg, g_sum, g_rec = sb("g_neg", [NH, 1]), sb("g_sum", [NH, 1]), sb("g_rec", [NH, 1])
        g_exp, g_prob = sb("g_exp", [NH, S]), sb("g_prob", [NH, S])
        g_pT = sb("g_pT", [P, 2, NH])
        g_out = sb("g_out", [NH, D])

        sc = psum[:, 0:4, :]
        pj = banks[4:6]
        ob = banks[6]
        gb = banks[7]
        O_N, S0_AT, MT_AT = NT_B * HG * HP * (HD + 1), 288, 320

        s_x = sem("s_x")
        s_w = sem("s_w")
        s_const = sem("s_const")
        s_setup = sem("s_setup")
        s_w1h, s_w2h, s_wl = sem("s_w1h"), sem("s_w2h"), sem("s_wl")
        ln_chain, ln_done = sem("ln_chain"), sem("ln_done")
        pT_full, xT_done, xh_done, xl_done = sem("pT_full"), sem("xT_done"), sem("xh_done"), sem("xl_done")
        lg_full, route_chain, e2_done, gates_done = sem("lg_full"), sem("route_chain"), sem("e2_done"), sem("gates_done")
        gates_kept = sem("gates_kept")
        delta_done = sem("delta_done")
        gT_full, gT_done, b2_full, b2_done = sem("gT_full"), sem("gT_done"), sem("b2_full"), sem("b2_done")
        z_full, r_done, rh_done, rl_done = sem("z_full"), sem("r_done"), sem("rh_done"), sem("rl_done")
        y_full, y_done = sem("y_full"), sem("y_done")
        s_out = sem("s_out")
        c_pool, c_dve, wT_full, wT_done, masks_done = (sem(n) for n in ("c_pool", "c_dve", "wT_full", "wT_done", "masks_done"))
        aln_chain, aln_done, aT_full, aT_done = (sem(n) for n in ("aln_chain", "aln_done", "aT_full", "aT_done"))
        pj_full, hi_done, qk_done, vb_done, vp_done, bd_done = (
            sem(n) for n in ("pj_full", "hi_done", "qk_done", "vb_done", "vp_done", "bd_done"))
        sc_full, mx_done, mxd_done, sub_done, exp_done, pt_done = (
            sem(n) for n in ("sc_full", "mx_done", "mxd_done", "sub_done", "exp_done", "pt_done"))
        gs_full, gneg_done, gexp_done, g_chain, p0_done, p0T_full, p0T_done, go_full, gm_done = (
            sem(n) for n in ("gs_full", "gneg_done", "gexp_done", "g_chain", "p0_done", "p0T_full", "p0T_done",
                             "go_full", "gm_done"))
        o_full, mg_chain, dd_done, ee_done, cr_done, t2_done, att_done = (
            sem(n) for n in ("o_full", "mg_chain", "dd_done", "ee_done", "cr_done", "t2_done", "att_done"))
        atT_full, atT_done, wo_full, res_done = (sem(n) for n in ("atT_full", "atT_done", "wo_full", "res_done"))
        aTr_done = sem("aTr_done")
        R0 = HC

        NEWTON = 4
        MG_LINKS = 7
        ALN_LINKS = NT_B + 7 + 3 + 3 * 4
        LN_LINKS = TT + 7 + 3 + 3 * NEWTON
        ROUTE_LINKS = 16
        N_W = 10
        b2s_done = sem("b2s_done")
        Y0 = 2
        b1_full, b1_done = sem("b1_full"), sem("b1_done")

        def moments(stats, mean, dif, var, link, settle):
            link(nc.vector.tensor_tensor(mean[:, :], stats[:, :, 1], stats[:, :, 4], ALU.add))
            link(nc.vector.tensor_tensor(dif[:, :], stats[:, :, 1], stats[:, :, 4], ALU.subtract))
            link(nc.vector.tensor_tensor(var[:, :], stats[:, :, 2], stats[:, :, 5], ALU.add))
            settle()
            link(nc.vector.tensor_scalar(mean[:, :], mean[:, :], 0.5, None, ALU.mult))
            link(nc.vector.tensor_tensor(dif[:, :], dif[:, :], dif[:, :], ALU.mult))
            link(nc.vector.tensor_scalar(var[:, :], var[:, :], 1.0 / D, EPS, ALU.mult, ALU.add))
            settle()
            link(nc.vector.scalar_tensor_tensor(out=var[:, :], in0=dif[:, :], scalar=0.25, in1=var[:, :],
                                                op0=ALU.mult, op1=ALU.add))
            settle()

        def rsqrt(out, var, half, guess, newton, link, settle):
            link(nc.vector.tensor_scalar(half[:, :], var[:, :], -0.5, None, ALU.mult))
            link(nc.vector.tensor_scalar(guess[:, :], var[:, :].bitcast(I32), 1, None, ALU.logical_shift_right))
            settle()
            link(nc.vector.tensor_scalar(out[:, :].bitcast(I32), guess[:, :], -1, 0x5F3759DF, ALU.mult, ALU.add))
            settle()
            for _ in range(NEWTON):
                link(nc.vector.tensor_tensor(newton[:, :], out[:, :], out[:, :], ALU.mult))
                settle()
                link(nc.vector.tensor_tensor(newton[:, :], newton[:, :], half[:, :], ALU.mult))
                settle()
                link(nc.vector.scalar_tensor_tensor(out=out[:, :], in0=newton[:, :], scalar=1.5, in1=out[:, :],
                                                    op0=ALU.add, op1=ALU.mult))
                settle()

        block = ctx.enter_context(nc.Block())

        def batches(eng, step):
            step(-1, True, False, False)
            step(0, True, True, False)
            step(1, True, True, True)
            step(2, True, True, True)
            with eng.Fori(0, (B - 4) // 2) as pair:
                step(3 + pair * 2, True, True, True)
                step(4 + pair * 2, True, True, True, 1)
            step(B - 1, False, True, True)
            step(B, False, False, True)

        def par(i, odd):
            return i % 2 if isinstance(i, int) else 1 - odd

        def chunks(eng, ffn, body):
            with eng.Fori(0, NC - 1) as c:
                body(ffn, c, False)
            body(ffn, NC - 1, True)

        @block.sync
        def _(sp):
            for k in range(4):
                n = NT // 4
                sp.dma_start(xres[:, k * n:(k + 1) * n, :], x_v[:, k * n:(k + 1) * n, :]).then_inc(s_x, 16)
            sp.dma_start(wr[:, :], Wr).then_inc(s_w, 16)
            sp.dma_start(br_bc[:, :], br[None, :].broadcast_to([P, E])).then_inc(s_w, 16)
            sp.dma_start(w1f[:, :, :], W1.rearrange("e d h -> d e h")).then_inc(s_w, 16)
            sp.dma_start(w2f[:, :, :, :], W2.rearrange("e (j p) d -> p e j d", p=P)).then_inc(s_w, 16)
            sp.dma_start(b1n[:, :], b1.rearrange("e (j p) -> (e j) p", p=P)).then_inc(s_w, 16)
            sp.dma_start(b2s[:, :], b2).then_inc(s_w, 16)
            for k, w in enumerate((Wq, Wk, Wv, Wo)):
                sp.dma_start(wnat[:, k, :], w).then_inc(s_w, 16)
            sp.wait_ge(y_done, 2 * STEPS + Y0)
            sp.dma_start(out_v, xres[:, :, :]).then_inc(s_out, 16)
            sp.wait_ge(s_out, 16)

        @block.gpsimd
        def _(pool):
            nc.gpsimd.memset(ident[:, :], 0.0).then_inc(s_setup, 1)
            nc.gpsimd.iota(tie[:, :], [[-1, E]], base=E, channel_multiplier=0,
                           allow_small_or_imprecise_dtypes=True).then_inc(s_const, 1)
            pool.wait_ge(s_setup, 1)
            nc.gpsimd.affine_select(out=ident[:, :], in_=ident[:, :], compare_op=ALU.not_equal, fill=1.0, base=0,
                                    pattern=[[-1, P]], channel_multiplier=1).then_inc(s_const, 1)
            n = [0]

            def settle(ins):
                ins.then_inc(c_pool, 1)
                n[0] += 1
                pool.wait_ge(c_pool, n[0])

            for j in range(HC):
                nc.gpsimd.memset(rl[:, 1, j, 0:1], 0.0).then_inc(rl_done, 1)
            nc.gpsimd.iota(row_no[:, :], [[0, 1]], base=0, channel_multiplier=1).then_inc(c_pool, 1)
            nc.gpsimd.memset(aT[:, :], 0.0).then_inc(c_pool, 1)
            nc.gpsimd.memset(vbd[:, :, :, :, :, :], 0.0).then_inc(c_pool, 1)
            nc.gpsimd.memset(strip[:, :], 0.0).then_inc(c_pool, 1)
            nc.gpsimd.memset(strip16[:, :, :], 0.0).then_inc(c_pool, 1)
            nc.gpsimd.memset(headrow[:, :], 1.0).then_inc(c_pool, 1)
            nc.gpsimd.memset(ones[:, :], 1.0).then_inc(c_pool, 1)
            nc.gpsimd.memset(maskb[:, :, :], 0.0).then_inc(c_pool, 1)
            n[0] = 8
            pool.wait_ge(c_pool, 8)
            s16 = strip16[:, :, :].rearrange("p g h -> p (g h)")
            for j in range(HP):
                sj = slice(QB * j, QB * (j + 1))
                settle(nc.gpsimd.memset(strip[sj, j:j + 1], 1.0))
                settle(nc.gpsimd.memset(s16[sj, j:j + 3 * (NH + HP) + 1:NH + HP], 1.0))
                for base, step, mult in ((0, 1, -1), (2 * WIN, -1, 1)):
                    settle(nc.gpsimd.affine_select(out=maskb[sj, :, :], in_=maskb[sj, :, :], compare_op=ALU.is_ge,
                                                   fill=NOT_SEEN, base=base, pattern=[[0, NQ], [step, 2 * QB]],
                                                   channel_multiplier=mult))
            for base, step in ((-WIN - 1, 1), (S - 1 + WIN, -1)):
                settle(nc.gpsimd.affine_select(out=maskb[:, :, :], in_=maskb[:, :, :], compare_op=ALU.is_ge,
                                               fill=NOT_SEEN, base=base, pattern=[[step * QB, NQ], [step, 2 * QB]],
                                               channel_multiplier=0))
            for base, step, mult in ((0, 1, -HD), (HD - 1, -1, HD)):
                settle(nc.gpsimd.affine_select(out=headrow[:, :], in_=headrow[:, :], compare_op=ALU.is_ge, fill=0.0,
                                               base=base, pattern=[[step, D]], channel_multiplier=mult))
            pool.wait_ge(s_const, 2)
            settle(nc.gpsimd.tensor_copy(identb[:, :], ident[:, :]))
            for j in range(HP):
                sj = slice(QB * j, QB * (j + 1))
                for u in range(2):
                    settle(nc.gpsimd.memset(vbd[sj, u, :, :, j, HD], 1.0))
                settle(nc.gpsimd.tensor_copy(fold[sj, :], ident[sj, sj]))
            nc.gpsimd.memset(row_bit[:, :], 0).then_inc(masks_done, 1)

            def attention_step(i, project, middle, finish, odd=0):
                if project:
                    pool.wait_ge(aT_done, i + 2)
                    if middle:
                        pool.wait_ge(pj_full, SLOTS * (i + 1))
                    nc.gpsimd.tensor_tensor(
                        aTr[:, :, :, :],
                        aT[:, :].rearrange("p (q k) -> p q k", k=QB)[:, :, None, :].broadcast_to([P, NQ + 1, HP, QB]),
                        ones[:, :, None, None].broadcast_to([P, NQ + 1, HP, QB]), ALU.mult).then_inc(aTr_done, 1)
                if middle:
                    pool.wait_ge(mx_done, i + 1)
                    if finish:
                        pool.wait_ge(o_full, i)
                    nc.gpsimd.tensor_tensor(
                        mxd[:, :, :, :], mx[:, :, :].rearrange("p g q -> p q g")[:, :, :, None].broadcast_to([P, NQ, HG, HP]),
                        strip[:, None, None, :].broadcast_to([P, NQ, HG, HP]), ALU.mult).then_inc(mxd_done, 1)
                if finish:
                    u = par(i - 1, 1 - odd)
                    pool.wait_ge(cr_done, i)
                    nc.gpsimd.tensor_tensor(
                        t2[:, :, :].rearrange("p t (h d) -> p t h d", d=HD),
                        vp[:, u, 2, :].rearrange("p (h d) -> p h d", d=HD)[:, None, :, :].broadcast_to([P, NT_B, NH, HD]),
                        cr[:, :].rearrange("p (t h) -> p t h", t=NT_B)[:, :, :, None].broadcast_to([P, NT_B, NH, HD]),
                        ALU.mult).then_inc(t2_done, 1)
                if project:
                    u = par(i + 1, 1 - odd)
                    pool.wait_ge(qk_done, 6 * (i + 1) + 6)
                    nc.gpsimd.tensor_tensor(k0[:, u, :, :], krow[:, u, :, WIN:WIN + 1].broadcast_to([P, HG, HP]),
                                            strip[:, None, :].broadcast_to([P, HG, HP]), ALU.mult).then_inc(bd_done, 1)
                    nc.gpsimd.tensor_tensor(q0[:, u, :, :], qrow[:, u, :, 0:1].broadcast_to([P, HG, NH]),
                                            strip16[:, :, :], ALU.mult).then_inc(bd_done, 1)

            def low_x(ffn, c):
                pool.wait_ge(xh_done, ffn * NC + c + 1)
                nc.gpsimd.tensor_tensor(xl[:, bass.ds(c * TOK, TOK)], xT[:, :], xh[:, bass.ds(c * TOK, TOK)],
                                        ALU.subtract).then_inc(xl_done, 1)

            def low_r(step, e):
                for j in range(HC):
                    pool.wait_ge(rh_done, HC * step + j + 1)
                    nc.gpsimd.tensor_tensor(rl[:, e % 2, j, :], r[:, e % 2, j, :], rh[:, e % 2, j, :],
                                            ALU.subtract).then_inc(rl_done, 1)

            def body(ffn, c, last):
                for e in range(E):
                    if e == 3 and not last:
                        low_x(ffn, c + 1)
                    if not (last and e == E - 1):
                        low_r(ffn * STEPS + c * E + e + 1, (e + 1) % E)

            for ffn in range(2):
                low_x(ffn, 0)
                low_r(ffn * STEPS, 0)
                chunks(pool, ffn, body)
                if ffn == 0:
                    batches(pool, attention_step)

        @block.scalar
        def _(act):
            act.wait_ge(s_w, 16 * N_W)
            nc.scalar.activation(w1h[:, :, :], w1f[:, :, :], ACT.Copy, scale=WSCALE).then_inc(s_w1h, 1)
            nc.scalar.activation(w2h[:, :, :, :], w2f[:, :, :, :], ACT.Copy, scale=WSCALE).then_inc(s_w2h, 1)

            act.wait_ge(b1_full, 1)
            nc.scalar.copy(b1T[:, :, :], misc[:, 0:E * HC].rearrange("p (e j) -> p e j", e=E)).then_inc(b1_done, 1)

            act.wait_ge(wT_full, 1)
            for k, w in enumerate((wqr, wkr)):
                nc.scalar.activation(
                    w[:, :, :].rearrange("p g (h r d) -> p (g h) r d", h=HP, d=HD),
                    z[0][:, k * D:(k + 1) * D].rearrange("p (h d) -> p h d", d=HD)[:, :, None, :].broadcast_to([P, NH, 4, HD]),
                    ACT.Copy, scale=HD ** -0.5 if k == 0 else 1.0).then_inc(wT_done, 1)
            nc.scalar.copy(wvT[:, :], z[0][:, 2 * D:3 * D]).then_inc(wT_done, 1)
            nc.scalar.copy(woT[:, :], z[0][:, 3 * D:4 * D]).then_inc(wT_done, 1)

            def attention_step(i, project, middle, finish, odd=0):
                b = i + 1
                if project:
                    act.wait_ge(aT_full, b + 1)
                    nc.scalar.copy(aT[:, WIN:WIN + S], pj[0][:, 0:S]).then_inc(aT_done, 1)
                if middle:
                    for h in range(2):
                        act.wait_ge(sub_done, 2 * i + h + 1)
                        half = prob[:, 16 * h:16 * h + 16, :]
                        nc.scalar.activation(half, half, ACT.Exp).then_inc(exp_done, 1)
                if finish:
                    act.wait_ge(p0T_full, i)
                    nc.scalar.copy(g_pT[:, :, :], gb[:, 256:256 + 2 * NH].rearrange("p (t h) -> p t h", t=2)
                                   ).then_inc(p0T_done, 1)
                    act.wait_ge(dd_done, i)
                    nc.scalar.activation(ee[:, :, :], dd[:, :, :], ACT.Exp).then_inc(ee_done, 1)
                if project:
                    u = par(b, 1 - odd)
                    for k in range(1, 7):
                        n = S * 2 if k < 3 else PADS
                        act.wait_ge(pj_full, SLOTS * b + k)
                        if not (isinstance(b, int) and 6 * b + k - 2 <= 0):
                            act.wait_ge(qk_done, 6 * b + k - 2)
                        nc.scalar.copy(hi[:, k % 2, 0:n], pj[k % 2][:, 0:n]).then_inc(hi_done, 1)
                    act.wait_ge(vb_done, 3 * b + 3)
                    if finish:
                        act.wait_ge(att_done, b - 1)
                    nc.scalar.copy(vp[:, u, :, :], pj[1][:, D:4 * D].rearrange("p (t d) -> p t d", t=3)
                                   ).then_inc(vp_done, 1)
                if middle:
                    act.wait_ge(gneg_done, i + 1)
                    nc.scalar.activation(g_exp[:, :], gb[0:NH, 0:S], ACT.Exp, bias=g_neg[:, 0:1], scale=1.0,
                                         accum_out=g_sum[:, 0:1]).then_inc(gexp_done, 1)
                if finish:
                    act.wait_ge(atT_full, i)
                    nc.scalar.copy(atT[:, 1:S], pj[0][:, 1:S])
                    nc.scalar.copy(atT[:, 0:1], pj[0][:, S:S + 1]).then_inc(atT_done, 1)

            def xT_copy(ffn, c):
                act.wait_ge(pT_full, ffn * NC + c + 1)
                if not (isinstance(c, int) and c == 0 and ffn == 0):
                    act.wait_ge(xl_done, ffn * NC + c)
                    act.wait_ge(lg_full, ffn * NC + c)
                nc.scalar.copy(xT[:, :], pT[:, :]).then_inc(xT_done, 1)

            def gate_exp(ffn, c):
                act.wait_ge(delta_done, ffn * NC + c + 1)
                nc.scalar.activation(e2[:, :], m2[:, :], ACT.Exp).then_inc(e2_done, 1)

            def gT_copy(ffn, c):
                act.wait_ge(gT_full, ffn * NC + c + 1)
                nc.scalar.copy(gT[:, :], misc[0:E, :]).then_inc(gT_done, 1)

            def relu(step, e, wait_free):
                for j in range(HC):
                    act.wait_ge(z_full, HC * step + j + 1)
                    if wait_free and j == 0:
                        act.wait_ge(rl_done, HC * (step - 1) + R0)
                    nc.scalar.activation(r[:, e % 2, j, :], z[j][:, :], ACT.Relu, bias=b1T[:, e, j:j + 1],
                                         scale=1.0 / WSCALE).then_inc(r_done, 1)

            def body(ffn, c, last):
                for e in range(E):
                    if not last:
                        if e == 2:
                            xT_copy(ffn, c + 1)
                        if e == 4:
                            gate_exp(ffn, c + 1)
                        if e == 6:
                            gT_copy(ffn, c + 1)
                    if not (last and e == E - 1):
                        relu(ffn * STEPS + c * E + e + 1, (e + 1) % E, True)

            for ffn in range(2):
                xT_copy(ffn, 0)
                gate_exp(ffn, 0)
                gT_copy(ffn, 0)
                relu(ffn * STEPS, 0, ffn > 0)
                chunks(act, ffn, body)
                if ffn == 0:
                    batches(act, attention_step)

        @block.vector
        def _(dve):
            dve.wait_ge(s_w, 16 * N_W)
            nc.vector.tensor_scalar(b2s[:, :], b2s[:, :], WSCALE, None, ALU.mult).then_inc(b2s_done, 1)
            nc.vector.memset(y[0][:, :], 0.0).then_inc(y_done, 1)
            nc.vector.memset(y[1][:, :], 0.0).then_inc(y_done, 1)
            dve.wait_ge(s_w1h, 1)
            nc.vector.scalar_tensor_tensor(out=w1l[:, :, :], in0=w1f[:, :, :], scalar=WSCALE, in1=w1h[:, :, :],
                                           op0=ALU.mult, op1=ALU.subtract).then_inc(s_wl, 1)
            dve.wait_ge(s_w2h, 1)
            nc.vector.scalar_tensor_tensor(out=w2l[:, :, :, :], in0=w2f[:, :, :, :], scalar=WSCALE,
                                           in1=w2h[:, :, :, :], op0=ALU.mult, op1=ALU.subtract).then_inc(s_wl, 1)

            dve.wait_ge(masks_done, 1)
            for k, (bit, neg) in enumerate(((16, neg_q), (8, neg_k))):
                nc.vector.tensor_scalar(row_bit[:, k:k + 1], row_no[:, :], bit, None, ALU.bitwise_and).then_inc(c_dve, 1)
                dve.wait_ge(c_dve, 2 * k + 1)
                nc.vector.tensor_scalar(neg[:, :], row_bit[:, k:k + 1], -1.0 / bit, None, ALU.mult).then_inc(c_dve, 1)
            dve.wait_ge(c_dve, 4)

            def attention_norm(b):
                k = [b * ALN_LINKS]

                def link(ins):
                    ins.then_inc(aln_chain, 1)
                    k[0] = k[0] + 1

                if not (isinstance(b, int) and b == 0):
                    dve.wait_ge(aT_full, b)
                for t in range(NT_B):
                    link(nc.vector.bn_stats(stats[:, t, :], xres[:, bass.ds(b * NT_B + t, 1), :]))
                dve.wait_ge(aln_chain, k[0])
                n = slice(0, NT_B)
                settle = lambda: dve.wait_ge(aln_chain, k[0])
                moments(stats[:, n, :], mean[:, n], dif[:, n], var[:, n], link, settle)
                rsqrt(rstd[:, n], var[:, n], half[:, n], guess[:, n], newton[:, n], link, settle)
                for t in range(NT_B):
                    last = nc.vector.tensor_scalar(axn[:, t, :], xres[:, bass.ds(b * NT_B + t, 1), :],
                                                   mean[:, t:t + 1], rstd[:, t:t + 1], ALU.subtract, ALU.mult)
                last.then_inc(aln_done, 1)

            def softmax_in(i):
                dve.wait_ge(sc_full, i + 1)
                if not (isinstance(i, int) and i == 0):
                    dve.wait_ge(mxd_done, i)
                    dve.wait_ge(pt_done, 2 * i)
                for h in range(2):
                    last = nc.vector.tensor_reduce(mx[:, 2 * h:2 * h + 2, :],
                                                   sc[:, 2 * h:2 * h + 2, :].rearrange("p g (q c) -> p g q c", q=NQ),
                                                   AX.X, ALU.max)
                last.then_inc(mx_done, 1)
                dve.wait_ge(mx_done, i + 1)
                for h in range(2):
                    nc.vector.tensor_tensor(
                        prob[:, 16 * h:16 * h + 16, :],
                        sc[:, 2 * h:2 * h + 2, :].rearrange("p g (q c) -> p (g q) c", q=NQ),
                        mx[:, 2 * h:2 * h + 2, :].rearrange("p g q -> p (g q)")[:, :, None].broadcast_to([P, 16, 2 * QB]),
                        ALU.subtract).then_inc(sub_done, 1)

            def merge(b):
                k = [b * MG_LINKS]

                def link(ins):
                    ins.then_inc(mg_chain, 1)
                    k[0] = k[0] + 1
                    dve.wait_ge(mg_chain, k[0])

                dve.wait_ge(o_full, b + 1)
                s0, mt = ob[:, S0_AT:S0_AT + NM], ob[:, MT_AT:MT_AT + NM]
                o = ob[:, 0:O_N].rearrange("p (n e) -> p n e", e=HD + 1)
                nc.vector.tensor_copy(mt_sb[:, :], mt).then_inc(mg_chain, 1)
                k[0] = k[0] + 1
                dve.wait_ge(mg_chain, k[0])
                link(nc.vector.tensor_tensor(mg[:, :], s0, mt_sb[:, :], ALU.max))
                nc.vector.tensor_tensor(dd[:, 0, :], mt_sb[:, :], mg[:, :], ALU.subtract)
                nc.vector.tensor_tensor(dd[:, 1, :], s0, mg[:, :], ALU.subtract).then_inc(dd_done, 1)
                dve.wait_ge(ee_done, b + 1)
                link(nc.vector.tensor_tensor(al[:, :], o[:, :, HD], ee[:, 0, :], ALU.mult))
                link(nc.vector.tensor_tensor(mden[:, :], al[:, :], ee[:, 1, :], ALU.add))
                link(nc.vector.reciprocal(mrec[:, :], mden[:, :]))
                if not (isinstance(b, int) and b == 0):
                    dve.wait_ge(t2_done, b)
                nc.vector.tensor_tensor(cr[:, :], ee[:, 1, :], mrec[:, :], ALU.mult).then_inc(cr_done, 1)
                link(nc.vector.tensor_tensor(ar[:, :], ee[:, 0, :], mrec[:, :], ALU.mult))
                if not (isinstance(b, int) and b == 0):
                    dve.wait_ge(atT_full, b)
                a = att[:, :, :].rearrange("p t (h d) -> p (t h) d", d=HD)
                link(nc.vector.tensor_tensor(a, o[:, :, 0:HD], ar[:, :, None].broadcast_to([P, NM, HD]), ALU.mult))
                dve.wait_ge(t2_done, b + 1)
                nc.vector.tensor_tensor(att[:, :, :], att[:, :, :], t2[:, :, :], ALU.add).then_inc(att_done, 1)

            def evacuate(b, u):
                for k in range(1, 7):
                    dve.wait_ge(hi_done, 6 * b + k)
                    if k < 3:
                        n, neg = 2 * S, neg_q
                        out_rows = qrow[:, u, 2 * k - 2:2 * k, :].rearrange("p g t -> p (g t)")
                    else:
                        n, neg = PADS, neg_k
                        out_rows = krow[:, u, k - 3, :]
                    nc.vector.scalar_tensor_tensor(out=out_rows, in0=hi[:, k % 2, 0:n], scalar=neg[:, 0:1],
                                                   in1=pj[k % 2][:, 0:n], op0=ALU.mult, op1=ALU.add).then_inc(qk_done, 1)
                for k in range(7, 10):
                    dve.wait_ge(pj_full, SLOTS * b + k)
                    q0_, m = 4 * (k - 7), (4 if k < 9 else 1)
                    nc.vector.tensor_tensor(
                        vbd[:, u, q0_:q0_ + m, :, :, 0:HD].rearrange("p q g h d -> p (q g) h d"),
                        pj[k % 2][:, 0:m * D].rearrange("p (n h d) -> p n h d", h=HP, d=HD),
                        strip[:, None, :, None].broadcast_to([P, m * HG, HP, HD]), ALU.mult).then_inc(vb_done, 1)

            def attention_step(i, project, middle, finish, odd=0):
                b = i + 1
                if project:
                    attention_norm(b)
                if middle:
                    softmax_in(i)
                if finish:
                    merge(i - 1)
                    dve.wait_ge(go_full, i)
                    nc.vector.tensor_tensor(g_out[:, :], gb[0:NH, 288:288 + D], headrow[:, :], ALU.mult).then_inc(gm_done, 1)
                if project:
                    evacuate(b, par(b, 1 - odd))
                if middle:
                    if finish:
                        dve.wait_ge(o_full, i)
                    for h in range(2):
                        dve.wait_ge(exp_done, 2 * i + h + 1)
                        nc.vector.transpose(probT[:, 16 * h:16 * h + 16, :, :].rearrange("p n a q -> p (n a q)"),
                                            prob[:, 16 * h:16 * h + 16, :].rearrange("p n c -> p (n c)")).then_inc(pt_done, 1)
                    dve.wait_ge(gs_full, i + 1)
                    nc.vector.tensor_reduce(g_neg[:, :], gb[0:NH, 0:S], AX.X, ALU.max, negate=True).then_inc(gneg_done, 1)
                    dve.wait_ge(gexp_done, i + 1)
                    nc.vector.reciprocal(g_rec[:, :], g_sum[:, :]).then_inc(g_chain, 1)
                    dve.wait_ge(g_chain, i + 1)
                    if finish:
                        dve.wait_ge(p0T_full, i)
                    nc.vector.tensor_scalar(g_prob[:, :], g_exp[:, :], g_rec[:, 0:1], None, ALU.mult).then_inc(p0_done, 1)
                if finish:
                    dve.wait_ge(wo_full, i)
                    xr = xres[:, bass.ds((i - 1) * NT_B, NT_B), :]
                    nc.vector.tensor_tensor(xr, xr, pj[1][:, 0:S].rearrange("p (t d) -> p t d", t=NT_B),
                                            ALU.add).then_inc(res_done, 1)

            def norm(ffn, c):
                k = [(ffn * NC + c) * LN_LINKS]

                def link(ins):
                    ins.then_inc(ln_chain, 1)
                    k[0] = k[0] + 1

                if ffn == 0:
                    dve.wait_ge(s_x, 16 * 4)
                if not (ffn == 0 and isinstance(c, int)):
                    dve.wait_ge(pT_full, ffn * NC + c)
                for t in range(TT):
                    link(nc.vector.bn_stats(stats[:, t, :], xres[:, bass.ds(c * TT + t, 1), :]))
                dve.wait_ge(ln_chain, k[0])
                moments(stats, mean, dif, var, link, lambda: dve.wait_ge(ln_chain, k[0]))
                rsqrt(rstd, var, half, guess, newton, link, lambda: dve.wait_ge(ln_chain, k[0]))
                for t in range(TT):
                    last = nc.vector.tensor_scalar(xn[:, t, :], xres[:, bass.ds(c * TT + t, 1), :], mean[:, t:t + 1],
                                                   rstd[:, t:t + 1], ALU.subtract, ALU.mult)
                last.then_inc(ln_done, 1)

            def high_x(ffn, c):
                dve.wait_ge(xT_done, ffn * NC + c + 1)
                nc.vector.tensor_copy(xh[:, bass.ds(c * TOK, TOK)], xT[:, :]).then_inc(xh_done, 1)

            def route(ffn, c, part):
                k = [(ffn * NC + c) * ROUTE_LINKS]
                n = [0]

                def link(ins):
                    ins.then_inc(route_chain, 1)
                    n[0] += 1
                    dve.wait_ge(route_chain, k[0] + n[0])

                def wide(a):
                    return a[:, :, None].broadcast_to([P, TT, E])

                tie_b = tie[:, None, :].broadcast_to([P, TT, E])
                if part == 0:
                    dve.wait_ge(lg_full, ffn * NC + c + 1)
                    link(nc.vector.tensor_tensor(lg[:, :, :], misc[:, 0:TT * E].rearrange("p (t e) -> p t e", t=TT),
                                                 br_bc[:, None, :].broadcast_to([P, TT, E]), ALU.add))
                    link(nc.vector.tensor_reduce(m1[:, :], lg[:, :, :], AX.X, ALU.max))
                    link(nc.vector.tensor_tensor(eq[:, :, :], lg[:, :, :], wide(m1), ALU.is_equal))
                    link(nc.vector.tensor_tensor(eq[:, :, :], eq[:, :, :], tie_b, ALU.mult))
                    link(nc.vector.tensor_reduce(pick[:, :], eq[:, :, :], AX.X, ALU.max))
                    link(nc.vector.tensor_tensor(one1[:, :, :], tie_b, wide(pick), ALU.is_equal))
                    link(nc.vector.scalar_tensor_tensor(out=lg2[:, :, :], in0=one1[:, :, :], scalar=-BIG,
                                                        in1=lg[:, :, :], op0=ALU.mult, op1=ALU.add))
                    link(nc.vector.tensor_reduce(m2[:, :], lg2[:, :, :], AX.X, ALU.max))
                    link(nc.vector.tensor_tensor(eq[:, :, :], lg2[:, :, :], wide(m2), ALU.is_equal))
                    link(nc.vector.tensor_tensor(eq[:, :, :], eq[:, :, :], tie_b, ALU.mult))
                    link(nc.vector.tensor_reduce(pick[:, :], eq[:, :, :], AX.X, ALU.max))
                    nc.vector.tensor_tensor(one2[:, :, :], tie_b, wide(pick), ALU.is_equal)
                    nc.vector.tensor_tensor(m2[:, :], m2[:, :], m1[:, :], ALU.subtract).then_inc(delta_done, 1)
                else:
                    n[0] = 11
                    dve.wait_ge(e2_done, ffn * NC + c + 1)
                    link(nc.vector.tensor_scalar(den[:, :], e2[:, :], 1.0, 2.0 * WSCALE, ALU.add, ALU.mult))
                    link(nc.vector.reciprocal(g1[:, :], den[:, :]))
                    link(nc.vector.tensor_tensor(g2[:, :], g1[:, :], e2[:, :], ALU.mult))
                    link(nc.vector.tensor_tensor(one1[:, :, :], one1[:, :, :], wide(g1), ALU.mult))
                    link(nc.vector.tensor_tensor(one2[:, :, :], one2[:, :, :], wide(g2), ALU.mult))
                    nc.vector.tensor_tensor(gnew[:, :, :], one1[:, :, :], one2[:, :, :], ALU.add).then_inc(gates_done, 1)
                    dve.wait_ge(gates_done, ffn * NC + c + 1)
                    nc.vector.tensor_copy(gates[:, bass.ds(c * TT, TT), :], gnew[:, :, :]).then_inc(gates_kept, 1)

            def add_b2(ffn, c):
                dve.wait_ge(b2_full, ffn * NC + c + 1)
                xr = xres[:, bass.ds(c * TT, TT), :]
                nc.vector.tensor_tensor(xr, xr, pT[:, :].rearrange("p (t d) -> p t d", t=TT),
                                        ALU.add).then_inc(b2_done, 1)

            def high_r(step, e):
                for j in range(HC):
                    dve.wait_ge(r_done, HC * step + j + 1)
                    nc.vector.tensor_copy(rh[:, e % 2, j, :], r[:, e % 2, j, :]).then_inc(rh_done, 1)

            def accumulate(ffn, c, e):
                step = ffn * STEPS + c * E + e
                dve.wait_ge(y_full, step + 1)
                if e == 0:
                    dve.wait_ge(b2_done, ffn * NC + c + 1)
                    dve.wait_ge(gates_kept, ffn * NC + c + 1)
                else:
                    dve.wait_ge(y_done, step + Y0)
                for t in range(TT):
                    xr = xres[:, bass.ds(c * TT + t, 1), :]
                    last = nc.vector.scalar_tensor_tensor(
                        out=xr, in0=y[e % 2][:, t * D:(t + 1) * D], scalar=gates[:, bass.ds(c * TT + t, 1), e],
                        in1=xr, op0=ALU.mult, op1=ALU.add)
                last.then_inc(y_done, 1)

            def body(ffn, c, last):
                for e in range(E):
                    if not last:
                        if e == 0:
                            norm(ffn, c + 1)
                        if e == 2:
                            high_x(ffn, c + 1)
                        if e == 3:
                            route(ffn, c + 1, 0)
                        if e == 4:
                            route(ffn, c + 1, 1)
                        if e == 7:
                            add_b2(ffn, c + 1)
                    if not (last and e == E - 1):
                        high_r(ffn * STEPS + c * E + e + 1, (e + 1) % E)
                    accumulate(ffn, c, e)

            for ffn in range(2):
                if ffn:
                    dve.wait_ge(y_done, STEPS + Y0)
                    batches(dve, attention_step)
                    dve.wait_ge(res_done, B)
                norm(ffn, 0)
                high_x(ffn, 0)
                route(ffn, 0, 0)
                route(ffn, 0, 1)
                high_r(ffn * STEPS, 0)
                add_b2(ffn, 0)
                chunks(dve, ffn, body)

        @block.tensor
        def _(pe):
            pe.wait_ge(s_const, 2)

            pe.wait_ge(s_w, 16 * N_W)
            nc.tensor.transpose(misc[:, 0:E * HC], b1n[:, :], ident[0:E * HC, 0:E * HC]).then_inc(b1_full, 1)
            pe.wait_ge(b1_done, 1)

            for k in range(4):
                last = nc.tensor.transpose(z[0][:, k * D:(k + 1) * D], wnat[:, k, :], ident[:, :])
            last.then_inc(wT_full, 1)
            pe.wait_ge(wT_done, 4)

            def slot_free(b, k):
                if k == 1:
                    if not (isinstance(b, int) and b == 0):
                        pe.wait_ge(vb_done, 3 * b)
                        pe.wait_ge(vp_done, b)
                    if not (isinstance(b, int) and b < 3):
                        pe.wait_ge(res_done, b - 2)
                elif 3 <= k <= 8:
                    pe.wait_ge(qk_done, 6 * b + k - 2)
                elif k == 9:
                    pe.wait_ge(vb_done, 3 * b + 1)

            def attention_step(i, project, middle, finish, odd=0):
                b = i + 1
                if project:
                    pe.wait_ge(aln_done, b + 1)
                    if not (isinstance(b, int) and b == 0):
                        pe.wait_ge(vb_done, 3 * b - 1)
                    if not (isinstance(b, int) and b < 3):
                        pe.wait_ge(atT_done, b - 2)
                    for t in range(NT_B):
                        last = nc.tensor.transpose(pj[0][:, t * P:(t + 1) * P], axn[:, t, :], ident[:, :])
                    last.then_inc(aT_full, 1)
                if middle:
                    scores(i, par(i, odd), finish)
                if finish:
                    weigh(i - 1, par(i - 1, 1 - odd))
                if project:
                    projections(b, par(b, 1 - odd))
                if middle:
                    u = par(i, odd)
                    pe.wait_ge(bd_done, 2 * i + 2)
                    if finish:
                        pe.wait_ge(gm_done, i)
                    for g in range(HG):
                        last = nc.tensor.matmul(gb[0:NH, 0:S], q0[:, u, g, :], krow[:, u, g, WIN:WIN + S],
                                                start=(g == 0), stop=(g == HG - 1))
                    last.then_inc(gs_full, 1)
                if finish:
                    pe.wait_ge(att_done, i)
                    pe.wait_ge(gm_done, i)
                    if project:
                        pe.wait_ge(vb_done, 3 * b + 2)
                    else:
                        pe.wait_ge(atT_done, i - 1)
                    for t in range(NT_B):
                        nc.tensor.transpose(pj[0][:, t * P:(t + 1) * P], att[:, t, :], ident[:, :])
                    nc.tensor.matmul(pj[0][:, S:S + 1], g_out[:, :], ones[0:NH, :], start=True, stop=True
                                     ).then_inc(atT_full, 1)
                    pe.wait_ge(atT_done, i)
                    if project:
                        pe.wait_ge(vb_done, 3 * b + 3)
                        pe.wait_ge(vp_done, b + 1)
                    else:
                        pe.wait_ge(res_done, i - 1)
                    for t in range(NT_B):
                        last = nc.tensor.matmul(pj[1][:, t * D:(t + 1) * D], atT[:, t * P:(t + 1) * P], woT[:, :],
                                                start=True, stop=True)
                    last.then_inc(wo_full, 1)

            def scores(b, u, again):
                pe.wait_ge(qk_done, 6 * b + 6)
                if not (isinstance(b, int) and b == 0):
                    pe.wait_ge(sub_done, 2 * b)
                for g in range(HG):
                    nc.tensor.matmul(sc[:, g, :], identb[:, :], maskb[:, :, :], start=True, stop=False,
                                     skip_group_check=True)
                for q in range(NQ):
                    for r_ in range(HG):
                        for h in range(HP):
                            g = (r_ + h) % HG
                            sh = slice(QB * h, QB * h + QB)
                            last = nc.tensor.matmul(sc[sh, g, 2 * QB * q:2 * QB * (q + 1)],
                                                    qrow[sh, u, g, QB * q:QB * (q + 1)],
                                                    krow[sh, u, g, QB * q:QB * (q + 2)], start=False,
                                                    stop=(q == NQ - 1), skip_group_check=True)
                last.then_inc(sc_full, 1)

            def weigh(b, u):
                pe.wait_ge(p0_done, b + 1)
                pe.wait_ge(mxd_done, b + 1)
                pe.wait_ge(bd_done, 2 * b + 2)
                if not (isinstance(b, int) and b == 0):
                    pe.wait_ge(att_done, b)
                for t in range(NT_B):
                    for g in range(HG):
                        at = S0_AT + t * NH + g * HP
                        nc.tensor.matmul(ob[:, at:at + HP], qrow[:, u, g, t * P:(t + 1) * P], k0[:, u, g, :],
                                         start=True, stop=True)
                for t in range(NT_B):
                    last = nc.tensor.transpose(gb[:, 256 + t * NH:256 + (t + 1) * NH], g_prob[:, t * P:(t + 1) * P],
                                               ident[0:NH, 0:NH])
                last.then_inc(p0T_full, 1)
                for j in range(P // QB):
                    nc.tensor.matmul(ob[QB * j:QB * (j + 1), MT_AT:MT_AT + NM], fold[:, :], mxd[:, j:NQ:P // QB, :, :],
                                     start=True, stop=True)
                pe.wait_ge(pt_done, 2 * b + 2)
                for q in range(NQ):
                    for g in range(HG):
                        j, t = q % (P // QB), q // (P // QB)
                        at = (t * HG + g) * HP * (HD + 1)
                        for half_ in range(2):
                            last = nc.tensor.matmul(
                                ob[QB * j:QB * (j + 1), at:at + HP * (HD + 1)], probT[:, g * NQ + q, half_, :],
                                vbd[:, u, q + half_, g, :, :].rearrange("p h e -> p (h e)"),
                                start=(half_ == 0), stop=(half_ == 1))
                last.then_inc(o_full, 1)
                pe.wait_ge(p0T_done, b + 1)
                for t in range(NT_B):
                    last = nc.tensor.matmul(gb[0:NH, 288:288 + D], g_pT[:, t, :], vp[:, u, t, :],
                                            start=(t == 0), stop=(t == NT_B - 1))
                last.then_inc(go_full, 1)

            def projections(b, u):
                pe.wait_ge(aT_done, b + 1)
                for k in range(1, 10):
                    slot_free(b, k)
                    o = pj[k % 2]
                    if k < 3:
                        for n in range(2):
                            last = nc.tensor.matmul(o[:, n * S:(n + 1) * S], wqr[:, 2 * k - 2 + n, :],
                                                    aT[:, WIN:WIN + S], start=True, stop=True)
                    elif k < 7:
                        last = nc.tensor.matmul(o[:, 0:PADS], wkr[:, k - 3, :], aT[:, :], start=True, stop=True)
                    else:
                        if k == 7:
                            pe.wait_ge(aTr_done, b + 1)
                        for n in range(4 if k < 9 else 1):
                            q = 4 * (k - 7) + n
                            last = nc.tensor.matmul(
                                o[:, n * D:(n + 1) * D],
                                aTr[:, q, :, :].rearrange("p h k -> p (h k)"), wvT[:, :],
                                start=True, stop=True)
                        if k == 9:
                            for t in range(NT_B):
                                nc.tensor.matmul(o[:, (t + 1) * D:(t + 2) * D], aT[:, WIN + t * P:WIN + (t + 1) * P],
                                                 wvT[:, :], start=True, stop=True)
                            last = nc.tensor.matmul(o[:, 3 * D:4 * D], aT[:, WIN:WIN + 1].broadcast_to([P, P]),
                                                    wvT[:, :], start=True, stop=True)
                    last.then_inc(pj_full, 1)

            def x_transposes(ffn, c):
                pe.wait_ge(ln_done, ffn * NC + c + 1)
                if not (ffn == 0 and isinstance(c, int)):
                    pe.wait_ge(b2_done, ffn * NC + c)
                for t in range(TT):
                    last = nc.tensor.transpose(pT[:, t * P:(t + 1) * P], xn[:, t, :], ident[:, :])
                last.then_inc(pT_full, 1)

            def logits(ffn, c):
                pe.wait_ge(xT_done, ffn * NC + c + 1)
                for t in range(TT):
                    last = nc.tensor.matmul(misc[:, t * E:(t + 1) * E], xT[:, t * P:(t + 1) * P], wr[:, :],
                                            start=True, stop=True)
                last.then_inc(lg_full, 1)

            def gate_transposes(ffn, c):
                pe.wait_ge(gates_done, ffn * NC + c + 1)
                for t in range(TT):
                    last = nc.tensor.transpose(misc[0:E, t * P:(t + 1) * P], gnew[:, t, :], ident[:, :])
                last.then_inc(gT_full, 1)

            def b2_rows(ffn, c):
                pe.wait_ge(b2s_done, 1)
                pe.wait_ge(gT_done, ffn * NC + c + 1)
                for t in range(TT):
                    last = nc.tensor.matmul(pT[:, t * D:(t + 1) * D], gT[:, t * P:(t + 1) * P], b2s[:, :],
                                            start=True, stop=True)
                last.then_inc(b2_full, 1)

            def up(ffn, c, e):
                step = ffn * STEPS + c * E + e
                first = ffn == 0 and isinstance(c, int) and c == 0 and e == 0
                if e == 0:
                    pe.wait_ge(xl_done, ffn * NC + c + 1)
                xs_h, xs_l = xh[:, bass.ds(c * TOK, TOK)], xl[:, bass.ds(c * TOK, TOK)]
                for j in range(HC):
                    if not first:
                        pe.wait_ge(r_done, HC * (step - 1) + j + 1)
                    hs = slice(j * P, (j + 1) * P)
                    nc.tensor.matmul(z[j][:, :], w1h[:, e, hs], xs_h, start=True, stop=False)
                    nc.tensor.matmul(z[j][:, :], w1h[:, e, hs], xs_l, start=False, stop=False)
                    nc.tensor.matmul(z[j][:, :], w1l[:, e, hs], xs_h, start=False, stop=True).then_inc(z_full, 1)

            def down(ffn, c, e):
                step = ffn * STEPS + c * E + e
                if True:
                    pe.wait_ge(y_done, step - 1 + Y0)
                for t in range(TT):
                    ts = slice(t * P, (t + 1) * P)
                    o = y[e % 2][:, t * D:(t + 1) * D]
                    for j in range(HC):
                        if t == 0:
                            pe.wait_ge(rl_done, HC * step + j + 1 + R0)
                        nc.tensor.matmul(o, rh[:, e % 2, j, ts], w2h[:, e, j, :], start=(j == 0), stop=False)
                        nc.tensor.matmul(o, rh[:, e % 2, j, ts], w2l[:, e, j, :], start=False, stop=False)
                        last = nc.tensor.matmul(o, rl[:, e % 2, j, ts], w2h[:, e, j, :], start=False,
                                                stop=(j == HC - 1))
                last.then_inc(y_full, 1)

            def body(ffn, c, last):
                for e in range(E):
                    if not last:
                        if e == 1:
                            x_transposes(ffn, c + 1)
                        if e == 2:
                            logits(ffn, c + 1)
                        if e == 5:
                            gate_transposes(ffn, c + 1)
                        if e == 6:
                            b2_rows(ffn, c + 1)
                    if e < E - 1:
                        up(ffn, c, e + 1)
                    elif not last:
                        up(ffn, c + 1, 0)
                    down(ffn, c, e)

            for ffn in range(2):
                if ffn:
                    pe.wait_ge(y_done, STEPS + Y0)
                    batches(pe, attention_step)
                    pe.wait_ge(res_done, B)
                x_transposes(ffn, 0)
                logits(ffn, 0)
                if ffn == 0:
                    pe.wait_ge(s_wl, 2)
                up(ffn, 0, 0)
                gate_transposes(ffn, 0)
                b2_rows(ffn, 0)
                chunks(pe, ffn, body)


_INS = ['L0_attn_x', 'L0_attn_Wq', 'L0_attn_Wk', 'L0_attn_Wv', 'L0_attn_Wo', 'L0_ffn_Wr', 'L0_ffn_br', 'L0_ffn_W1',
        'L0_ffn_b1', 'L0_ffn_W2', 'L0_ffn_b2']
_OUTS = [((16, 256, 128), 'float32')]


def kernel(**inputs):
    import numpy as _np
    import concourse.bacc as _bacc
    from concourse import mybir as _mybir
    from concourse.bass_utils import run_bass_kernel_spmd as _run

    nc = _bacc.Bacc("TRN2", target_bir_lowering=False, num_devices=1)
    arrays, args = {}, []
    for name in _INS:
        a = _np.ascontiguousarray(inputs[name])
        arrays[f"in_{name}_dram"] = a
        args.append(nc.dram_tensor(f"in_{name}_dram", a.shape, _mybir.dt.from_np(a.dtype), kind="ExternalInput").ap())
    for i, (shape, dtype) in enumerate(_OUTS):
        dt = _mybir.dt.from_np(_np.dtype(dtype))
        args.append(nc.dram_tensor(f"out_{i}_dram", shape, dt, kind="ExternalOutput").ap())
    macaron_kernel(nc, *args)
    r = _run(nc, [arrays], core_ids=[0])
    got = tuple(r.results[0][f"out_{i}_dram"] for i in range(len(_OUTS)))
    return got[0]
```

```python
from contextlib import ExitStack

import concourse.bass as bass
from concourse import mybir

ALU = mybir.AluOpType
ACT = mybir.ActivationFunctionType
AX = mybir.AxisListType
F32 = mybir.dt.float32
F16 = mybir.dt.float16
BF16 = mybir.dt.bfloat16
I32 = mybir.dt.int32

P = 128
WSCALE = 64.0
EPS = 1e-5
BIG = 3.0e38
NOT_SEEN = -1.0e30


def macaron_kernel(nc, x, Wq, Wk, Wv, Wo, Wr, br, W1, b1, W2, b2, out):
    B, S, D = x.shape
    E, _, H = W1.shape
    NT = B * S // P
    EB = (E - 1).bit_length()
    HC = H // P
    SLOT_T = 2 * P
    SH = SLOT_T // P
    TOPK = 2
    TILES = B * S * TOPK // SLOT_T + E - 1
    REGION = B * S + SLOT_T
    AHEAD = 4
    PAIRS = (TILES - AHEAD) // 2
    HD, NH, WIN = 8, 16, 16
    HP, HG = 4, 4
    QB = 32
    NQ = S // QB
    NT_B = S // P
    W = (2 * NT_B, NT_B)
    UNITS = (NT // W[0], NT // W[1])
    BASE = (0, UNITS[0])
    UT = NT_B
    NM = NT_B * NH
    PADS = S + 2 * WIN
    SLOTS = 9
    x_v = x.rearrange("b s d -> (b s) d").rearrange("(n p) d -> p n d", p=P)
    out_v = out.rearrange("b s d -> (b s) d").rearrange("(n p) d -> p n d", p=P)

    with ExitStack() as ctx:
        def sb(name, shape, dt=F32):
            return ctx.enter_context(nc.sbuf_tensor(name, shape, dt))

        def sem(name):
            return ctx.enter_context(nc.semaphore(name))

        xres = sb("xres", [P, NT, D])
        w1f = sb("w1f", [P, E, H])
        w1h, w1l = sb("w1h", [P, E, H], F16), sb("w1l", [P, E, H], F16)
        w2f = sb("w2f", [P, E, HC, D])
        w2h, w2l = sb("w2h", [P, E, HC, D], F16), sb("w2l", [P, E, HC, D], F16)
        b1n = sb("b1n", [E * HC, P])
        b1T = sb("b1T", [P, E * HC])
        wr = sb("wr", [P, E])
        br_bc = sb("br_bc", [P, E])
        b2s = sb("b2s", [E, D])
        gsum, gtmp = sb("gsum", [P, W[0], E]), sb("gtmp", [P, W[0], E])
        gsT = sb("gsT", [E, W[0] * P])
        ident = sb("ident", [P, P])
        before = sb("before", [P, P], F16)
        ones16 = sb("ones16", [P, P], F16)
        tie = sb("tie", [P, E])
        region0 = sb("region0", [P, E])
        exp_no = sb("exp_no", [P, E])
        tri_e = sb("tri_e", [P, E, E])
        tile_no = sb("tile_no", [P, TILES])
        zeros = sb("zeros", [P, SH, D])
        xn = sb("xn", [P, NT, D])
        xT = sb("xT", [P, 2, W[0] * P])
        stats = sb("stats", [P, NT, 6])
        mean, dif, rstd, var, half, newton = (sb(n, [P, NT]) for n in ("mean", "dif", "rstd", "var", "half", "newton"))
        guess = sb("guess", [P, NT], I32)
        lg, lg2, eq = (sb(n, [P, W[0], E]) for n in ("lg", "lg2", "eq"))
        one = sb("one", [P, TOPK, NT, E])
        both = sb("both", [P, 2, W[0], E], F16)
        m1, m2, pick, den = (sb(n, [P, W[0]]) for n in ("m1", "m2", "pick", "den"))
        edelta, e2 = sb("edelta", [P, 2, W[0]]), sb("e2", [P, 2, W[0]])
        gate = sb("gate", [P, TOPK, NT])
        place = sb("place", [P, W[0], E])
        taken = sb("taken", [P, E])
        slot = sb("slot", [P, TOPK, NT])
        slot_i = sb("slot_i", [P, 2, TOPK, W[0]], I32)
        cnt, cnt_f, cum, cum_ex, shift = (sb(n, [P, E]) for n in ("cnt", "cnt_f", "cum", "cum_ex", "shift"))
        cnt_i = sb("cnt_i", [P, E], I32)
        tri_w = sb("tri_w", [P, E, E])
        b1_t = sb("b1_t", [P, TILES, HC])
        t_e, t_sum, t_ok, t_pack = (sb(n, [P, TILES]) for n in ("t_e", "t_sum", "t_ok", "t_pack"))
        tab_e, tab_row = sb("tab_e", [1, TILES], I32), sb("tab_row", [1, TILES], I32)
        pad_row = sb("pad_row", [1, E], I32)
        pickw = sb("pickw", [P, NT, E])
        ysl = sb("ysl", [P, TOPK, NT])
        carrier = sb("carrier", [P, 2])
        yix = sb("yix", [P, 2, TOPK, UT], I32)
        xg = sb("xg", [P, 2, SH, D])
        gh, gl = sb("gh", [P, 2, SLOT_T], F16), sb("gl", [P, 2, SLOT_T], F16)
        r = sb("r", [P, 2, HC, SLOT_T])
        rh, rl = sb("rh", [P, 2, HC, SLOT_T], F16), sb("rl", [P, 2, HC, SLOT_T], F16)
        ysb = sb("ysb", [P, 2, SH, D])
        yg = sb("yg", [P, 2, TOPK, UT, D])
        xs = nc.dram_tensor("dispatch_rows", [E * REGION, D], F32).ap()
        ys = nc.dram_tensor("expert_rows", [TILES * SLOT_T, D], F32).ap()

        psum = ctx.enter_context(nc.psum_tensor("psum", [P, 8, 512], F32))
        banks = [psum[:, i, :] for i in range(8)]
        z = banks[0:4]
        y = banks[4:6]
        gT = banks[6:8]

        O_N, S0_AT, MT_AT, LG_AT, PX_AT = NT_B * HG * HP * (HD + 1), 288, 320, 352, 384

        wnat = sb("wnat", [P, 4, D])
        wqr, wkr = sb("wqr", [P, HG, P]), sb("wkr", [P, HG, P])
        wvT, woT = sb("wvT", [P, D]), sb("woT", [P, D])
        identb = sb("identb", [P, P], BF16)
        maskb = sb("maskb", [P, NQ, 2 * QB], BF16)
        strip = sb("strip", [P, HP])
        strip16 = sb("strip16", [P, HG, NH])
        headrow = sb("headrow", [NH, D])
        fold = sb("fold", [P, QB])
        row_no = sb("row_no", [P, 1], I32)
        row_bit = sb("row_bit", [P, 2], I32)
        neg_q, neg_k = sb("neg_q", [P, 1]), sb("neg_k", [P, 1])
        ones = sb("ones", [P, 1])
        axn = sb("axn", [P, 2, D])
        aT = sb("aT", [P, PADS])
        aTr = sb("aTr", [P, NQ + 1, HP, QB])
        hi_q, hi_k = sb("hi_q", [P, 2, 2 * S], F16), sb("hi_k", [P, HG, PADS], F16)
        qrow = sb("qrow", [P, 2, HG, S], F16)
        krow = sb("krow", [P, 2, HG, PADS], F16)
        k0 = sb("k0", [P, 2, HG, HP], F16)
        q0 = sb("q0", [P, 2, HG, NH], F16)
        vbd = sb("vbd", [P, 2, NQ + 1, HG, HP, HD + 1])
        vp = sb("vp", [P, 2, 3, D])
        mx = sb("mx", [P, HG, NQ])
        mxd = sb("mxd", [P, NQ, HG, HP])
        prob = sb("prob", [P, HG * NQ, 2 * QB])
        probT = sb("probT", [P, HG * NQ, 2, QB])
        past, past_w = (prob[:, k * 16:k * 16 + 16, :].rearrange("p n c -> p (n c)")[:, 0:TILES * E]
                        .rearrange("p (t e) -> p t e", e=E) for k in range(2))
        b1_w = probT[:, :, :, :].rearrange("p n a q -> p (n a q)")[:, 0:TILES * HC * E].rearrange(
            "p (t j e) -> p t j e", t=TILES, e=E)
        o_sb = sb("o_sb", [P, MT_AT + NM])
        ahead = sb("ahead", [P, NM])
        dd = sb("dd", [P, 2, NM])
        ee = sb("ee", [P, 2, NM])
        al, mden, mrec = sb("al", [P, NM]), sb("mden", [P, NM]), sb("mrec", [P, NM])
        ar, cr = sb("ar", [P, NM]), sb("cr", [P, NM])
        t2 = sb("t2", [P, 2, D])
        att = sb("att", [P, 2, D])
        atT = sb("atT", [P, S])
        g_neg, g_sum, g_rec = sb("g_neg", [NH, 1]), sb("g_sum", [NH, 1]), sb("g_rec", [NH, 1])
        g_exp, g_prob = sb("g_exp", [NH, S]), sb("g_prob", [NH, S])
        g_pT = sb("g_pT", [P, 2, NH])
        g_out = sb("g_out", [NH, D])

        sc = psum[:, 0:4, :]
        pj = banks[4:6]
        slots = (None, *banks[4:6], *banks[0:4], *banks[4:6], banks[0])
        ob = banks[6]
        gb = banks[7]

        s_x = [sem(f"s_x{k}") for k in range(4)]
        s_w, s_r = sem("s_w"), sem("s_r")
        s_const = sem("s_const")
        s_setup = sem("s_setup")
        s_w1h, s_w2h, s_wl = sem("s_w1h"), sem("s_w2h"), sem("s_wl")
        ln_chain, ln_done = sem("ln_chain"), sem("ln_done")
        pT_full, xT_done = sem("pT_full"), sem("xT_done")
        lg_full, route_chain, delta_done, both_done, e2_done = (
            sem(n) for n in ("lg_full", "route_chain", "delta_done", "both_done", "e2_done"))
        px_full, place_chain, slot_done = sem("px_full"), sem("place_chain"), sem("slot_done")
        scattered = [sem(f"scattered{u}") for u in range(2)]
        gsum_chain, gsum_done, gsT_full, gsT_done, b2_full, b2_done, b2s_done = (
            sem(n) for n in ("gsum_chain", "gsum_done", "gsT_full", "gsT_done", "b2_full", "b2_done", "b2s_done"))
        table_chain, table_done, padded = sem("table_chain"), sem("table_done"), sem("padded")
        loaded, stored = [sem(f"loaded{u}") for u in range(2)], [sem(f"stored{u}") for u in range(2)]
        gT_full, gh_done, gl_done = sem("gT_full"), sem("gh_done"), sem("gl_done")
        z_full, r_done, rh_done, rl0_done, rl1_done = (
            sem(n) for n in ("z_full", "r_done", "rh_done", "rl0_done", "rl1_done"))
        y_full, y_done = sem("y_full"), sem("y_done")
        yix_done, gathered, add_chain, added = (
            sem("yix_done"), [sem(f"gathered{u}") for u in range(2)], sem("add_chain"), sem("added"))
        s_out = sem("s_out")
        carried = [sem("carried_scatter"), sem("carried_gather")]
        c_pool, c_dve, wT_full, wT_done, masks_done = (sem(n) for n in ("c_pool", "c_dve", "wT_full", "wT_done", "masks_done"))
        aln_chain, aln_done, aT_full, aT_done = (sem(n) for n in ("aln_chain", "aln_done", "aT_full", "aT_done"))
        pj_full, hi_done, qk_done, vb_done, vp_done, bd_done = (
            sem(n) for n in ("pj_full", "hi_done", "qk_done", "vb_done", "vp_done", "bd_done"))
        sc_full, mx_done, mxd_done, sub_done, exp_done, pt_done = (
            sem(n) for n in ("sc_full", "mx_done", "mxd_done", "sub_done", "exp_done", "pt_done"))
        gs_full, gneg_done, gexp_done, g_chain, p0_done, p0T_full, p0T_done, go_full, gm_done = (
            sem(n) for n in ("gs_full", "gneg_done", "gexp_done", "g_chain", "p0_done", "p0T_full", "p0T_done",
                             "go_full", "gm_done"))
        o_full, mg_chain, dd_done, ee_done, mden_done, mrec_done, att_done = (
            sem(n) for n in ("o_full", "mg_chain", "dd_done", "ee_done", "mden_done", "mrec_done", "att_done"))
        atT_full, atT_done, wo_full, res_done = (sem(n) for n in ("atT_full", "atT_done", "wo_full", "res_done"))
        aTr_done = sem("aTr_done")

        signs_chain, lack_done, ob_done, beside = (
            sem(n) for n in ("signs_chain", "lack_done", "ob_done", "beside"))
        NEWTON = 3
        MG_LINKS = 5
        LN_LINKS = 1 + 7 + 3 + 3 * NEWTON
        ROUTE_LINKS = 12
        PLACE_LINKS = 9
        TABLE_LINKS = 24
        N_W = 7
        b1t_chain, b1t_done = sem("b1t_chain"), sem("b1t_done")
        ysl_chain, ysl_last = sem("ysl_chain"), sem("ysl_last")
        b1_full, b1_done = sem("b1_full"), sem("b1_done")

        def moments(stats, mean, dif, var, link, settle):
            link(nc.vector.tensor_tensor(mean[:, :], stats[:, :, 1], stats[:, :, 4], ALU.add))
            link(nc.vector.tensor_tensor(dif[:, :], stats[:, :, 1], stats[:, :, 4], ALU.subtract))
            link(nc.vector.tensor_tensor(var[:, :], stats[:, :, 2], stats[:, :, 5], ALU.add))
            settle()
            link(nc.vector.tensor_scalar(mean[:, :], mean[:, :], 0.5, None, ALU.mult))
            link(nc.vector.tensor_tensor(dif[:, :], dif[:, :], dif[:, :], ALU.mult))
            link(nc.vector.tensor_scalar(var[:, :], var[:, :], 1.0 / D, EPS, ALU.mult, ALU.add))
            settle()
            link(nc.vector.scalar_tensor_tensor(out=var[:, :], in0=dif[:, :], scalar=0.25, in1=var[:, :],
                                                op0=ALU.mult, op1=ALU.add))
            settle()

        def rsqrt(out, var, half, guess, newton, link, settle):
            link(nc.vector.tensor_scalar(half[:, :], var[:, :], -0.5, None, ALU.mult))
            link(nc.vector.tensor_scalar(guess[:, :], var[:, :].bitcast(I32), 1, None, ALU.logical_shift_right))
            settle()
            link(nc.vector.tensor_scalar(out[:, :].bitcast(I32), guess[:, :], -1, 0x5F3759DF, ALU.mult, ALU.add))
            settle()
            for _ in range(NEWTON):
                link(nc.vector.tensor_tensor(newton[:, :], out[:, :], out[:, :], ALU.mult))
                settle()
                link(nc.vector.tensor_tensor(newton[:, :], newton[:, :], half[:, :], ALU.mult))
                settle()
                link(nc.vector.scalar_tensor_tensor(out=out[:, :], in0=newton[:, :], scalar=1.5, in1=out[:, :],
                                                    op0=ALU.add, op1=ALU.mult))
                settle()

        block = ctx.enter_context(nc.Block())

        def batches(eng, step):
            def some(i):
                step(i, 1 - i % 2, *(0 <= i + n < B for n in (2, 1, 0, -1, -2)))

            for i in range(-2, 3):
                some(i)
            with eng.Fori(0, (B - 5) // 2) as pair:
                step(3 + pair * 2, 0, True, True, True, True, True)
                step(4 + pair * 2, 1, True, True, True, True, True)
            for i in range(3 + (B - 5) // 2 * 2, B + 2):
                some(i)

        def par(i, odd):
            return i % 2 if isinstance(i, int) else 1 - odd

        def route_beats(beat):
            for k in range(UNITS[0] + 3):
                beat(k, k % 2)

        def there(k):
            return 0 <= k < UNITS[0]

        def place_of(ffn, m, u, t):
            return m * W[0] + t if ffn == 0 else u * W[1] + t

        def tiles(eng, step):
            for t in range(2):
                step(t, t, AHEAD)
            with eng.Fori(1, PAIRS) as pair:
                step(pair * 2, 0, AHEAD)
                step(pair * 2 + 1, 1, AHEAD)
            for t in range(2 * PAIRS, TILES):
                step(t, t % 2, min(AHEAD, TILES - 1 - t))

        def pairs_ahead(eng, step):
            with eng.Fori(0, B // 2 - 1) as pair:
                step(pair)
            step(B // 2 - 1)

        def unit_pairs(eng, step):
            step(0)
            with eng.Fori(1, B // 2) as pair:
                step(pair)

        UNIT_DMAS = 16 * TOPK * UT

        def scattered_by(ffn, m, u):
            before_ = sum(16 * TOPK * W[f] * UNITS[f] // 2 for f in range(ffn))
            return before_ + 8 * TOPK * W[ffn] * (m - u)

        def wait_some(eng, s, value):
            if not (isinstance(value, int) and value <= 0):
                eng.wait_ge(s, value)

        @block.sync
        def _(sp):
            for k in range(4):
                n = NT // 4
                sp.dma_start(xres[:, k * n:(k + 1) * n, :], x_v[:, k * n:(k + 1) * n, :]).then_inc(s_x[k], 16)
            sp.dma_start(wr[:, :], Wr).then_inc(s_r, 16)
            sp.dma_start(br_bc[:, :], br[None, :].broadcast_to([P, E])).then_inc(s_r, 16)
            sp.dma_start(b2s[:, :], b2).then_inc(s_r, 16)
            sp.dma_start(w1f[:, :, :], W1.rearrange("e d h -> d e h")).then_inc(s_w, 16)
            sp.dma_start(w2f[:, :, :, :], W2.rearrange("e (j p) d -> p e j d", p=P)).then_inc(s_w, 16)
            sp.dma_start(b1n[:, :], b1.rearrange("e (j p) -> (e j) p", p=P)).then_inc(s_w, 16)
            for k, w in enumerate((Wq, Wk, Wv, Wo)):
                sp.dma_start(wnat[:, k, :], w).then_inc(s_w, 16)

            def rows(table, n, top):
                return nc.values_load_multi_w_load_instructions(table, engines=(mybir.EngineType.SP,), min_val=0,
                                                                max_val=top)[1]

            def load(row, u):
                sp.dma_start(xg[:, u, :, :], xs[bass.ds(row, SLOT_T), :].rearrange("(s p) d -> p s d", p=P)
                             ).then_inc(loaded[u], 16)

            def store(t, u):
                sp.dma_start(ys[bass.ds(t * SLOT_T, SLOT_T), :].rearrange("(s p) d -> p s d", p=P),
                             ysb[:, u, :, :]).then_inc(stored[u], 16)

            for ffn in range(2):
                sp.wait_ge(table_done, ffn + 1)
                for u in range(2):
                    sp.wait_ge(scattered[u], scattered_by(ffn, UNITS[ffn] + u, u))
                pads = rows(pad_row[0:1, :], E, E * REGION - SLOT_T)
                first = rows(tab_row[0:1, 0:AHEAD], AHEAD, E * REGION - SLOT_T)
                for row in pads:
                    sp.dma_start(xs[bass.ds(row, SLOT_T), :].rearrange("(s p) d -> p s d", p=P), zeros[:, :, :]
                                 ).then_inc(padded, 16)
                sp.wait_ge(padded, 16 * E * (ffn + 1))
                for t in range(2):
                    load(first[t], t)
                for t in range(2):
                    sp.wait_ge(gT_full, ffn * TILES + t + 1)
                    load(first[2 + t], t)

                def step(t, u, left):
                    if left >= AHEAD:
                        row, = rows(tab_row[0:1, bass.ds(t + AHEAD, 1)], 1, E * REGION - SLOT_T)
                        sp.wait_ge(gT_full, ffn * TILES + t + 3)
                        load(row, u)
                    sp.wait_ge(y_done, ffn * TILES + t + 1)
                    store(t, u)

                tiles(sp, step)
            for k in range(4):
                sp.wait_ge(added, B + B // 4 * (k + 1))
                n = NT // 4
                sp.dma_start(out_v[:, k * n:(k + 1) * n, :], xres[:, k * n:(k + 1) * n, :]).then_inc(s_out, 16)
            sp.wait_ge(s_out, 16 * 4)

        @block.gpsimd
        def _(pool):
            nc.gpsimd.memset(ident[:, :], 0.0).then_inc(s_setup, 1)
            nc.gpsimd.iota(tie[:, :], [[-1, E]], base=E, channel_multiplier=0,
                           allow_small_or_imprecise_dtypes=True).then_inc(s_const, 1)
            pool.wait_ge(s_setup, 1)
            nc.gpsimd.affine_select(out=ident[:, :], in_=ident[:, :], compare_op=ALU.not_equal, fill=1.0, base=0,
                                    pattern=[[-1, P]], channel_multiplier=1).then_inc(s_const, 1)
            for a, v in ((ones16, 1.0), (before, 1.0), (tri_e, 1.0), (zeros, 0.0)):
                nc.gpsimd.memset(a[:], v).then_inc(s_setup, 1)
            pool.wait_ge(s_setup, 5)
            nc.gpsimd.affine_select(out=before[:, :], in_=before[:, :], compare_op=ALU.is_ge, fill=0.0, base=-1,
                                    pattern=[[1, P]], channel_multiplier=-1).then_inc(s_const, 1)
            nc.gpsimd.affine_select(out=tri_e[:, :, :], in_=tri_e[:, :, :], compare_op=ALU.is_ge, fill=0.0, base=0,
                                    pattern=[[1, E], [-1, E]], channel_multiplier=0).then_inc(s_const, 1)
            nc.gpsimd.iota(region0[:, :], [[REGION, E]], base=0, channel_multiplier=0,
                           allow_small_or_imprecise_dtypes=True).then_inc(s_const, 1)
            nc.gpsimd.iota(exp_no[:, :], [[1, E]], base=0, channel_multiplier=0,
                           allow_small_or_imprecise_dtypes=True).then_inc(s_const, 1)
            nc.gpsimd.iota(tile_no[:, :], [[1, TILES]], base=0, channel_multiplier=0,
                           allow_small_or_imprecise_dtypes=True).then_inc(s_const, 1)
            n = [0]

            def settle(ins):
                ins.then_inc(c_pool, 1)
                n[0] += 1
                pool.wait_ge(c_pool, n[0])

            for c in range(2):
                nc.gpsimd.memset(carrier[:, c:c + 1], 0.0).then_inc(carried[c], 1)
            nc.gpsimd.iota(row_no[:, :], [[0, 1]], base=0, channel_multiplier=1).then_inc(c_pool, 1)
            nc.gpsimd.memset(aT[:, :], 0.0).then_inc(c_pool, 1)
            nc.gpsimd.memset(vbd[:, :, :, :, :, :], 0.0).then_inc(c_pool, 1)
            nc.gpsimd.memset(strip[:, :], 0.0).then_inc(c_pool, 1)
            nc.gpsimd.memset(strip16[:, :, :], 0.0).then_inc(c_pool, 1)
            nc.gpsimd.memset(headrow[:, :], 1.0).then_inc(c_pool, 1)
            nc.gpsimd.memset(ones[:, :], 1.0).then_inc(c_pool, 1)
            nc.gpsimd.memset(maskb[:, :, :], 0.0).then_inc(c_pool, 1)
            n[0] = 8
            pool.wait_ge(c_pool, 8)
            s16 = strip16[:, :, :].rearrange("p g h -> p (g h)")
            for j in range(HP):
                sj = slice(QB * j, QB * (j + 1))
                settle(nc.gpsimd.memset(strip[sj, j:j + 1], 1.0))
                settle(nc.gpsimd.memset(s16[sj, j:j + 3 * (NH + HP) + 1:NH + HP], 1.0))
                for base, step, mult in ((0, 1, -1), (2 * WIN, -1, 1)):
                    settle(nc.gpsimd.affine_select(out=maskb[sj, :, :], in_=maskb[sj, :, :], compare_op=ALU.is_ge,
                                                   fill=NOT_SEEN, base=base, pattern=[[0, NQ], [step, 2 * QB]],
                                                   channel_multiplier=mult))
            for base, step in ((-WIN - 1, 1), (S - 1 + WIN, -1)):
                settle(nc.gpsimd.affine_select(out=maskb[:, :, :], in_=maskb[:, :, :], compare_op=ALU.is_ge,
                                               fill=NOT_SEEN, base=base, pattern=[[step * QB, NQ], [step, 2 * QB]],
                                               channel_multiplier=0))
            for base, step, mult in ((0, 1, -HD), (HD - 1, -1, HD)):
                settle(nc.gpsimd.affine_select(out=headrow[:, :], in_=headrow[:, :], compare_op=ALU.is_ge, fill=0.0,
                                               base=base, pattern=[[step, D]], channel_multiplier=mult))
            pool.wait_ge(s_const, 7)
            settle(nc.gpsimd.tensor_copy(identb[:, :], ident[:, :]))
            for j in range(HP):
                sj = slice(QB * j, QB * (j + 1))
                for u in range(2):
                    settle(nc.gpsimd.memset(vbd[sj, u, :, :, j, HD], 1.0))
                settle(nc.gpsimd.tensor_copy(fold[sj, :], ident[sj, sj]))
            nc.gpsimd.memset(row_bit[:, :], 0).then_inc(masks_done, 1)

            def attention_step(i, odd, fetch, project, middle, finish, route):
                if finish:
                    pool.wait_ge(ob_done, i)
                    nc.gpsimd.tensor_tensor(ahead[:, :], o_sb[:, S0_AT:S0_AT + NM], o_sb[:, MT_AT:MT_AT + NM],
                                            ALU.subtract).then_inc(dd_done, 1)
                if project:
                    pool.wait_ge(aT_done, i + 2)
                    if middle:
                        pool.wait_ge(pj_full, SLOTS * (i + 1))
                    nc.gpsimd.tensor_tensor(
                        aTr[:, :, :, :],
                        aT[:, :].rearrange("p (q k) -> p q k", k=QB)[:, :, None, :].broadcast_to([P, NQ + 1, HP, QB]),
                        ones[:, :, None, None].broadcast_to([P, NQ + 1, HP, QB]), ALU.mult).then_inc(aTr_done, 1)
                if finish:
                    merge(i - 1, 1 - par(i, odd))
                if middle:
                    pool.wait_ge(mx_done, i + 1)
                    if finish:
                        pool.wait_ge(o_full, i)
                    nc.gpsimd.tensor_tensor(
                        mxd[:, :, :, :], mx[:, :, :].rearrange("p g q -> p q g")[:, :, :, None].broadcast_to([P, NQ, HG, HP]),
                        strip[:, None, None, :].broadcast_to([P, NQ, HG, HP]), ALU.mult).then_inc(mxd_done, 1)
                if project:
                    u = 1 - par(i, odd)
                    pool.wait_ge(qk_done, 6 * (i + 1) + 6)
                    nc.gpsimd.tensor_tensor(k0[:, u, :, :], krow[:, u, :, WIN:WIN + 1].broadcast_to([P, HG, HP]),
                                            strip[:, None, :].broadcast_to([P, HG, HP]), ALU.mult).then_inc(bd_done, 1)
                    nc.gpsimd.tensor_tensor(q0[:, u, :, :], qrow[:, u, :, 0:1].broadcast_to([P, HG, NH]),
                                            strip16[:, :, :], ALU.mult).then_inc(bd_done, 1)
                if fetch:
                    gather(0, i + 2, par(i, odd))
                if route:
                    scatter(1, i - 2, par(i, odd))

            def merge(b, u):
                k = [b * MG_LINKS]

                def link(ins):
                    ins.then_inc(mg_chain, 1)
                    k[0] = k[0] + 1

                def settle():
                    pool.wait_ge(mg_chain, k[0])

                o = o_sb[:, 0:O_N].rearrange("p (n e) -> p n e", e=HD + 1)
                pool.wait_ge(ee_done, b + 1)
                link(nc.gpsimd.tensor_tensor(al[:, :], o[:, :, HD], ee[:, 0, :], ALU.mult))
                settle()
                nc.gpsimd.tensor_tensor(mden[:, :], al[:, :], ee[:, 1, :], ALU.add).then_inc(mden_done, 1)
                pool.wait_ge(mrec_done, b + 1)
                link(nc.gpsimd.tensor_tensor(ar[:, :], ee[:, 0, :], mrec[:, :], ALU.mult))
                link(nc.gpsimd.tensor_tensor(cr[:, :], ee[:, 1, :], mrec[:, :], ALU.mult))
                settle()
                if not (isinstance(b, int) and b == 0):
                    pool.wait_ge(atT_full, b)
                a = att[:, :, :].rearrange("p t (h d) -> p (t h) d", d=HD)
                link(nc.gpsimd.tensor_tensor(a, o[:, :, 0:HD], ar[:, :, None].broadcast_to([P, NM, HD]), ALU.mult))
                link(nc.gpsimd.tensor_tensor(
                    t2[:, :, :].rearrange("p t (h d) -> p t h d", d=HD),
                    vp[:, u, 2, :].rearrange("p (h d) -> p h d", d=HD)[:, None, :, :].broadcast_to([P, NT_B, NH, HD]),
                    cr[:, :].rearrange("p (t h) -> p t h", t=NT_B)[:, :, :, None].broadcast_to([P, NT_B, NH, HD]),
                    ALU.mult))
                settle()
                nc.gpsimd.tensor_tensor(att[:, :, :], att[:, :, :], t2[:, :, :], ALU.add).then_inc(att_done, 1)

            def wait_ahead_of_dma(s, value, c, nth):
                pool.wait_ge(carried[c], nth + 1)
                pool.wait_ge(s, value)
                nc.gpsimd.tensor_tensor(carrier[:, c:c + 1], ones[:, :], ones[:, :], ALU.mult).then_inc(carried[c], 1)

            def scatter(ffn, m, u):
                n = BASE[ffn] + m
                wait_ahead_of_dma(slot_done, n + 1, 0, n)
                for t in range(W[ffn]):
                    for k in range(TOPK):
                        pool.indirect_dma_start(
                            xs, bass.IndirectOffsetOnAxis(ap=slot_i[:, u, k, t:t + 1], axis=0),
                            xn[:, place_of(ffn, m, u, t), :], None).then_inc(scattered[u], 16)

            def scatter_beat(k, u):
                if there(k - 2):
                    scatter(0, k - 2, u)

            def gather(ffn, m, u):
                wait_some(pool, added, ffn * B + m - 1)
                wait_ahead_of_dma(yix_done, ffn * B + m + 1, 1, ffn * B + m)
                for t in range(UT):
                    for k in range(TOPK):
                        pool.indirect_dma_start(yg[:, u, k, t, :], None, ys,
                                                bass.IndirectOffsetOnAxis(ap=yix[:, u, k, t:t + 1], axis=0)
                                                ).then_inc(gathered[u], 16)

            def low_r(step, u):
                pool.wait_ge(rh_done, 2 * step + 1)
                nc.gpsimd.tensor_tensor(rl[:, u, 0:2, :], r[:, u, 0:2, :], rh[:, u, 0:2, :], ALU.subtract
                                        ).then_inc(rl0_done, 1)

            def tile_step(t, u, left):
                if left >= 1:
                    low_r(now[0] * TILES + t + 1, 1 - u)

            now = [0]
            route_beats(scatter_beat)
            for ffn in range(2):
                now[0] = ffn
                low_r(ffn * TILES, 0)
                tiles(pool, tile_step)
                for u in range(2):
                    pool.wait_ge(stored[u], 16 * (ffn + 1) * ((TILES + 1 - u) // 2))
                if ffn == 0:
                    batches(pool, attention_step)

            def gather_pair(pair):
                for u in range(2):
                    gather(1, pair * 2 + u, u)

            unit_pairs(pool, gather_pair)

        @block.scalar
        def _(act):
            def prepare_weights():
                act.wait_ge(s_w, 16 * N_W)
                nc.scalar.activation(w1h[:, :, :], w1f[:, :, :], ACT.Copy, scale=WSCALE).then_inc(s_w1h, 1)
                nc.scalar.activation(w2h[:, :, :, :], w2f[:, :, :, :], ACT.Copy, scale=WSCALE).then_inc(s_w2h, 1)


            def turn_weights():
                act.wait_ge(b1_full, 1)
                nc.scalar.copy(b1T[:, :], gT[1][:, 0:E * HC]).then_inc(b1_done, 1)
                act.wait_ge(wT_full, 1)
                for k, w in enumerate((wqr, wkr)):
                    nc.scalar.activation(
                        w[:, :, :].rearrange("p g (h r d) -> p (g h) r d", h=HP, d=HD),
                        z[0][:, k * D:(k + 1) * D].rearrange("p (h d) -> p h d", d=HD)[:, :, None, :]
                        .broadcast_to([P, NH, 4, HD]),
                        ACT.Copy, scale=HD ** -0.5 if k == 0 else 1.0).then_inc(wT_done, 1)
                nc.scalar.copy(wvT[:, :], z[0][:, 2 * D:3 * D]).then_inc(wT_done, 1)
                nc.scalar.copy(woT[:, :], z[0][:, 3 * D:4 * D]).then_inc(wT_done, 1)

            def attention_step(i, odd, fetch, project, middle, finish, route):
                b = i + 1
                if finish:
                    act.wait_ge(p0T_full, i)
                    nc.scalar.copy(g_pT[:, :, :], gb[:, 256:256 + 2 * NH].rearrange("p (t h) -> p t h", t=2)
                                   ).then_inc(p0T_done, 1)
                if finish:
                    act.wait_ge(o_full, i)
                    nc.scalar.copy(o_sb[:, :], ob[:, 0:MT_AT + NM]).then_inc(ob_done, 1)
                if project:
                    act.wait_ge(aT_full, b + 1)
                    nc.scalar.copy(aT[:, WIN:WIN + S], pj[0][:, 0:S]).then_inc(aT_done, 1)
                if finish:
                    act.wait_ge(dd_done, i)
                    nc.scalar.activation(dd[:, 0, :], ahead[:, :], ACT.Relu)
                    nc.scalar.activation(dd[:, 1, :], ahead[:, :], ACT.Relu, scale=-1.0).then_inc(lack_done, 1)
                    act.wait_ge(lack_done, i)
                    nc.scalar.activation(ee[:, :, :], dd[:, :, :], ACT.Exp, scale=-1.0).then_inc(ee_done, 1)
                if middle:
                    for h in range(2):
                        act.wait_ge(sub_done, 2 * i + h + 1)
                        half = prob[:, 16 * h:16 * h + 16, :]
                        nc.scalar.activation(half, half, ACT.Exp).then_inc(exp_done, 1)
                if project:
                    for k in (1, 2):
                        act.wait_ge(pj_full, SLOTS * b + k)
                        nc.scalar.copy(hi_q[:, k - 1, :], slots[k]).then_inc(hi_done, 1)
                if route:
                    route_x(1, i - 2, par(i, odd), banks[3])
                if project:
                    for k in range(3, 7):
                        act.wait_ge(pj_full, SLOTS * b + k)
                        nc.scalar.copy(hi_k[:, k - 3, :], slots[k][:, 0:PADS]).then_inc(hi_done, 1)
                    values(b, 1 - par(i, odd), finish)
                if middle:
                    act.wait_ge(gneg_done, i + 1)
                    nc.scalar.activation(g_exp[:, :], gb[0:NH, 0:S], ACT.Exp, bias=g_neg[:, 0:1], scale=1.0,
                                         accum_out=g_sum[:, 0:1]).then_inc(gexp_done, 1)
                if route:
                    route_e(1, i - 2, par(i, odd))
                if finish and not project:
                    turned_output(i)

            def values(b, u, finish):
                for k in range(7, 10):
                    act.wait_ge(pj_full, SLOTS * b + k)
                    q0_, m = 4 * (k - 7), (4 if k < 9 else 1)
                    for j in range(HP):
                        sj = slice(QB * j, QB * (j + 1))
                        last = nc.scalar.copy(
                            vbd[sj, u, q0_:q0_ + m, :, j, 0:HD].rearrange("p q g d -> p (q g) d"),
                            slots[k][sj, 0:m * D].rearrange("p (n h d) -> p n h d", h=HP, d=HD)[:, :, j, :])
                    last.then_inc(vb_done, 1)
                if finish:
                    act.wait_ge(att_done, b - 1)
                nc.scalar.copy(vp[:, u, :, :], slots[9][:, D:4 * D].rearrange("p (t d) -> p t d", t=3)
                               ).then_inc(vp_done, 1)
                if finish:
                    turned_output(b - 1)

            def turned_output(i):
                act.wait_ge(atT_full, i)
                nc.scalar.copy(atT[:, 1:S], pj[0][:, 1:S])
                nc.scalar.copy(atT[:, 0:1], pj[0][:, S:S + 1]).then_inc(atT_done, 1)

            def route_x(ffn, m, u, bank):
                act.wait_ge(pT_full, BASE[ffn] + m + 1)
                n = W[ffn] * P
                nc.scalar.copy(xT[:, u, 0:n], bank[:, 0:n]).then_inc(xT_done, 1)

            def route_e(ffn, m, u):
                n = W[ffn]
                act.wait_ge(delta_done, BASE[ffn] + m + 1)
                nc.scalar.activation(e2[:, u, 0:n], edelta[:, u, 0:n], ACT.Exp).then_inc(e2_done, 1)

            def b2_copy(ffn, m):
                act.wait_ge(gsT_full, BASE[ffn] + m + 1)
                n = W[ffn] * P
                nc.scalar.copy(gsT[:, 0:n], banks[6][0:E, 0:n]).then_inc(gsT_done, 1)

            def route_beat(k, u):
                if there(k):
                    route_x(0, k, u, banks[u])
                if there(k - 2):
                    b2_copy(0, k - 2)
                if there(k - 1):
                    route_e(0, k - 1, 1 - u)

            def high_g(step, u):
                act.wait_ge(gT_full, step + 1)
                nc.scalar.copy(gh[:, u, :], gT[u][:, 0:SLOT_T]).then_inc(gh_done, 1)

            def relu(t, u):
                step = now[0] * TILES + t
                for j in range(HC):
                    if j % 2 == 0:
                        act.wait_ge(z_full, 2 * step + j // 2 + 1)
                    if j == 0:
                        wait_some(act, rl0_done, step - 1)
                        wait_some(act, rl1_done, step - 1)
                    ins = nc.scalar.activation(r[:, u, j, :], z[2 * u + j // 2][:, (j % 2) * SLOT_T:(j % 2 + 1) * SLOT_T],
                                               ACT.Relu, bias=b1_t[:, bass.ds(t, 1), j], scale=1.0 / WSCALE)
                    if j % 2:
                        ins.then_inc(r_done, 1)

            def tile_step(t, u, left):
                if left >= 2:
                    high_g(now[0] * TILES + t + 2, u)
                if left >= 1:
                    relu(t + 1, 1 - u)

            now = [0]
            route_beats(route_beat)
            turn_weights()
            prepare_weights()
            for ffn in range(2):
                now[0] = ffn
                act.wait_ge(table_done, ffn + 1)
                high_g(ffn * TILES, 0)
                high_g(ffn * TILES + 1, 1)
                act.wait_ge(b1t_done, ffn + 1)
                relu(0, 0)
                tiles(act, tile_step)
                if ffn == 0:
                    batches(act, attention_step)

            def b2_pair(pair):
                for u in range(2):
                    b2_copy(1, pair * 2 + u)

            unit_pairs(act, b2_pair)

        @block.vector
        def _(dve):
            def prepare_weights():
                dve.wait_ge(s_w1h, 1)
                nc.vector.scalar_tensor_tensor(out=w1l[:, :, :], in0=w1f[:, :, :], scalar=WSCALE, in1=w1h[:, :, :],
                                               op0=ALU.mult, op1=ALU.subtract).then_inc(s_wl, 1)
                dve.wait_ge(s_w2h, 1)
                nc.vector.scalar_tensor_tensor(out=w2l[:, :, :, :], in0=w2f[:, :, :, :], scalar=WSCALE,
                                               in1=w2h[:, :, :, :], op0=ALU.mult, op1=ALU.subtract).then_inc(s_wl, 1)

            def row_signs():
                dve.wait_ge(masks_done, 1)
                for k, (bit, neg) in enumerate(((16, neg_q), (8, neg_k))):
                    nc.vector.tensor_scalar(row_bit[:, k:k + 1], row_no[:, :], bit, None, ALU.bitwise_and
                                            ).then_inc(signs_chain, 1)
                    dve.wait_ge(signs_chain, 2 * k + 1)
                    nc.vector.tensor_scalar(neg[:, :], row_bit[:, k:k + 1], -1.0 / bit, None, ALU.mult
                                            ).then_inc(signs_chain, 1)
                dve.wait_ge(signs_chain, 4)

            def stats_to_scale(n, k, ins):
                k = [k * LN_LINKS]

                def link(ins):
                    ins.then_inc(ln_chain, 1)
                    k[0] = k[0] + 1

                def settle():
                    dve.wait_ge(ln_chain, k[0])

                link(ins)
                settle()
                moments(stats[:, n, :], mean[:, n], dif[:, n], var[:, n], link, settle)
                rsqrt(rstd[:, n], var[:, n], half[:, n], guess[:, n], newton[:, n], link, settle)

            def normalise(out, c, at):
                return nc.vector.tensor_scalar(out, xres[:, bass.ds(c, 1), :], mean[:, at:at + 1], rstd[:, at:at + 1],
                                               ALU.subtract, ALU.mult)

            def batch_stats(b, at):
                for t in range(NT_B):
                    last = nc.vector.bn_stats(stats[:, at + t, :], xres[:, bass.ds(b * NT_B + t, 1), :])
                return last

            def first_stats():
                for t in range(NT):
                    if t % (NT // 4) == 0:
                        dve.wait_ge(s_x[t // (NT // 4)], 16)
                    last = nc.vector.bn_stats(stats[:, t, :], xres[:, t, :])
                stats_to_scale(slice(0, NT), 0, last)

            def first_norm(k):
                for t in range(k * W[0], (k + 1) * W[0]):
                    last = normalise(xn[:, t:t + 1, :], t, t)
                last.then_inc(ln_done, 1)

            def norms(i, u, project, route):
                b, m = i + 1, i - 2
                if project:
                    last = batch_stats(b, 0)
                else:
                    dve.wait_ge(res_done, m + 1)
                    last = batch_stats(m, NT_B)
                if route and project:
                    dve.wait_ge(beside, m + 1)
                stats_to_scale(slice(0 if project else NT_B, 2 * NT_B if route else NT_B), i + 2, last)
                if project:
                    if not (isinstance(b, int) and b == 0):
                        dve.wait_ge(aT_full, b)
                    for t in range(NT_B):
                        last = normalise(axn[:, t:t + 1, :], b * NT_B + t, t)
                    last.then_inc(aln_done, 1)
                if route:
                    dve.wait_ge(scattered[u], scattered_by(1, m, u))
                    for t in range(NT_B):
                        at = place_of(1, m, u, t)
                        last = normalise(xn[:, at:at + 1, :], m * NT_B + t, NT_B + t)
                    last.then_inc(ln_done, 1)

            def softmax_in(i):
                dve.wait_ge(sc_full, i + 1)
                if not (isinstance(i, int) and i == 0):
                    dve.wait_ge(mxd_done, i)
                    dve.wait_ge(pt_done, 2 * i)
                for h in range(2):
                    last = nc.vector.tensor_reduce(mx[:, 2 * h:2 * h + 2, :],
                                                   sc[:, 2 * h:2 * h + 2, :].rearrange("p g (q c) -> p g q c", q=NQ),
                                                   AX.X, ALU.max)
                last.then_inc(mx_done, 1)
                dve.wait_ge(mx_done, i + 1)
                for h in range(2):
                    nc.vector.tensor_tensor(
                        prob[:, 16 * h:16 * h + 16, :],
                        sc[:, 2 * h:2 * h + 2, :].rearrange("p g (q c) -> p (g q) c", q=NQ),
                        mx[:, 2 * h:2 * h + 2, :].rearrange("p g q -> p (g q)")[:, :, None].broadcast_to([P, 16, 2 * QB]),
                        ALU.subtract).then_inc(sub_done, 1)

            def queries_keys(b, u):
                for k in range(1, 7):
                    dve.wait_ge(hi_done, 6 * b + k)
                    if k < 3:
                        n, neg, high = 2 * S, neg_q, hi_q[:, k - 1, :]
                        out_rows = qrow[:, u, 2 * k - 2:2 * k, :].rearrange("p g t -> p (g t)")
                    else:
                        n, neg, high = PADS, neg_k, hi_k[:, k - 3, :]
                        out_rows = krow[:, u, k - 3, :]
                    nc.vector.scalar_tensor_tensor(out=out_rows, in0=high, scalar=neg[:, 0:1], in1=slots[k][:, 0:n],
                                                   op0=ALU.mult, op1=ALU.add).then_inc(qk_done, 1)

            def attention_step(i, odd, fetch, project, middle, finish, route):
                b = i + 1
                if project:
                    add_rows(0, b, 1 - par(i, odd), i - 2 if route else None)
                if fetch:
                    row_numbers(0, i + 2, par(i, odd))
                if project or route:
                    norms(i, par(i, odd), project, route)
                if middle:
                    softmax_in(i)
                if finish:
                    dve.wait_ge(mden_done, i)
                    nc.vector.reciprocal(mrec[:, :], mden[:, :]).then_inc(mrec_done, 1)
                    dve.wait_ge(go_full, i)
                    nc.vector.tensor_tensor(g_out[:, :], gb[0:NH, 288:288 + D], headrow[:, :], ALU.mult).then_inc(gm_done, 1)
                if middle:
                    if finish:
                        dve.wait_ge(o_full, i)
                    for h in range(2):
                        dve.wait_ge(exp_done, 2 * i + h + 1)
                        nc.vector.transpose(probT[:, 16 * h:16 * h + 16, :, :].rearrange("p n a q -> p (n a q)"),
                                            prob[:, 16 * h:16 * h + 16, :].rearrange("p n c -> p (n c)")).then_inc(pt_done, 1)
                if project:
                    queries_keys(b, 1 - par(i, odd))
                if route:
                    choose(1, i - 2, par(i, odd), ob[:, LG_AT:LG_AT + W[1] * E])
                if middle:
                    dve.wait_ge(gs_full, i + 1)
                    nc.vector.tensor_reduce(g_neg[:, :], gb[0:NH, 0:S], AX.X, ALU.max, negate=True).then_inc(gneg_done, 1)
                if route:
                    assign(1, i - 2, par(i, odd), ob[:, PX_AT:PX_AT + (W[1] + 1) * E])
                if middle:
                    dve.wait_ge(gexp_done, i + 1)
                    nc.vector.reciprocal(g_rec[:, :], g_sum[:, :]).then_inc(g_chain, 1)
                    dve.wait_ge(g_chain, i + 1)
                    if finish:
                        dve.wait_ge(p0T_full, i)
                    nc.vector.tensor_scalar(g_prob[:, :], g_exp[:, :], g_rec[:, 0:1], None, ALU.mult).then_inc(p0_done, 1)
                if finish:
                    dve.wait_ge(wo_full, i)
                    xr = xres[:, bass.ds((i - 1) * NT_B, NT_B), :]
                    nc.vector.tensor_tensor(xr, xr, pj[1][:, 0:S].rearrange("p (t d) -> p t d", t=NT_B),
                                            ALU.add).then_inc(res_done, 1)

            def choose(ffn, m, u, logits):
                n, w = BASE[ffn] + m, W[ffn]
                k = [n * ROUTE_LINKS]

                def link(ins):
                    ins.then_inc(route_chain, 1)
                    k[0] = k[0] + 1
                    dve.wait_ge(route_chain, k[0])

                def wide(a):
                    return a[:, 0:w, None].broadcast_to([P, w, E])

                tie_b = tie[:, None, :].broadcast_to([P, w, E])
                one1, one2 = (one[:, h, bass.ds(m * w, w), :] for h in range(TOPK))
                lg_, lg2_, eq_ = lg[:, 0:w, :], lg2[:, 0:w, :], eq[:, 0:w, :]
                m1_, m2_, pick_ = m1[:, 0:w], m2[:, 0:w], pick[:, 0:w]
                dve.wait_ge(lg_full, n + 1)
                link(nc.vector.tensor_tensor(lg_, logits.rearrange("p (t e) -> p t e", t=w),
                                             br_bc[:, None, :].broadcast_to([P, w, E]), ALU.add))
                link(nc.vector.tensor_reduce(m1_, lg_, AX.X, ALU.max))
                link(nc.vector.tensor_tensor(eq_, lg_, wide(m1), ALU.is_equal))
                link(nc.vector.tensor_tensor(eq_, eq_, tie_b, ALU.mult))
                link(nc.vector.tensor_reduce(pick_, eq_, AX.X, ALU.max))
                link(nc.vector.tensor_tensor(one1, tie_b, wide(pick), ALU.is_equal))
                link(nc.vector.scalar_tensor_tensor(out=lg2_, in0=one1, scalar=-BIG, in1=lg_, op0=ALU.mult, op1=ALU.add))
                link(nc.vector.tensor_reduce(m2_, lg2_, AX.X, ALU.max))
                nc.vector.tensor_tensor(edelta[:, u, 0:w], m2_, m1_, ALU.subtract)
                link(nc.vector.tensor_tensor(eq_, lg2_, wide(m2), ALU.is_equal))
                link(nc.vector.tensor_tensor(eq_, eq_, tie_b, ALU.mult))
                link(nc.vector.tensor_reduce(pick_, eq_, AX.X, ALU.max))
                link(nc.vector.tensor_tensor(one2, tie_b, wide(pick), ALU.is_equal))
                nc.vector.tensor_tensor(both[:, u, 0:w, :], one1, one2, ALU.add).then_inc(delta_done, 1)

            def assign(ffn, m, u, px):
                n, w = BASE[ffn] + m, W[ffn]
                k = [n * PLACE_LINKS]

                def link(ins):
                    ins.then_inc(place_chain, 1)
                    k[0] = k[0] + 1

                def settle():
                    dve.wait_ge(place_chain, k[0])

                at = bass.ds(m * w, w)
                place_, eq_ = place[:, 0:w, :], eq[:, 0:w, :]
                dve.wait_ge(px_full, n + 1)
                link(nc.vector.tensor_tensor(place_, px[:, 0:w * E].rearrange("p (t e) -> p t e", t=w),
                                             taken[:, None, :].broadcast_to([P, w, E]), ALU.add))
                settle()
                link(nc.vector.tensor_tensor(taken[:, :], taken[:, :], px[:, w * E:w * E + E], ALU.add))
                link(nc.vector.tensor_tensor(eq_, place_, one[:, 0, at, :], ALU.mult))
                link(nc.vector.tensor_tensor(lg2[:, 0:w, :], place_, one[:, 1, at, :], ALU.mult))
                settle()
                link(nc.vector.tensor_reduce(slot[:, 0, at], eq_, AX.X, ALU.add))
                link(nc.vector.tensor_reduce(slot[:, 1, at], lg2[:, 0:w, :], AX.X, ALU.add))
                settle()
                if ffn == 0:
                    wait_some(dve, scattered[u], scattered_by(0, m, u))
                nc.vector.tensor_scalar(slot_i[:, u, :, 0:w], slot[:, :, at], 0.0, None, ALU.add).then_inc(slot_done, 1)
                dve.wait_ge(e2_done, n + 1)
                link(nc.vector.tensor_scalar(den[:, 0:w], e2[:, u, 0:w], 1.0, 2.0 * WSCALE, ALU.add, ALU.mult))
                settle()
                link(nc.vector.reciprocal(gate[:, 0, at], den[:, 0:w]))
                settle()
                link(nc.vector.tensor_tensor(gate[:, 1, at], gate[:, 0, at], e2[:, u, 0:w], ALU.mult))

            def gate_sums(ffn, m):
                n, w = BASE[ffn] + m, W[ffn]
                at = bass.ds(m * w, w)
                if ffn == 0:
                    dve.wait_ge(place_chain, (n + 1) * PLACE_LINKS)
                wait_some(dve, gsT_full, n)
                for h, a in enumerate((gsum, gtmp)):
                    nc.vector.tensor_tensor(a[:, 0:w, :], one[:, h, at, :],
                                            gate[:, h, at][:, :, None].broadcast_to([P, w, E]), ALU.mult
                                            ).then_inc(gsum_chain, 1)
                dve.wait_ge(gsum_chain, n * 2 + 2)
                nc.vector.tensor_tensor(gsum[:, 0:w, :], gsum[:, 0:w, :], gtmp[:, 0:w, :], ALU.add).then_inc(gsum_done, 1)

            def add_b2(ffn, m):
                n, w = BASE[ffn] + m, W[ffn]
                dve.wait_ge(b2_full, n + 1)
                xr = xres[:, bass.ds(m * w, w), :]
                nc.vector.tensor_tensor(xr, xr, banks[7][:, 0:w * D].rearrange("p (t d) -> p t d", t=w), ALU.add
                                        ).then_inc(b2_done, 1)

            def route_beat(k, u):
                if there(k - 2):
                    assign(0, k - 2, u, banks[4 + u])
                if there(k - 1):
                    choose(0, k - 1, 1 - u, banks[3 - u][:, 0:W[0] * E])
                if there(k - 2):
                    gate_sums(0, k - 2)
                if there(k - 3):
                    add_b2(0, k - 3)
                if k >= 1 and there(k + 1):
                    first_norm(k + 1)

            def tile_table(ffn):
                k = [ffn * TABLE_LINKS]

                def link(ins):
                    ins.then_inc(table_chain, 1)
                    k[0] = k[0] + 1
                    dve.wait_ge(table_chain, k[0])

                V = nc.vector
                link(V.tensor_tensor(cnt[:, :], taken[:, :], region0[:, :], ALU.subtract))
                link(V.tensor_scalar(cnt_f[:, :], cnt[:, :], float(SLOT_T - 1), None, ALU.add))
                link(V.tensor_copy(cnt_i[:, :], cnt_f[:, :]))
                link(V.tensor_scalar(cnt_i[:, :], cnt_i[:, :], SLOT_T.bit_length() - 1, None, ALU.logical_shift_right))
                link(V.tensor_copy(cnt[:, :], cnt_i[:, :]))
                link(V.tensor_tensor(tri_w[:, :, :], tri_e[:, :, :], cnt[:, None, :].broadcast_to([P, E, E]), ALU.mult))
                link(V.tensor_reduce(cum[:, :], tri_w[:, :, :], AX.X, ALU.add))
                link(V.tensor_tensor(past[:, :, :], tile_no[:, :, None].broadcast_to([P, TILES, E]),
                                     cum[:, None, :].broadcast_to([P, TILES, E]), ALU.is_ge))
                link(V.tensor_tensor(past_w[:, :, :], past[:, :, :], cnt[:, None, :].broadcast_to([P, TILES, E]),
                                     ALU.mult))
                link(V.tensor_reduce(t_e[:, :], past[:, :, :], AX.X, ALU.add))
                link(V.tensor_reduce(t_sum[:, :], past_w[:, :, :], AX.X, ALU.add))
                link(V.tensor_scalar(t_ok[:, :], past[:, :, E - 1], -1.0, 1.0, ALU.mult, ALU.add))
                link(V.tensor_tensor(t_sum[:, :], tile_no[:, :], t_sum[:, :], ALU.subtract))
                link(V.tensor_scalar(t_sum[:, :], t_sum[:, :], float(SLOT_T), None, ALU.mult))
                link(V.scalar_tensor_tensor(out=t_sum[:, :], in0=t_e[:, :], scalar=float(REGION), in1=t_sum[:, :],
                                            op0=ALU.mult, op1=ALU.add))
                link(V.tensor_tensor(tab_row[:, :], t_sum[0:1, :], t_ok[0:1, :], ALU.mult))
                link(V.tensor_tensor(t_e[:, :], t_e[:, :], t_ok[:, :], ALU.mult))
                link(V.tensor_copy(t_pack[:, :], t_e[:, :]))
                for k_ in range(1, 3):
                    link(V.scalar_tensor_tensor(out=t_pack[:, 0:TILES - k_], in0=t_e[:, k_:TILES],
                                                scalar=float(1 << EB * k_), in1=t_pack[:, 0:TILES - k_],
                                                op0=ALU.mult, op1=ALU.add))
                V.tensor_copy(tab_e[:, :], t_pack[0:1, :])
                V.tensor_copy(pad_row[:, :], taken[0:1, :]).then_inc(table_done, 1)
                link(V.tensor_tensor(past[:, :, :], t_e[:, :, None].broadcast_to([P, TILES, E]),
                                     exp_no[:, None, :].broadcast_to([P, TILES, E]), ALU.is_equal))
                if ffn == 0:
                    dve.wait_ge(b1_done, 1)
                link(V.tensor_tensor(b1_w[:, :, :, :], past[:, :, None, :].broadcast_to([P, TILES, HC, E]),
                                     b1T[:, :].rearrange("p (e j) -> p j e", e=E)[:, None, :, :]
                                     .broadcast_to([P, TILES, HC, E]), ALU.mult))
                V.tensor_reduce(b1_t[:, :, :], b1_w[:, :, :, :], AX.X, ALU.add).then_inc(b1t_done, 1)
                if ffn == 0:
                    prepare_weights()
                low_g(ffn * TILES, 0)
                low_g(ffn * TILES + 1, 1)
                link(V.tensor_tensor(cum_ex[:, :], cum[:, :], cnt[:, :], ALU.subtract))
                link(V.scalar_tensor_tensor(out=shift[:, :], in0=cum_ex[:, :], scalar=float(SLOT_T), in1=region0[:, :],
                                            op0=ALU.mult, op1=ALU.subtract))
                for h in range(TOPK):
                    V.tensor_tensor(pickw[:, :, :], one[:, h, :, :], shift[:, None, :].broadcast_to([P, NT, E]),
                                    ALU.mult).then_inc(ysl_chain, 1)
                    dve.wait_ge(ysl_chain, ffn * 6 + 3 * h + 1)
                    V.tensor_reduce(ysl[:, h, :], pickw[:, :, :], AX.X, ALU.add).then_inc(ysl_chain, 1)
                    dve.wait_ge(ysl_chain, ffn * 6 + 3 * h + 2)
                    V.tensor_tensor(ysl[:, h, :], ysl[:, h, :], slot[:, h, :], ALU.add).then_inc(ysl_chain, 1)
                V.tensor_copy(taken[:, :], region0[:, :]).then_inc(ysl_last, 1)
                dve.wait_ge(ysl_last, ffn + 1)
                dve.wait_ge(ysl_chain, ffn * 6 + 6)
                assert k[0] == (ffn + 1) * TABLE_LINKS

            def low_g(step, u):
                dve.wait_ge(gh_done, step + 1)
                nc.vector.tensor_tensor(gl[:, u, :], gT[u][:, 0:SLOT_T], gh[:, u, :], ALU.subtract).then_inc(gl_done, 1)

            def split_r(step, u):
                for h in range(2):
                    dve.wait_ge(r_done, 2 * step + h + 1)
                    nc.vector.tensor_copy(rh[:, u, 2 * h:2 * h + 2, :], r[:, u, 2 * h:2 * h + 2, :]).then_inc(rh_done, 1)
                dve.wait_ge(rh_done, 2 * step + 2)
                nc.vector.tensor_tensor(rl[:, u, 2:4, :], r[:, u, 2:4, :], rh[:, u, 2:4, :], ALU.subtract
                                        ).then_inc(rl1_done, 1)

            def result(t, u):
                step = now[0] * TILES + t
                dve.wait_ge(y_full, step + 1)
                wait_some(dve, stored[u], stored_before(t, u))
                nc.vector.tensor_copy(ysb[:, u, :, :], y[u][:, 0:SLOT_T].rearrange("p (s d) -> p s d", s=SH)
                                      ).then_inc(y_done, 1)

            def stored_before(t, u):
                return 16 * (now[0] * ((TILES + 1 - u) // 2)) + (t - u) * 8

            def tile_step(t, u, left):
                if left >= 2:
                    low_g(now[0] * TILES + t + 2, u)
                if left >= 1:
                    split_r(now[0] * TILES + t + 1, 1 - u)
                result(t, u)

            def row_numbers(ffn, m, u):
                wait_some(dve, gathered[u], UNIT_DMAS // 2 * (ffn * B + m - u))
                nc.vector.tensor_scalar(yix[:, u, :, :], ysl[:, :, bass.ds(m * UT, UT)], 0.0, None, ALU.add
                                        ).then_inc(yix_done, 1)

            def add_rows(ffn, m, u, other=None):
                n = ffn * B + m
                if other is not None:
                    dve.wait_ge(res_done, other + 1)
                dve.wait_ge(gathered[u], UNIT_DMAS // 2 * (n - u) + UNIT_DMAS)
                for h in range(TOPK):
                    for t in range(UT):
                        c = m * UT + t
                        xr = xres[:, bass.ds(c, 1), :]
                        last = nc.vector.scalar_tensor_tensor(out=xr, in0=yg[:, u, h, t, :],
                                                              scalar=gate[:, h, bass.ds(c, 1)], in1=xr,
                                                              op0=ALU.mult, op1=ALU.add)
                    if h == 0:
                        last.then_inc(add_chain, 1)
                        if other is not None:
                            batch_stats(other, NT_B).then_inc(beside, 1)
                        dve.wait_ge(add_chain, n + 1)
                last.then_inc(added, 1)
                dve.wait_ge(added, n + 1)

            first_stats()
            for k in range(2):
                first_norm(k)
            dve.wait_ge(s_r, 16 * 3)
            nc.vector.tensor_scalar(b2s[:, :], b2s[:, :], WSCALE, None, ALU.mult).then_inc(c_dve, 1)
            dve.wait_ge(s_const, 7)
            nc.vector.tensor_copy(taken[:, :], region0[:, :]).then_inc(c_dve, 1)
            dve.wait_ge(c_dve, 2)
            now = [0]
            route_beats(route_beat)
            row_signs()
            for ffn in range(2):
                now[0] = ffn
                tile_table(ffn)
                split_r(ffn * TILES, 0)
                tiles(dve, tile_step)
                if ffn == 0:
                    batches(dve, attention_step)

            def add_pair(pair):
                for u in range(2):
                    m = pair * 2 + u
                    more = u == 0 or not isinstance(pair, int)
                    if more:
                        gate_sums(1, m + 1)
                    add_b2(1, m)
                    dve.wait_ge(b2_done, BASE[1] + m + 1)
                    add_rows(1, m, u)
                    if not isinstance(pair, int):
                        row_numbers(1, m + 2, u)

            gate_sums(1, 0)
            row_numbers(1, 0, 0)
            row_numbers(1, 1, 1)
            pairs_ahead(dve, add_pair)

        @block.tensor
        def _(pe):
            def turn_weights():
                pe.wait_ge(s_w, 16 * N_W)
                pe.wait_ge(b2_done, UNITS[0])
                nc.tensor.transpose(gT[1][:, 0:E * HC], b1n[:, :], ident[0:E * HC, 0:E * HC]).then_inc(b1_full, 1)
                pe.wait_ge(b1_done, 1)
                for k in range(4):
                    last = nc.tensor.transpose(z[0][:, k * D:(k + 1) * D], wnat[:, k, :], ident[:, :])
                last.then_inc(wT_full, 1)
                pe.wait_ge(wT_done, 4)

            def slot_free(b, k, middle, route):
                if k == 2:
                    if not (isinstance(b, int) and b < 3):
                        pe.wait_ge(res_done, b - 2)
                elif k == 3:
                    if middle:
                        pe.wait_ge(sub_done, 2 * b)
                elif k == 6:
                    if route:
                        pe.wait_ge(xT_done, BASE[1] + b - 2)
                elif k >= 7:
                    pe.wait_ge(qk_done, 6 * b + k - 6)

            def attention_step(i, odd, fetch, project, middle, finish, route):
                b = i + 1
                if middle:
                    scores(i, par(i, odd))
                if finish:
                    weigh(i - 1, 1 - par(i, odd))
                if project:
                    pe.wait_ge(aln_done, b + 1)
                    if not (isinstance(b, int) and b == 0):
                        pe.wait_ge(vb_done, 3 * b - 1)
                    if not (isinstance(b, int) and b < 3):
                        pe.wait_ge(atT_done, b - 2)
                    for t in range(NT_B):
                        last = nc.tensor.transpose(pj[0][:, t * P:(t + 1) * P], axn[:, t, :], ident[:, :])
                    last.then_inc(aT_full, 1)
                    project_slots(b, (1, 2), middle, route)
                if route:
                    pe.wait_ge(sub_done, 2 * (i + 1) if middle else 2 * B)
                    route_t(1, i - 2, par(i, odd), banks[3])
                if project:
                    project_slots(b, range(3, 7), middle, route)
                if route:
                    if finish:
                        pe.wait_ge(ob_done, i)
                    route_l(1, i - 2, par(i, odd), ob[:, LG_AT:LG_AT + W[1] * E])
                if project:
                    project_slots(b, range(7, 10), middle, route)
                if finish:
                    pe.wait_ge(att_done, i)
                    pe.wait_ge(gm_done, i)
                    if project:
                        pe.wait_ge(vb_done, 3 * b + 1)
                    elif not (isinstance(i, int) and i < 2):
                        pe.wait_ge(atT_done, i - 1)
                    for t in range(NT_B):
                        nc.tensor.transpose(pj[0][:, t * P:(t + 1) * P], att[:, t, :], ident[:, :])
                    nc.tensor.matmul(pj[0][:, S:S + 1], g_out[:, :], ones[0:NH, :], start=True, stop=True
                                     ).then_inc(atT_full, 1)
                if middle:
                    u = par(i, odd)
                    pe.wait_ge(bd_done, 2 * i + 2)
                    if finish:
                        pe.wait_ge(gm_done, i)
                    for g in range(HG):
                        last = nc.tensor.matmul(gb[0:NH, 0:S], q0[:, u, g, :], krow[:, u, g, WIN:WIN + S],
                                                start=(g == 0), stop=(g == HG - 1))
                    last.then_inc(gs_full, 1)
                if route:
                    route_p(1, i - 2, par(i, odd), ob[:, PX_AT:PX_AT + (W[1] + 1) * E])
                if finish:
                    pe.wait_ge(atT_done, i)
                    if project:
                        pe.wait_ge(vb_done, 3 * b + 2)
                    elif not (isinstance(i, int) and i < 2):
                        pe.wait_ge(res_done, i - 1)
                    for t in range(NT_B):
                        last = nc.tensor.matmul(pj[1][:, t * D:(t + 1) * D], atT[:, t * P:(t + 1) * P], woT[:, :],
                                                start=True, stop=True)
                    last.then_inc(wo_full, 1)

            def scores(b, u):
                pe.wait_ge(qk_done, 6 * b + 6)
                pe.wait_ge(vp_done, b + 1)
                if not (isinstance(b, int) and b == 0):
                    pe.wait_ge(sub_done, 2 * b)
                if not (isinstance(b, int) and b < 3):
                    pe.wait_ge(xT_done, BASE[1] + b - 2)
                for g in range(HG):
                    nc.tensor.matmul(sc[:, g, :], identb[:, :], maskb[:, :, :], start=True, stop=False,
                                     skip_group_check=True)
                for q in range(NQ):
                    for r_ in range(HG):
                        for h in range(HP):
                            g = (r_ + h) % HG
                            sh = slice(QB * h, QB * h + QB)
                            last = nc.tensor.matmul(sc[sh, g, 2 * QB * q:2 * QB * (q + 1)],
                                                    qrow[sh, u, g, QB * q:QB * (q + 1)],
                                                    krow[sh, u, g, QB * q:QB * (q + 2)], start=False,
                                                    stop=(q == NQ - 1), skip_group_check=True)
                last.then_inc(sc_full, 1)

            def weigh(b, u):
                pe.wait_ge(p0_done, b + 1)
                pe.wait_ge(mxd_done, b + 1)
                pe.wait_ge(bd_done, 2 * b + 2)
                if not (isinstance(b, int) and b == 0):
                    pe.wait_ge(ob_done, b)
                if not (isinstance(b, int) and b < 2):
                    pe.wait_ge(slot_done, BASE[1] + b - 1)
                for t in range(NT_B):
                    for g in range(HG):
                        at = S0_AT + t * NH + g * HP
                        nc.tensor.matmul(ob[:, at:at + HP], qrow[:, u, g, t * P:(t + 1) * P], k0[:, u, g, :],
                                         start=True, stop=True)
                for t in range(NT_B):
                    last = nc.tensor.transpose(gb[:, 256 + t * NH:256 + (t + 1) * NH], g_prob[:, t * P:(t + 1) * P],
                                               ident[0:NH, 0:NH])
                last.then_inc(p0T_full, 1)
                for j in range(P // QB):
                    nc.tensor.matmul(ob[QB * j:QB * (j + 1), MT_AT:MT_AT + NM], fold[:, :], mxd[:, j:NQ:P // QB, :, :],
                                     start=True, stop=True)
                pe.wait_ge(pt_done, 2 * b + 2)
                for q in range(NQ):
                    for g in range(HG):
                        j, t = q % (P // QB), q // (P // QB)
                        at = (t * HG + g) * HP * (HD + 1)
                        for half_ in range(2):
                            last = nc.tensor.matmul(
                                ob[QB * j:QB * (j + 1), at:at + HP * (HD + 1)], probT[:, g * NQ + q, half_, :],
                                vbd[:, u, q + half_, g, :, :].rearrange("p h e -> p (h e)"),
                                start=(half_ == 0), stop=(half_ == 1))
                last.then_inc(o_full, 1)
                pe.wait_ge(p0T_done, b + 1)
                for t in range(NT_B):
                    last = nc.tensor.matmul(gb[0:NH, 288:288 + D], g_pT[:, t, :], vp[:, u, t, :],
                                            start=(t == 0), stop=(t == NT_B - 1))
                last.then_inc(go_full, 1)

            def project_slots(b, which, middle, route):
                pe.wait_ge(aT_done, b + 1)
                for k in which:
                    slot_free(b, k, middle, route)
                    o = slots[k]
                    if k < 3:
                        for n in range(2):
                            last = nc.tensor.matmul(o[:, n * S:(n + 1) * S], wqr[:, 2 * k - 2 + n, :],
                                                    aT[:, WIN:WIN + S], start=True, stop=True)
                    elif k < 7:
                        last = nc.tensor.matmul(o[:, 0:PADS], wkr[:, k - 3, :], aT[:, :], start=True, stop=True)
                    else:
                        if k == 7:
                            pe.wait_ge(aTr_done, b + 1)
                        for n in range(4 if k < 9 else 1):
                            q = 4 * (k - 7) + n
                            last = nc.tensor.matmul(
                                o[:, n * D:(n + 1) * D],
                                aTr[:, q, :, :].rearrange("p h k -> p (h k)"), wvT[:, :],
                                start=True, stop=True)
                        if k == 9:
                            for t in range(NT_B):
                                nc.tensor.matmul(o[:, (t + 1) * D:(t + 2) * D], aT[:, WIN + t * P:WIN + (t + 1) * P],
                                                 wvT[:, :], start=True, stop=True)
                            last = nc.tensor.matmul(o[:, 3 * D:4 * D], aT[:, WIN:WIN + 1].broadcast_to([P, P]),
                                                    wvT[:, :], start=True, stop=True)
                    last.then_inc(pj_full, 1)

            def route_t(ffn, m, u, bank):
                pe.wait_ge(ln_done, BASE[ffn] + m + 1)
                for t in range(W[ffn]):
                    last = nc.tensor.transpose(bank[:, t * P:(t + 1) * P], xn[:, place_of(ffn, m, u, t), :], ident[:, :])
                last.then_inc(pT_full, 1)

            def route_l(ffn, m, u, logits):
                pe.wait_ge(xT_done, BASE[ffn] + m + 1)
                for t in range(W[ffn]):
                    last = nc.tensor.matmul(logits[:, t * E:(t + 1) * E], xT[:, u, t * P:(t + 1) * P], wr[:, :],
                                            start=True, stop=True)
                last.then_inc(lg_full, 1)

            def route_p(ffn, m, u, px):
                w = W[ffn]
                pe.wait_ge(delta_done, BASE[ffn] + m + 1)
                wait_some(pe, slot_done, BASE[ffn] + m)
                for t in range(w):
                    nc.tensor.matmul(px[:, t * E:(t + 1) * E], before[:, :], both[:, u, t, :], start=True, stop=(t == 0))
                    for s_ in range(t):
                        nc.tensor.matmul(px[:, t * E:(t + 1) * E], ones16[:, :], both[:, u, s_, :], start=False,
                                         stop=(s_ == t - 1))
                for t in range(w):
                    last = nc.tensor.matmul(px[:, w * E:w * E + E], ones16[:, :], both[:, u, t, :],
                                            start=(t == 0), stop=(t == w - 1))
                last.then_inc(px_full, 1)

            def gates_t(ffn, m):
                pe.wait_ge(gsum_done, BASE[ffn] + m + 1)
                for t in range(W[ffn]):
                    last = nc.tensor.transpose(banks[6][0:E, t * P:(t + 1) * P], gsum[:, t, :], ident[:, :])
                last.then_inc(gsT_full, 1)

            def gates_b2(ffn, m):
                pe.wait_ge(gsT_done, BASE[ffn] + m + 1)
                wait_some(pe, b2_done, BASE[ffn] + m)
                for t in range(W[ffn]):
                    last = nc.tensor.matmul(banks[7][:, t * D:(t + 1) * D], gsT[:, t * P:(t + 1) * P], b2s[:, :],
                                            start=True, stop=True)
                last.then_inc(b2_full, 1)

            def route_beat(k, u):
                if there(k - 1):
                    route_l(0, k - 1, 1 - u, banks[3 - u][:, 0:W[0] * E])
                if there(k):
                    route_t(0, k, u, banks[u])
                if there(k - 1):
                    route_p(0, k - 1, 1 - u, banks[5 - u])
                if there(k - 2):
                    gates_t(0, k - 2)
                    gates_b2(0, k - 2)

            def g_transposes(t, u):
                step = now[0] * TILES + t
                pe.wait_ge(loaded[u], 16 * (now[0] * ((TILES + 1 - u) // 2) + 1) + (t - u) * 8)
                wait_some(pe, gl_done, step - 1)
                for h in range(SH):
                    last = nc.tensor.transpose(gT[u][:, h * P:(h + 1) * P], xg[:, u, h, :], ident[:, :])
                last.then_inc(gT_full, 1)

            def up(t, u, e):
                step = now[0] * TILES + t
                pe.wait_ge(gl_done, step + 1)
                for j in range(HC):
                    if j % 2 == 0:
                        wait_some(pe, r_done, 2 * (step - 2) + j // 2 + 1)
                    o = z[2 * u + j // 2][:, (j % 2) * SLOT_T:(j % 2 + 1) * SLOT_T]
                    wh, wl = (w[:, bass.ds(e, 1), j * P:(j + 1) * P] for w in (w1h, w1l))
                    nc.tensor.matmul(o, wh, gh[:, u, :], start=True, stop=False)
                    nc.tensor.matmul(o, wh, gl[:, u, :], start=False, stop=False)
                    last = nc.tensor.matmul(o, wl, gh[:, u, :], start=False, stop=True)
                    if j % 2:
                        last.then_inc(z_full, 1)

            def down(t, u, e):
                step = now[0] * TILES + t
                wait_some(pe, y_done, step - 1)
                for h in range(SH):
                    o = y[u][:, h * D:(h + 1) * D]
                    for j in range(HC):
                        if h == 0 and j == 0:
                            pe.wait_ge(rl0_done, step + 1)
                        if h == 0 and j == 2:
                            pe.wait_ge(rl1_done, step + 1)
                        wh, wl = (w[:, bass.ds(e, 1), j, :] for w in (w2h, w2l))
                        a = slice(h * P, (h + 1) * P)
                        nc.tensor.matmul(o, rh[:, u, j, a], wh, start=(j == 0), stop=False)
                        nc.tensor.matmul(o, rh[:, u, j, a], wl, start=False, stop=False)
                        last = nc.tensor.matmul(o, rl[:, u, j, a], wh, start=False, stop=(j == HC - 1))
                last.then_inc(y_full, 1)

            def experts(t):
                v = pe.value_load(tab_e[0:1, bass.ds(t, 1)], min_val=0, max_val=(1 << 3 * EB) - 1)
                return tuple((v >> EB * k) & ((1 << EB) - 1) for k in range(3))

            e_of = [()]

            def tile_step(t, u, left):
                if u == 0:
                    e_of[0] = experts(t)
                if left >= 2:
                    g_transposes(t + 2, u)
                if left >= 1:
                    up(t + 1, 1 - u, e_of[0][u + 1])
                down(t, u, e_of[0][u])

            now = [0]
            pe.wait_ge(s_const, 7)
            pe.wait_ge(s_r, 16 * 3)
            route_beats(route_beat)
            turn_weights()
            for ffn in range(2):
                now[0] = ffn
                pe.wait_ge(table_done, ffn + 1)
                first = experts(0)[0]
                g_transposes(0, 0)
                g_transposes(1, 1)
                if ffn == 0:
                    pe.wait_ge(s_wl, 2)
                up(0, 0, first)
                tiles(pe, tile_step)
                if ffn == 0:
                    pe.wait_ge(y_done, TILES)
                    batches(pe, attention_step)

            def b2_pair(pair):
                for u in range(2):
                    gates_t(1, pair * 2 + u)
                    gates_b2(1, pair * 2 + u)

            unit_pairs(pe, b2_pair)


_INS = ['L0_attn_x', 'L0_attn_Wq', 'L0_attn_Wk', 'L0_attn_Wv', 'L0_attn_Wo', 'L0_ffn_Wr', 'L0_ffn_br', 'L0_ffn_W1',
        'L0_ffn_b1', 'L0_ffn_W2', 'L0_ffn_b2']
_OUTS = [((16, 256, 128), 'float32')]


def kernel(**inputs):
    import numpy as _np
    import concourse.bacc as _bacc
    from concourse import mybir as _mybir
    from concourse.bass_utils import run_bass_kernel_spmd as _run

    nc = _bacc.Bacc("TRN2", target_bir_lowering=False, num_devices=1)
    arrays, args = {}, []
    for name in _INS:
        a = _np.ascontiguousarray(inputs[name])
        arrays[f"in_{name}_dram"] = a
        args.append(nc.dram_tensor(f"in_{name}_dram", a.shape, _mybir.dt.from_np(a.dtype), kind="ExternalInput").ap())
    for i, (shape, dtype) in enumerate(_OUTS):
        dt = _mybir.dt.from_np(_np.dtype(dtype))
        args.append(nc.dram_tensor(f"out_{i}_dram", shape, dt, kind="ExternalOutput").ap())
    macaron_kernel(nc, *args)
    r = _run(nc, [arrays], core_ids=[0])
    got = tuple(r.results[0][f"out_{i}_dram"] for i in range(len(_OUTS)))
    return got[0]
```

```python
from contextlib import ExitStack

import concourse.bass as bass
from concourse import mybir

ALU = mybir.AluOpType
ACT = mybir.ActivationFunctionType
AX = mybir.AxisListType
F32 = mybir.dt.float32
F16 = mybir.dt.float16
BF16 = mybir.dt.bfloat16
I32 = mybir.dt.int32

P = 128
WSCALE = 64.0
EPS = 1e-5
BIG = 3.0e38
NOT_SEEN = -1.0e30


def macaron_kernel(nc, x, Wq, Wk, Wv, Wo, Wr, br, W1, b1, W2, b2, out):
    B, S, D = x.shape
    E, _, H = W1.shape
    NT = B * S // P
    EB = (E - 1).bit_length()
    HC = H // P
    SLOT_T = 2 * P
    SH = SLOT_T // P
    TOPK = 2
    TILES = B * S * TOPK // SLOT_T + E - 1
    REGION = B * S + SLOT_T
    AHEAD = 4
    assert B * S * TOPK // SLOT_T >= E
    TURN = 4
    TURNS = (TILES - AHEAD - 2) // TURN
    HD, NH, WIN = 8, 16, 16
    HP, HG = 4, 4
    QB = 32
    NQ = S // QB
    NT_B = S // P
    W = (2 * NT_B, NT_B)
    UNITS = (NT // W[0], NT // W[1])
    BASE = (0, UNITS[0])
    RING = 4
    DW = D + 2
    UT = NT_B
    NM = NT_B * NH
    PADS = S + 2 * WIN
    SLOTS = 9
    x_v = x.rearrange("b s d -> (b s) d").rearrange("(n p) d -> p n d", p=P)
    out_v = out.rearrange("b s d -> (b s) d").rearrange("(n p) d -> p n d", p=P)

    with ExitStack() as ctx:
        def sb(name, shape, dt=F32):
            return ctx.enter_context(nc.sbuf_tensor(name, shape, dt))

        def sem(name):
            return ctx.enter_context(nc.semaphore(name))

        xres = sb("xres", [P, NT, D])
        w1f = sb("w1f", [P, E, H])
        w1h, w1l = sb("w1h", [P, E, H], F16), sb("w1l", [P, E, H], F16)
        w2f = sb("w2f", [P, E, HC, D])
        w2h, w2l = sb("w2h", [P, E, HC, D], F16), sb("w2l", [P, E, HC, D], F16)
        b1n = sb("b1n", [E * HC, P])
        b1T = sb("b1T", [P, E * HC])
        wr = sb("wr", [P, E])
        br_bc = sb("br_bc", [P, E])
        b2hl = sb("b2hl", [2, E, D], F16)
        neg_row = sb("neg_row", [2, 1])
        ident = sb("ident", [P, P])
        before = sb("before", [P, P], F16)
        ones16 = sb("ones16", [P, P], F16)
        tie = sb("tie", [P, E])
        region0 = sb("region0", [P, E])
        exp_no = sb("exp_no", [P, E])
        tri_e = sb("tri_e", [P, E, E])
        tile_no = sb("tile_no", [P, TILES])
        no_token = sb("no_token", [P, SH, D + 2 * E])
        xn = sb("xn", [P, RING * W[0], TOPK, DW])
        xT = sb("xT", [P, 2, W[0] * P])
        stats = sb("stats", [P, NT, 6])
        mean, dif, rstd, var, half, newton = (sb(n, [P, NT]) for n in ("mean", "dif", "rstd", "var", "half", "newton"))
        guess = sb("guess", [P, NT], I32)
        lg, lg2, eq = (sb(n, [P, W[0], E]) for n in ("lg", "lg2", "eq"))
        one = sb("one", [P, TOPK, NT, E])
        both = sb("both", [P, 2, W[0], E], F16)
        m1, m2, pick, den = (sb(n, [P, W[0]]) for n in ("m1", "m2", "pick", "den"))
        edelta, e2 = sb("edelta", [P, 2, W[0]]), sb("e2", [P, 2, W[0]])
        tag = sb("tag", [P, TOPK, NT, 2])
        gate = tag[:, :, :, 1]
        place = sb("place", [P, W[0], E])
        taken = sb("taken", [P, E])
        slot = sb("slot", [P, TOPK, NT])
        slot_i = sb("slot_i", [P, 2, TOPK, W[0]], I32)
        cnt, cnt_f, cum = (sb(n, [P, E]) for n in ("cnt", "cnt_f", "cum"))
        cnt_i = sb("cnt_i", [P, E], I32)
        tri_w = sb("tri_w", [P, E, E])
        b1_t = sb("b1_t", [P, TILES, HC])
        t_e, t_sum, t_ok, t_pack, t_off = (sb(n, [P, TILES]) for n in ("t_e", "t_sum", "t_ok", "t_pack", "t_off"))
        tab_e, tab_row = sb("tab_e", [1, TILES], I32), sb("tab_row", [1, TILES], I32)
        pad_row = sb("pad_row", [1, E], I32)
        carrier = sb("carrier", [P, 2])
        xg = sb("xg", [P, 2, SH, DW])
        meta = sb("meta", [P, TILES, SH, 2])
        y_row = sb("y_row", [P, 2, SH], I32)
        held, idle = sb("held", [P, 1]), sb("idle", [P, 1])
        gh, gl = sb("gh", [P, 2, SLOT_T], F16), sb("gl", [P, 2, SLOT_T], F16)
        r = sb("r", [P, 2, HC, SLOT_T])
        rh, rl = sb("rh", [P, 2, HC, SLOT_T], F16), sb("rl", [P, 2, HC, SLOT_T], F16)
        b2f, b2r = (a[0:2, 0, :, :].rearrange("p j (k d) -> p (j k) d", d=D) for a in (r, rh))
        LAST_U = RING * W[0] * TOPK * DW // (TOPK * UT * D)
        y_last = xn[:, :, :, :].rearrange("p n k c -> p (n k c)")[:, 0:LAST_U * TOPK * UT * D].rearrange(
            "p (u k t d) -> p u k t d", u=LAST_U, k=TOPK, t=UT)
        ysb = sb("ysb", [P, 2, SH, D])
        yg = sb("yg", [P, 2, TOPK, UT, D])
        xs = nc.dram_tensor("dispatch_rows", [E * REGION, DW], F32).ap()
        ys = nc.dram_tensor("result_rows", [TOPK * B * S + TILES * SLOT_T, D], F32).ap()
        ys_v = ys[0:TOPK * B * S, :].rearrange("(k n p) d -> p k n d", k=TOPK, p=P)

        psum = ctx.enter_context(nc.psum_tensor("psum", [P, 8, 512], F32))
        banks = [psum[:, i, :] for i in range(8)]
        z = banks[0:4]
        y = banks[4:6]
        gT = banks[6:8]

        O_N, S0_AT, MT_AT, LG_AT, PX_AT = NT_B * HG * HP * (HD + 1), 288, 320, 352, 384

        wnat = sb("wnat", [P, 4, D])
        wqr, wkr = sb("wqr", [P, HG, P]), sb("wkr", [P, HG, P])
        wvT, woT = sb("wvT", [P, D]), sb("woT", [P, D])
        identb = sb("identb", [P, P], BF16)
        maskb = sb("maskb", [P, NQ, 2 * QB], BF16)
        strip = sb("strip", [P, HP])
        strip16 = sb("strip16", [P, HG, NH])
        headrow = sb("headrow", [NH, D])
        fold = sb("fold", [P, QB])
        row_no = sb("row_no", [P, 1], I32)
        row_bit = sb("row_bit", [P, 2], I32)
        neg_q, neg_k = sb("neg_q", [P, 1]), sb("neg_k", [P, 1])
        ones = sb("ones", [P, 1])
        axn = sb("axn", [P, 2, D])
        aT = sb("aT", [P, PADS])
        aTr = sb("aTr", [P, NQ + 1, HP, QB])
        hi_q, hi_k = sb("hi_q", [P, 2, 2 * S], F16), sb("hi_k", [P, HG, PADS], F16)
        qrow = sb("qrow", [P, 2, HG, S], F16)
        krow = sb("krow", [P, 2, HG, PADS], F16)
        k0 = sb("k0", [P, 2, HG, HP], F16)
        q0 = sb("q0", [P, 2, HG, NH], F16)
        vbd = sb("vbd", [P, 2, NQ + 1, HG, HP, HD + 1])
        vp = sb("vp", [P, 2, 3, D])
        mx = sb("mx", [P, HG, NQ])
        mxd = sb("mxd", [P, NQ, HG, HP])
        prob = sb("prob", [P, HG * NQ, 2 * QB])
        probT = sb("probT", [P, HG * NQ, 2, QB])
        past, past_w = (prob[:, k * 16:k * 16 + 16, :].rearrange("p n c -> p (n c)")[:, 0:TILES * E]
                        .rearrange("p (t e) -> p t e", e=E) for k in range(2))
        b1_w = probT[:, :, :, :].rearrange("p n a q -> p (n a q)")[:, 0:TILES * HC * E].rearrange(
            "p (t j e) -> p t j e", t=TILES, e=E)
        o_sb = sb("o_sb", [P, MT_AT + NM])
        ahead = sb("ahead", [P, NM])
        dd = sb("dd", [P, 2, NM])
        ee = sb("ee", [P, 2, NM])
        al, mden, mrec = sb("al", [P, NM]), sb("mden", [P, NM]), sb("mrec", [P, NM])
        ar, cr = sb("ar", [P, NM]), sb("cr", [P, NM])
        t2 = sb("t2", [P, 2, D])
        att = sb("att", [P, 2, D])
        atT = sb("atT", [P, S])
        g_neg, g_sum, g_rec = sb("g_neg", [NH, 1]), sb("g_sum", [NH, 1]), sb("g_rec", [NH, 1])
        g_exp, g_prob = sb("g_exp", [NH, S]), sb("g_prob", [NH, S])
        g_pT = sb("g_pT", [P, 2, NH])
        g_out = sb("g_out", [NH, D])

        sc = psum[:, 0:4, :]
        pj = banks[4:6]
        slots = (None, *banks[4:6], *banks[0:4], *banks[4:6], banks[0])
        ob = banks[6]
        gb = banks[7]

        x_loaded = [sem(f"x_loaded{k}") for k in range(4)]
        weights_loaded, router_loaded = sem("weights_loaded"), sem("router_loaded")
        const_done = sem("const_done")
        filled = sem("filled")
        w1h_done, w2h_done, low_weights_done = sem("w1h_done"), sem("w2h_done"), sem("low_weights_done")
        ln_chain, ln_done = sem("ln_chain"), sem("ln_done")
        pT_full, xT_done = sem("pT_full"), sem("xT_done")
        lg_full, route_chain, delta_done, e2_done = (
            sem(n) for n in ("lg_full", "route_chain", "delta_done", "e2_done"))
        px_full, place_chain, slot_done = sem("px_full"), sem("place_chain"), sem("slot_done")
        scattered = [sem(f"scattered{u}") for u in range(2)]
        b2_chain = sem("b2_chain")
        table_chain, table_done, padded = sem("table_chain"), sem("table_done"), sem("padded")
        loaded, stored = [sem(f"loaded{u}") for u in range(2)], [sem(f"stored{u}") for u in range(2)]
        gT_full, gh_done, gl_done = sem("gT_full"), sem("gh_done"), sem("gl_done")
        z_full, r_done, rh_done, rl0_done, rl1_done = (
            sem(n) for n in ("z_full", "r_done", "rh_done", "rl0_done", "rl1_done"))
        y_full, y_done = sem("y_full"), sem("y_done")
        fetched, add_chain, added = [sem(f"fetched{u}") for u in range(2)], sem("add_chain"), sem("added")
        tagged, centred = sem("tagged"), sem("centred")
        fetched_last = [sem(f"fetched_last{u}") for u in range(LAST_U)]
        out_stored = sem("out_stored")
        carried = [sem("carried_scatter"), sem("carried_result")]
        masks_chain, taken_done, wT_full, wT_done, masks_done = (
            sem(n) for n in ("masks_chain", "taken_done", "wT_full", "wT_done", "masks_done"))
        aln_done, aT_full, aT_done = (sem(n) for n in ("aln_done", "aT_full", "aT_done"))
        pj_full, hi_done, qk_done, vb_done, vp_done, bd_done = (
            sem(n) for n in ("pj_full", "hi_done", "qk_done", "vb_done", "vp_done", "bd_done"))
        sc_full, mx_done, mxd_done, sub_done, exp_done, pt_done = (
            sem(n) for n in ("sc_full", "mx_done", "mxd_done", "sub_done", "exp_done", "pt_done"))
        gs_full, gneg_done, gexp_done, g_chain, p0_done, p0T_full, p0T_done, go_full, gm_done = (
            sem(n) for n in ("gs_full", "gneg_done", "gexp_done", "g_chain", "p0_done", "p0T_full", "p0T_done",
                             "go_full", "gm_done"))
        o_full, mg_chain, dd_done, ee_done, mden_done, mrec_done, att_done = (
            sem(n) for n in ("o_full", "mg_chain", "dd_done", "ee_done", "mden_done", "mrec_done", "att_done"))
        atT_full, atT_done, wo_full, res_done = (sem(n) for n in ("atT_full", "atT_done", "wo_full", "res_done"))
        aTr_done = sem("aTr_done")

        signs_chain, lack_done, ob_done, beside_done = (
            sem(n) for n in ("signs_chain", "lack_done", "ob_done", "beside_done"))
        NEWTON = 3
        MG_LINKS = 5
        LN_LINKS = 1 + 7 + 3 + 3 * NEWTON
        ROUTE_LINKS = 12
        PLACE_LINKS = 9
        TABLE_LINKS = 24 + TURN - 2
        N_WEIGHT_LOADS = 7
        N_CONSTS = 10
        b1t_done = sem("b1t_done")
        taken_reset = sem("taken_reset")
        b1_full, b1_done = sem("b1_full"), sem("b1_done")

        def moments(stats, mean, dif, var, link, settle):
            link(nc.vector.tensor_tensor(mean[:, :], stats[:, :, 1], stats[:, :, 4], ALU.add))
            link(nc.vector.tensor_tensor(dif[:, :], stats[:, :, 1], stats[:, :, 4], ALU.subtract))
            link(nc.vector.tensor_tensor(var[:, :], stats[:, :, 2], stats[:, :, 5], ALU.add))
            settle()
            link(nc.vector.tensor_scalar(mean[:, :], mean[:, :], 0.5, None, ALU.mult))
            link(nc.vector.tensor_tensor(dif[:, :], dif[:, :], dif[:, :], ALU.mult))
            link(nc.vector.tensor_scalar(var[:, :], var[:, :], 1.0 / D, EPS, ALU.mult, ALU.add))
            settle()
            link(nc.vector.scalar_tensor_tensor(out=var[:, :], in0=dif[:, :], scalar=0.25, in1=var[:, :],
                                                op0=ALU.mult, op1=ALU.add))
            settle()

        def rsqrt(out, var, half, guess, newton, link, settle):
            link(nc.vector.tensor_scalar(half[:, :], var[:, :], -0.5, None, ALU.mult))
            link(nc.vector.tensor_scalar(guess[:, :], var[:, :].bitcast(I32), 1, None, ALU.logical_shift_right))
            settle()
            link(nc.vector.tensor_scalar(out[:, :].bitcast(I32), guess[:, :], -1, 0x5F3759DF, ALU.mult, ALU.add))
            settle()
            for _ in range(NEWTON):
                link(nc.vector.tensor_tensor(newton[:, :], out[:, :], out[:, :], ALU.mult))
                settle()
                link(nc.vector.tensor_tensor(newton[:, :], newton[:, :], half[:, :], ALU.mult))
                settle()
                link(nc.vector.scalar_tensor_tensor(out=out[:, :], in0=newton[:, :], scalar=1.5, in1=out[:, :],
                                                    op0=ALU.add, op1=ALU.mult))
                settle()

        block = ctx.enter_context(nc.Block())

        def batches(eng, step):
            def some(i):
                step(i, 1 - i % 2, *(0 <= i + n < B for n in (2, 1, 0, -1, -2)))

            for i in range(-2, 3):
                some(i)
            with eng.Fori(0, (B - 5) // 2) as pair:
                step(3 + pair * 2, 0, True, True, True, True, True)
                step(4 + pair * 2, 1, True, True, True, True, True)
            for i in range(3 + (B - 5) // 2 * 2, B + 2):
                some(i)

        def par(i, odd):
            return i % 2 if isinstance(i, int) else 1 - odd

        def route_beats(beat):
            for k in range(UNITS[0] + 2):
                beat(k, k % 2)

        def there(k):
            return 0 <= k < UNITS[0]

        def place_of(ffn, m, u, t):
            return m % RING * W[0] + t if ffn == 0 else u * W[1] + t

        def tiles(eng, step):
            for t in range(2):
                step(t, t, AHEAD, t)
            with eng.Fori(0, TURNS) as turn:
                for lead in range(TURN):
                    step(turn * TURN + 2 + lead, lead % 2, AHEAD, lead)
            for t in range(2 + TURN * TURNS, TILES):
                step(t, t % 2, min(AHEAD, TILES - 1 - t), (t - 2) % TURN)

        def scattered_by(ffn, m, u):
            rows_before = sum(16 * TOPK * W[f] * UNITS[f] // 2 for f in range(ffn))
            return rows_before + 8 * TOPK * W[ffn] * (m - u)

        def wait_some(eng, s, value):
            if not (isinstance(value, int) and value <= 0):
                eng.wait_ge(s, value)

        def pad(eng, its_type, experts):
            starts = nc.values_load_multi_w_load_instructions(
                pad_row[0:1, experts[0]:experts[-1] + 1], engines=(its_type,), min_val=0, max_val=E * REGION - SLOT_T)[1]
            for e in experts:
                row = starts[e - experts[0]]
                eng.dma_start(xs[bass.ds(row, SLOT_T), :].rearrange("(s p) d -> p s d", p=P),
                              no_token[:, :, 2 * e:2 * e + DW]).then_inc(padded, 16)

        @block.sync
        def _(sp):
            for k in range(4):
                n = NT // 4
                sp.dma_start(xres[:, k * n:(k + 1) * n, :], x_v[:, k * n:(k + 1) * n, :]).then_inc(x_loaded[k], 16)
            sp.dma_start(wr[:, :], Wr).then_inc(router_loaded, 16)
            sp.dma_start(br_bc[:, :], br[None, :].broadcast_to([P, E])).then_inc(router_loaded, 16)
            sp.dma_start(b2f[:, :, :], b2[None, :, :].broadcast_to([2, E, D])).then_inc(router_loaded, 16)
            sp.dma_start(w1f[:, :, :], W1.rearrange("e d h -> d e h")).then_inc(weights_loaded, 16)
            sp.dma_start(w2f[:, :, :, :], W2.rearrange("e (j p) d -> p e j d", p=P)).then_inc(weights_loaded, 16)
            sp.dma_start(b1n[:, :], b1.rearrange("e (j p) -> (e j) p", p=P)).then_inc(weights_loaded, 16)
            for k, w in enumerate((Wq, Wk, Wv, Wo)):
                sp.dma_start(wnat[:, k, :], w).then_inc(weights_loaded, 16)

            def rows(table, n, top):
                return nc.values_load_multi_w_load_instructions(table, engines=(mybir.EngineType.SP,), min_val=0,
                                                                max_val=top)[1]

            def load(row, u):
                sp.dma_start(xg[:, u, :, :], xs[bass.ds(row, SLOT_T), :].rearrange("(s p) d -> p s d", p=P)
                             ).then_inc(loaded[u], 16)

            def fetch(m, u):
                wait_some(sp, added, m - 1)
                for k in range(TOPK):
                    sp.dma_start(yg[:, u, k, :, :], ys_v[:, k, bass.ds(m * UT, UT), :]).then_inc(fetched[u], 16)

            def fetch_last(m):
                wait_some(sp, added, B + m - LAST_U + 1 if m >= LAST_U else 0)
                for k in range(TOPK):
                    sp.dma_start(y_last[:, m % LAST_U, k, :, :], ys_v[:, k, m * UT:(m + 1) * UT, :]
                                 ).then_inc(fetched_last[m % LAST_U], 16)

            def attention_step(i, odd, fetch_next, project, middle, finish, route):
                if fetch_next:
                    fetch(i + 2, par(i, odd))

            for ffn in range(2):
                sp.wait_ge(table_done, ffn + 1)
                pad(sp, mybir.EngineType.SP, range(E // 2))
                first = rows(tab_row[0:1, 0:AHEAD], AHEAD, E * REGION - SLOT_T)
                for u in range(2):
                    sp.wait_ge(scattered[u], scattered_by(ffn, UNITS[ffn] + u, u))
                sp.wait_ge(padded, 16 * E * (ffn + 1))
                for t in range(2):
                    load(first[t], t)
                for t in range(2):
                    sp.wait_ge(gh_done, ffn * TILES + t + 1)
                    load(first[2 + t], t)

                def step(t, u, left, lead):
                    if left >= AHEAD:
                        row, = rows(tab_row[0:1, bass.ds(t + AHEAD, 1)], 1, E * REGION - SLOT_T)
                        sp.wait_ge(gh_done, ffn * TILES + t + 3)
                        load(row, u)

                tiles(sp, step)
                for u in range(2):
                    sp.wait_ge(stored[u], 32 * (ffn + 1) * ((TILES + 1 - u) // 2))
                if ffn == 0:
                    batches(sp, attention_step)

            def store_out(k):
                n = NT // 4
                sp.wait_ge(added, B + B // 4 * (k + 1))
                sp.dma_start(out_v[:, k * n:(k + 1) * n, :], xres[:, k * n:(k + 1) * n, :]).then_inc(out_stored, 16)

            for m in range(B):
                fetch_last(m)
                if m >= B // 4 and m % (B // 4) == 1:
                    store_out(m // (B // 4) - 1)
            store_out(3)
            sp.wait_ge(out_stored, 16 * 4)

        @block.gpsimd
        def _(pool):
            nc.gpsimd.memset(ident[:, :], 0.0).then_inc(filled, 1)
            nc.gpsimd.iota(tie[:, :], [[-1, E]], base=E, channel_multiplier=0,
                           allow_small_or_imprecise_dtypes=True).then_inc(const_done, 1)
            pool.wait_ge(filled, 1)
            nc.gpsimd.affine_select(out=ident[:, :], in_=ident[:, :], compare_op=ALU.not_equal, fill=1.0, base=0,
                                    pattern=[[-1, P]], channel_multiplier=1).then_inc(const_done, 1)
            for a, v in ((ones16, 1.0), (before, 1.0), (tri_e, 1.0), (no_token, 0.0)):
                nc.gpsimd.memset(a[:], v).then_inc(filled, 1)
            pool.wait_ge(filled, 5)
            nc.gpsimd.affine_select(out=before[:, :], in_=before[:, :], compare_op=ALU.is_ge, fill=0.0, base=-1,
                                    pattern=[[1, P]], channel_multiplier=-1).then_inc(const_done, 1)
            nc.gpsimd.affine_select(out=tri_e[:, :, :], in_=tri_e[:, :, :], compare_op=ALU.is_ge, fill=0.0, base=0,
                                    pattern=[[1, E], [-1, E]], channel_multiplier=0).then_inc(const_done, 1)
            nc.gpsimd.iota(no_token[:, :, D::2], [[P, SH], [SLOT_T, E]], base=TOPK * B * S, channel_multiplier=1,
                           allow_small_or_imprecise_dtypes=True).then_inc(const_done, 1)
            nc.gpsimd.iota(tag[:, :, :, 0], [[B * S, TOPK], [P, NT]], base=0, channel_multiplier=1,
                           allow_small_or_imprecise_dtypes=True).then_inc(const_done, 1)
            nc.gpsimd.iota(neg_row[:, :], [[0, 1]], base=0, channel_multiplier=-1,
                           allow_small_or_imprecise_dtypes=True).then_inc(const_done, 1)
            nc.gpsimd.iota(region0[:, :], [[REGION, E]], base=0, channel_multiplier=0,
                           allow_small_or_imprecise_dtypes=True).then_inc(const_done, 1)
            nc.gpsimd.iota(exp_no[:, :], [[1, E]], base=0, channel_multiplier=0,
                           allow_small_or_imprecise_dtypes=True).then_inc(const_done, 1)
            nc.gpsimd.iota(tile_no[:, :], [[1, TILES]], base=0, channel_multiplier=0,
                           allow_small_or_imprecise_dtypes=True).then_inc(const_done, 1)
            n = [0]

            def settle(ins):
                ins.then_inc(masks_chain, 1)
                n[0] += 1
                pool.wait_ge(masks_chain, n[0])

            for c in range(2):
                nc.gpsimd.memset(carrier[:, c:c + 1], 0.0).then_inc(carried[c], 1)
            nc.gpsimd.iota(row_no[:, :], [[0, 1]], base=0, channel_multiplier=1).then_inc(masks_chain, 1)
            nc.gpsimd.memset(aT[:, :], 0.0).then_inc(masks_chain, 1)
            nc.gpsimd.memset(vbd[:, :, :, :, :, :], 0.0).then_inc(masks_chain, 1)
            nc.gpsimd.memset(strip[:, :], 0.0).then_inc(masks_chain, 1)
            nc.gpsimd.memset(strip16[:, :, :], 0.0).then_inc(masks_chain, 1)
            nc.gpsimd.memset(headrow[:, :], 1.0).then_inc(masks_chain, 1)
            nc.gpsimd.memset(ones[:, :], 1.0).then_inc(masks_chain, 1)
            nc.gpsimd.memset(maskb[:, :, :], 0.0).then_inc(masks_chain, 1)
            n[0] = 8
            pool.wait_ge(masks_chain, 8)
            s16 = strip16[:, :, :].rearrange("p g h -> p (g h)")
            for j in range(HP):
                sj = slice(QB * j, QB * (j + 1))
                settle(nc.gpsimd.memset(strip[sj, j:j + 1], 1.0))
                settle(nc.gpsimd.memset(s16[sj, j:j + 3 * (NH + HP) + 1:NH + HP], 1.0))
                for base, step, mult in ((0, 1, -1), (2 * WIN, -1, 1)):
                    settle(nc.gpsimd.affine_select(out=maskb[sj, :, :], in_=maskb[sj, :, :], compare_op=ALU.is_ge,
                                                   fill=NOT_SEEN, base=base, pattern=[[0, NQ], [step, 2 * QB]],
                                                   channel_multiplier=mult))
            for base, step in ((-WIN - 1, 1), (S - 1 + WIN, -1)):
                settle(nc.gpsimd.affine_select(out=maskb[:, :, :], in_=maskb[:, :, :], compare_op=ALU.is_ge,
                                               fill=NOT_SEEN, base=base, pattern=[[step * QB, NQ], [step, 2 * QB]],
                                               channel_multiplier=0))
            for base, step, mult in ((0, 1, -HD), (HD - 1, -1, HD)):
                settle(nc.gpsimd.affine_select(out=headrow[:, :], in_=headrow[:, :], compare_op=ALU.is_ge, fill=0.0,
                                               base=base, pattern=[[step, D]], channel_multiplier=mult))
            pool.wait_ge(const_done, N_CONSTS)
            settle(nc.gpsimd.tensor_copy(identb[:, :], ident[:, :]))
            for j in range(HP):
                sj = slice(QB * j, QB * (j + 1))
                for u in range(2):
                    settle(nc.gpsimd.memset(vbd[sj, u, :, :, j, HD], 1.0))
                settle(nc.gpsimd.tensor_copy(fold[sj, :], ident[sj, sj]))
            nc.gpsimd.memset(row_bit[:, :], 0).then_inc(masks_done, 1)

            def attention_step(i, odd, fetch, project, middle, finish, route):
                if project or route:
                    norms(i, par(i, odd), project, route)
                if finish:
                    pool.wait_ge(ob_done, i)
                    nc.gpsimd.tensor_tensor(ahead[:, :], o_sb[:, S0_AT:S0_AT + NM], o_sb[:, MT_AT:MT_AT + NM],
                                            ALU.subtract).then_inc(dd_done, 1)
                    merge(i - 1, 1 - par(i, odd))
                if project:
                    pool.wait_ge(aT_done, i + 2)
                    if middle:
                        pool.wait_ge(pj_full, SLOTS * (i + 1))
                    nc.gpsimd.tensor_tensor(
                        aTr[:, :, :, :],
                        aT[:, :].rearrange("p (q k) -> p q k", k=QB)[:, :, None, :].broadcast_to([P, NQ + 1, HP, QB]),
                        ones[:, :, None, None].broadcast_to([P, NQ + 1, HP, QB]), ALU.mult).then_inc(aTr_done, 1)
                if middle:
                    pool.wait_ge(mx_done, i + 1)
                    if finish:
                        pool.wait_ge(o_full, i)
                    nc.gpsimd.tensor_tensor(
                        mxd[:, :, :, :],
                        mx[:, :, :].rearrange("p g q -> p q g")[:, :, :, None].broadcast_to([P, NQ, HG, HP]),
                        strip[:, None, None, :].broadcast_to([P, NQ, HG, HP]), ALU.mult).then_inc(mxd_done, 1)
                if project:
                    u = 1 - par(i, odd)
                    pool.wait_ge(qk_done, 6 * (i + 1) + 6)
                    nc.gpsimd.tensor_tensor(k0[:, u, :, :], krow[:, u, :, WIN:WIN + 1].broadcast_to([P, HG, HP]),
                                            strip[:, None, :].broadcast_to([P, HG, HP]), ALU.mult).then_inc(bd_done, 1)
                    nc.gpsimd.tensor_tensor(q0[:, u, :, :], qrow[:, u, :, 0:1].broadcast_to([P, HG, NH]),
                                            strip16[:, :, :], ALU.mult).then_inc(bd_done, 1)
                if route:
                    scatter(1, i - 2, par(i, odd))

            def merge(b, u):
                k = [b * MG_LINKS]

                def link(ins):
                    ins.then_inc(mg_chain, 1)
                    k[0] = k[0] + 1

                def settle():
                    pool.wait_ge(mg_chain, k[0])

                o = o_sb[:, 0:O_N].rearrange("p (n e) -> p n e", e=HD + 1)
                pool.wait_ge(ee_done, b + 1)
                link(nc.gpsimd.tensor_tensor(al[:, :], o[:, :, HD], ee[:, 0, :], ALU.mult))
                settle()
                nc.gpsimd.tensor_tensor(mden[:, :], al[:, :], ee[:, 1, :], ALU.add).then_inc(mden_done, 1)
                pool.wait_ge(mrec_done, b + 1)
                link(nc.gpsimd.tensor_tensor(ar[:, :], ee[:, 0, :], mrec[:, :], ALU.mult))
                link(nc.gpsimd.tensor_tensor(cr[:, :], ee[:, 1, :], mrec[:, :], ALU.mult))
                settle()
                if not (isinstance(b, int) and b == 0):
                    pool.wait_ge(atT_full, b)
                a = att[:, :, :].rearrange("p t (h d) -> p (t h) d", d=HD)
                link(nc.gpsimd.tensor_tensor(a, o[:, :, 0:HD], ar[:, :, None].broadcast_to([P, NM, HD]), ALU.mult))
                link(nc.gpsimd.tensor_tensor(
                    t2[:, :, :].rearrange("p t (h d) -> p t h d", d=HD),
                    vp[:, u, 2, :].rearrange("p (h d) -> p h d", d=HD)[:, None, :, :].broadcast_to([P, NT_B, NH, HD]),
                    cr[:, :].rearrange("p (t h) -> p t h", t=NT_B)[:, :, :, None].broadcast_to([P, NT_B, NH, HD]),
                    ALU.mult))
                settle()
                nc.gpsimd.tensor_tensor(att[:, :, :], att[:, :, :], t2[:, :, :], ALU.add).then_inc(att_done, 1)

            def norms(i, u, project, route):
                b, m = i + 1, i - 2
                if project:
                    if not (isinstance(b, int) and b == 0):
                        pool.wait_ge(aT_full, b)
                if route:
                    pool.wait_ge(scattered[u], scattered_by(1, m, u))
                pool.wait_ge(ln_chain, (i + 3) * LN_LINKS)
                nc.gpsimd.tensor_tensor(held[:, :], ones[:, :], ones[:, :], ALU.mult)
                a = place_of(1, m, u, 0)
                parts = [(axn[:, :, :], b, 0, aln_done)] * project
                parts += [(xn[:, a:a + NT_B, 0, 0:D], m, NT_B, ln_done)] * route

                def wide(v, at):
                    return v[:, at:at + NT_B, None].broadcast_to([P, NT_B, D])

                for out, n, at, _ in parts:
                    last = nc.gpsimd.tensor_tensor(out, xres[:, bass.ds(n * NT_B, NT_B), :], wide(mean, at),
                                                   ALU.subtract)
                last.then_inc(centred, 1)
                pool.wait_ge(centred, i + 2)
                for out, _, at, done in parts:
                    nc.gpsimd.tensor_tensor(out, out, wide(rstd, at), ALU.mult).then_inc(done, 1)

            def wait_ahead_of_dma(s, value, c, nth):
                pool.wait_ge(carried[c], nth + 1)
                pool.wait_ge(s, value)
                nc.gpsimd.tensor_tensor(carrier[:, c:c + 1], ones[:, :], ones[:, :], ALU.mult).then_inc(carried[c], 1)

            def scatter(ffn, m, u):
                n = BASE[ffn] + m
                wait_ahead_of_dma(tagged, n + 1, 0, n)
                for t in range(W[ffn]):
                    for k in range(TOPK):
                        pool.indirect_dma_start(
                            xs, bass.IndirectOffsetOnAxis(ap=slot_i[:, u, k, t:t + 1], axis=0),
                            xn[:, place_of(ffn, m, u, t), k, :], None).then_inc(scattered[u], 16)

            def scatter_beat(k, u):
                if there(k - 2):
                    scatter(0, k - 2, u)

            def scatter_results(t, u):
                step = now[0] * TILES + t
                wait_ahead_of_dma(y_done, step + 1, 1, step)
                for h in range(SH):
                    pool.indirect_dma_start(ys, bass.IndirectOffsetOnAxis(ap=y_row[:, u, h:h + 1], axis=0),
                                            ysb[:, u, h, :], None).then_inc(stored[u], 16)

            def tile_step(t, u, left, lead):
                scatter_results(t, u)

            now = [0]
            route_beats(scatter_beat)
            for ffn in range(2):
                now[0] = ffn
                tiles(pool, tile_step)
                if ffn == 0:
                    batches(pool, attention_step)

        @block.scalar
        def _(act):
            def prepare_weights():
                act.wait_ge(weights_loaded, 16 * N_WEIGHT_LOADS)
                nc.scalar.activation(w1h[:, :, :], w1f[:, :, :], ACT.Copy, scale=WSCALE).then_inc(w1h_done, 1)
                nc.scalar.activation(w2h[:, :, :, :], w2f[:, :, :, :], ACT.Copy, scale=WSCALE).then_inc(w2h_done, 1)

            def turn_weights():
                act.wait_ge(b1_full, 1)
                nc.scalar.copy(b1T[:, :], gT[1][:, 0:E * HC]).then_inc(b1_done, 1)
                act.wait_ge(wT_full, 1)
                for k, w in enumerate((wqr, wkr)):
                    nc.scalar.activation(
                        w[:, :, :].rearrange("p g (h r d) -> p (g h) r d", h=HP, d=HD),
                        z[0][:, k * D:(k + 1) * D].rearrange("p (h d) -> p h d", d=HD)[:, :, None, :]
                        .broadcast_to([P, NH, 4, HD]),
                        ACT.Copy, scale=HD ** -0.5 if k == 0 else 1.0).then_inc(wT_done, 1)
                nc.scalar.copy(wvT[:, :], z[0][:, 2 * D:3 * D]).then_inc(wT_done, 1)
                nc.scalar.copy(woT[:, :], z[0][:, 3 * D:4 * D]).then_inc(wT_done, 1)

            def attention_step(i, odd, fetch, project, middle, finish, route):
                b = i + 1
                if finish:
                    act.wait_ge(p0T_full, i)
                    nc.scalar.copy(g_pT[:, :, :], gb[:, 256:256 + 2 * NH].rearrange("p (t h) -> p t h", t=2)
                                   ).then_inc(p0T_done, 1)
                    act.wait_ge(o_full, i)
                    nc.scalar.copy(o_sb[:, :], ob[:, 0:MT_AT + NM]).then_inc(ob_done, 1)
                if project:
                    act.wait_ge(aT_full, b + 1)
                    nc.scalar.copy(aT[:, WIN:WIN + S], pj[0][:, 0:S]).then_inc(aT_done, 1)
                if finish:
                    act.wait_ge(dd_done, i)
                    nc.scalar.activation(dd[:, 0, :], ahead[:, :], ACT.Relu)
                    nc.scalar.activation(dd[:, 1, :], ahead[:, :], ACT.Relu, scale=-1.0).then_inc(lack_done, 1)
                    act.wait_ge(lack_done, i)
                    nc.scalar.activation(ee[:, :, :], dd[:, :, :], ACT.Exp, scale=-1.0).then_inc(ee_done, 1)
                if middle:
                    for h in range(2):
                        act.wait_ge(sub_done, 2 * i + h + 1)
                        half = prob[:, 16 * h:16 * h + 16, :]
                        nc.scalar.activation(half, half, ACT.Exp).then_inc(exp_done, 1)
                if project:
                    for k in (1, 2):
                        act.wait_ge(pj_full, SLOTS * b + k)
                        nc.scalar.copy(hi_q[:, k - 1, :], slots[k]).then_inc(hi_done, 1)
                if route:
                    route_x(1, i - 2, par(i, odd), banks[3])
                    twin(1, i - 2, par(i, odd))
                if project:
                    for k in range(3, 7):
                        act.wait_ge(pj_full, SLOTS * b + k)
                        nc.scalar.copy(hi_k[:, k - 3, :], slots[k][:, 0:PADS]).then_inc(hi_done, 1)
                    values(b, 1 - par(i, odd), finish)
                if middle:
                    act.wait_ge(gneg_done, i + 1)
                    nc.scalar.activation(g_exp[:, :], gb[0:NH, 0:S], ACT.Exp, bias=g_neg[:, 0:1], scale=1.0,
                                         accum_out=g_sum[:, 0:1]).then_inc(gexp_done, 1)
                if route:
                    route_e(1, i - 2, par(i, odd))
                    tag_rows(1, i - 2, par(i, odd))
                if middle:
                    act.wait_ge(g_chain, i + 1)
                    nc.scalar.activation(g_prob[:, :], g_exp[:, :], ACT.Identity, scale=g_rec[:, 0:1]
                                         ).then_inc(p0_done, 1)
                if finish and not project:
                    turned_output(i)

            def values(b, u, finish):
                for k in range(7, 10):
                    act.wait_ge(pj_full, SLOTS * b + k)
                    first, m = 4 * (k - 7), (4 if k < 9 else 1)
                    for j in range(HP):
                        sj = slice(QB * j, QB * (j + 1))
                        last = nc.scalar.copy(
                            vbd[sj, u, first:first + m, :, j, 0:HD].rearrange("p q g d -> p (q g) d"),
                            slots[k][sj, 0:m * D].rearrange("p (n h d) -> p n h d", h=HP, d=HD)[:, :, j, :])
                    last.then_inc(vb_done, 1)
                if finish:
                    act.wait_ge(att_done, b - 1)
                nc.scalar.copy(vp[:, u, :, :], slots[9][:, D:4 * D].rearrange("p (t d) -> p t d", t=3)
                               ).then_inc(vp_done, 1)
                if finish:
                    turned_output(b - 1)

            def turned_output(i):
                act.wait_ge(atT_full, i)
                nc.scalar.copy(atT[:, 1:S], pj[0][:, 1:S])
                nc.scalar.copy(atT[:, 0:1], pj[0][:, S:S + 1]).then_inc(atT_done, 1)

            def route_x(ffn, m, u, bank):
                act.wait_ge(pT_full, BASE[ffn] + m + 1)
                n = W[ffn] * P
                nc.scalar.copy(xT[:, u, 0:n], bank[:, 0:n]).then_inc(xT_done, 1)

            def route_e(ffn, m, u):
                n = W[ffn]
                act.wait_ge(delta_done, BASE[ffn] + m + 1)
                nc.scalar.activation(e2[:, u, 0:n], edelta[:, u, 0:n], ACT.Exp).then_inc(e2_done, 1)

            def twin(ffn, m, u):
                act.wait_ge(ln_done, BASE[ffn] + m + 1)
                a = place_of(ffn, m, u, 0)
                nc.scalar.copy(xn[:, a:a + W[ffn], 1, 0:D], xn[:, a:a + W[ffn], 0, 0:D])

            def tag_rows(ffn, m, u):
                n = BASE[ffn] + m
                act.wait_ge(place_chain, (n + 1) * PLACE_LINKS)
                a = place_of(ffn, m, u, 0)
                nc.scalar.copy(xn[:, a:a + W[ffn], :, D:DW],
                               tag[:, :, bass.ds(m * W[ffn], W[ffn]), :].rearrange("p k t c -> p t k c")
                               ).then_inc(tagged, 1)

            def route_beat(k, u):
                if there(k - 2):
                    tag_rows(0, k - 2, u)
                if there(k):
                    route_x(0, k, u, banks[u])
                    twin(0, k, u)
                if there(k - 1):
                    route_e(0, k - 1, 1 - u)

            def high_g(t, u):
                act.wait_ge(gT_full, now[0] * TILES + t + 1)
                nc.scalar.copy(meta[:, bass.ds(t, 1), :, :], xg[:, u:u + 1, :, D:DW])
                nc.scalar.copy(gh[:, u, :], gT[u][:, 0:SLOT_T]).then_inc(gh_done, 1)

            def relu(t, u):
                step = now[0] * TILES + t
                for j in range(HC):
                    if j % 2 == 0:
                        act.wait_ge(z_full, 2 * step + j // 2 + 1)
                    if j == 0:
                        wait_some(act, rl0_done, step - 1)
                        wait_some(act, rl1_done, step - 1)
                    hidden = z[2 * u + j // 2][:, (j % 2) * SLOT_T:(j % 2 + 1) * SLOT_T]
                    ins = nc.scalar.activation(r[:, u, j, :], hidden, ACT.Relu, bias=b1_t[:, bass.ds(t, 1), j],
                                               scale=1.0 / WSCALE)
                    if j % 2:
                        ins.then_inc(r_done, 1)

            def tile_step(t, u, left, lead):
                if left >= 2:
                    high_g(t + 2, u)
                if left >= 1:
                    relu(t + 1, 1 - u)

            now = [0]
            act.wait_ge(const_done, N_CONSTS)
            route_beats(route_beat)
            turn_weights()
            prepare_weights()
            for ffn in range(2):
                now[0] = ffn
                act.wait_ge(table_done, ffn + 1)
                pad(act, mybir.EngineType.Activation, range(E // 2, E))
                high_g(0, 0)
                high_g(1, 1)
                act.wait_ge(b1t_done, ffn + 1)
                relu(0, 0)
                tiles(act, tile_step)
                if ffn == 0:
                    batches(act, attention_step)

        @block.vector
        def _(dve):
            def prepare_weights():
                dve.wait_ge(w1h_done, 1)
                nc.vector.scalar_tensor_tensor(out=w1l[:, :, :], in0=w1f[:, :, :], scalar=WSCALE, in1=w1h[:, :, :],
                                               op0=ALU.mult, op1=ALU.subtract).then_inc(low_weights_done, 1)
                dve.wait_ge(w2h_done, 1)
                nc.vector.scalar_tensor_tensor(out=w2l[:, :, :, :], in0=w2f[:, :, :, :], scalar=WSCALE,
                                               in1=w2h[:, :, :, :], op0=ALU.mult, op1=ALU.subtract
                                              ).then_inc(low_weights_done, 1)

            def split_b2():
                nc.vector.tensor_scalar(b2f[:, :, :], b2f[:, :, :], WSCALE, None, ALU.mult).then_inc(b2_chain, 1)
                dve.wait_ge(b2_chain, 1)
                nc.vector.tensor_copy(b2r[:, :, :], b2f[:, :, :]).then_inc(b2_chain, 1)
                dve.wait_ge(b2_chain, 2)
                nc.vector.scalar_tensor_tensor(out=b2hl[:, :, :], in0=b2r[:, :, :], scalar=neg_row[:, 0:1],
                                               in1=b2f[:, :, :], op0=ALU.mult, op1=ALU.add
                                              ).then_inc(low_weights_done, 1)

            def row_signs():
                dve.wait_ge(masks_done, 1)
                for k, (bit, neg) in enumerate(((16, neg_q), (8, neg_k))):
                    nc.vector.tensor_scalar(row_bit[:, k:k + 1], row_no[:, :], bit, None, ALU.bitwise_and
                                            ).then_inc(signs_chain, 1)
                    dve.wait_ge(signs_chain, 2 * k + 1)
                    nc.vector.tensor_scalar(neg[:, :], row_bit[:, k:k + 1], -1.0 / bit, None, ALU.mult
                                            ).then_inc(signs_chain, 1)
                dve.wait_ge(signs_chain, 4)

            def stats_to_scale(n, k, ins):
                k = [k * LN_LINKS]

                def link(ins):
                    ins.then_inc(ln_chain, 1)
                    k[0] = k[0] + 1

                def settle():
                    dve.wait_ge(ln_chain, k[0])

                link(ins)
                settle()
                moments(stats[:, n, :], mean[:, n], dif[:, n], var[:, n], link, settle)
                rsqrt(rstd[:, n], var[:, n], half[:, n], guess[:, n], newton[:, n], link, settle)

            def normalise(out, c, at):
                return nc.vector.tensor_scalar(out, xres[:, bass.ds(c, 1), :], mean[:, at:at + 1], rstd[:, at:at + 1],
                                               ALU.subtract, ALU.mult)

            def batch_stats(b, at):
                for t in range(NT_B):
                    last = nc.vector.bn_stats(stats[:, at + t, :], xres[:, bass.ds(b * NT_B + t, 1), :])
                return last

            def first_stats():
                for t in range(NT):
                    if t % (NT // 4) == 0:
                        dve.wait_ge(x_loaded[t // (NT // 4)], 16)
                    last = nc.vector.bn_stats(stats[:, t, :], xres[:, t, :])
                stats_to_scale(slice(0, NT), 0, last)

            def first_norm(k):
                if k >= RING:
                    dve.wait_ge(scattered[k % 2], scattered_by(0, k - RING + 2, k % 2))
                for t in range(k * W[0], (k + 1) * W[0]):
                    at = place_of(0, k, 0, t - k * W[0])
                    last = normalise(xn[:, at:at + 1, 0, 0:D], t, t)
                last.then_inc(ln_done, 1)

            def norms(i, u, project, route):
                b, m = i + 1, i - 2
                if project:
                    nc.vector.tensor_scalar(idle[:, :], mean[:, 0:1], 0.0, None, ALU.mult)
                    last = batch_stats(b, 0)
                else:
                    dve.wait_ge(res_done, m + 1)
                    last = batch_stats(m, NT_B)
                if route and project:
                    dve.wait_ge(beside_done, m + 1)
                stats_to_scale(slice(0 if project else NT_B, 2 * NT_B if route else NT_B), i + 2, last)

            def softmax_in(i):
                dve.wait_ge(sc_full, i + 1)
                if not (isinstance(i, int) and i == 0):
                    dve.wait_ge(mxd_done, i)
                    dve.wait_ge(pt_done, 2 * i)
                for h in range(2):
                    last = nc.vector.tensor_reduce(mx[:, 2 * h:2 * h + 2, :],
                                                   sc[:, 2 * h:2 * h + 2, :].rearrange("p g (q c) -> p g q c", q=NQ),
                                                   AX.X, ALU.max)
                last.then_inc(mx_done, 1)
                dve.wait_ge(mx_done, i + 1)
                for h in range(2):
                    nc.vector.tensor_tensor(
                        prob[:, 16 * h:16 * h + 16, :],
                        sc[:, 2 * h:2 * h + 2, :].rearrange("p g (q c) -> p (g q) c", q=NQ),
                        mx[:, 2 * h:2 * h + 2, :].rearrange("p g q -> p (g q)")[:, :, None]
                        .broadcast_to([P, 2 * NQ, 2 * QB]),
                        ALU.subtract).then_inc(sub_done, 1)

            def queries_keys(b, u):
                for k in range(1, 7):
                    dve.wait_ge(hi_done, 6 * b + k)
                    if k < 3:
                        n, neg, high = 2 * S, neg_q, hi_q[:, k - 1, :]
                        out_rows = qrow[:, u, 2 * k - 2:2 * k, :].rearrange("p g t -> p (g t)")
                    else:
                        n, neg, high = PADS, neg_k, hi_k[:, k - 3, :]
                        out_rows = krow[:, u, k - 3, :]
                    nc.vector.scalar_tensor_tensor(out=out_rows, in0=high, scalar=neg[:, 0:1], in1=slots[k][:, 0:n],
                                                   op0=ALU.mult, op1=ALU.add).then_inc(qk_done, 1)

            def attention_step(i, odd, fetch, project, middle, finish, route):
                b = i + 1
                if project:
                    add_rows(0, b, 1 - par(i, odd), i - 2 if route else None)
                if project or route:
                    norms(i, par(i, odd), project, route)
                if middle:
                    softmax_in(i)
                if finish:
                    dve.wait_ge(mden_done, i)
                    nc.vector.reciprocal(mrec[:, :], mden[:, :]).then_inc(mrec_done, 1)
                    dve.wait_ge(go_full, i)
                    nc.vector.tensor_tensor(g_out[:, :], gb[0:NH, 288:288 + D], headrow[:, :], ALU.mult
                                              ).then_inc(gm_done, 1)
                if middle:
                    if finish:
                        dve.wait_ge(o_full, i)
                    for h in range(2):
                        dve.wait_ge(exp_done, 2 * i + h + 1)
                        nc.vector.transpose(probT[:, 16 * h:16 * h + 16, :, :].rearrange("p n a q -> p (n a q)"),
                                            prob[:, 16 * h:16 * h + 16, :].rearrange("p n c -> p (n c)")
                                              ).then_inc(pt_done, 1)
                if project:
                    queries_keys(b, 1 - par(i, odd))
                if route:
                    choose(1, i - 2, par(i, odd), ob[:, LG_AT:LG_AT + W[1] * E])
                if middle:
                    dve.wait_ge(gs_full, i + 1)
                    nc.vector.tensor_reduce(g_neg[:, :], gb[0:NH, 0:S], AX.X, ALU.max, negate=True
                                              ).then_inc(gneg_done, 1)
                if route:
                    assign(1, i - 2, par(i, odd), ob[:, PX_AT:PX_AT + (W[1] + 1) * E])
                if middle:
                    dve.wait_ge(gexp_done, i + 1)
                    nc.vector.reciprocal(g_rec[:, :], g_sum[:, :]).then_inc(g_chain, 1)
                if finish:
                    dve.wait_ge(wo_full, i)
                    xr = xres[:, bass.ds((i - 1) * NT_B, NT_B), :]
                    nc.vector.tensor_tensor(xr, xr, pj[1][:, 0:S].rearrange("p (t d) -> p t d", t=NT_B),
                                            ALU.add).then_inc(res_done, 1)

            def choose(ffn, m, u, logits):
                n, w = BASE[ffn] + m, W[ffn]
                k = [n * ROUTE_LINKS]

                def link(ins):
                    ins.then_inc(route_chain, 1)
                    k[0] = k[0] + 1
                    dve.wait_ge(route_chain, k[0])

                def wide(a):
                    return a[:, 0:w, None].broadcast_to([P, w, E])

                tie_b = tie[:, None, :].broadcast_to([P, w, E])
                one1, one2 = (one[:, h, bass.ds(m * w, w), :] for h in range(TOPK))
                lg_, lg2_, eq_ = lg[:, 0:w, :], lg2[:, 0:w, :], eq[:, 0:w, :]
                m1_, m2_, pick_ = m1[:, 0:w], m2[:, 0:w], pick[:, 0:w]
                dve.wait_ge(lg_full, n + 1)
                link(nc.vector.tensor_tensor(lg_, logits.rearrange("p (t e) -> p t e", t=w),
                                             br_bc[:, None, :].broadcast_to([P, w, E]), ALU.add))
                link(nc.vector.tensor_reduce(m1_, lg_, AX.X, ALU.max))
                link(nc.vector.tensor_tensor(eq_, lg_, wide(m1), ALU.is_equal))
                link(nc.vector.tensor_tensor(eq_, eq_, tie_b, ALU.mult))
                link(nc.vector.tensor_reduce(pick_, eq_, AX.X, ALU.max))
                link(nc.vector.tensor_tensor(one1, tie_b, wide(pick), ALU.is_equal))
                link(nc.vector.scalar_tensor_tensor(out=lg2_, in0=one1, scalar=-BIG, in1=lg_, op0=ALU.mult,
                                                    op1=ALU.add))
                link(nc.vector.tensor_reduce(m2_, lg2_, AX.X, ALU.max))
                nc.vector.tensor_tensor(edelta[:, u, 0:w], m2_, m1_, ALU.subtract)
                link(nc.vector.tensor_tensor(eq_, lg2_, wide(m2), ALU.is_equal))
                link(nc.vector.tensor_tensor(eq_, eq_, tie_b, ALU.mult))
                link(nc.vector.tensor_reduce(pick_, eq_, AX.X, ALU.max))
                link(nc.vector.tensor_tensor(one2, tie_b, wide(pick), ALU.is_equal))
                nc.vector.tensor_tensor(both[:, u, 0:w, :], one1, one2, ALU.add).then_inc(delta_done, 1)

            def assign(ffn, m, u, px):
                n, w = BASE[ffn] + m, W[ffn]
                k = [n * PLACE_LINKS]

                def link(ins):
                    ins.then_inc(place_chain, 1)
                    k[0] = k[0] + 1

                def settle():
                    dve.wait_ge(place_chain, k[0])

                at = bass.ds(m * w, w)
                place_, eq_ = place[:, 0:w, :], eq[:, 0:w, :]
                dve.wait_ge(px_full, n + 1)
                link(nc.vector.tensor_tensor(place_, px[:, 0:w * E].rearrange("p (t e) -> p t e", t=w),
                                             taken[:, None, :].broadcast_to([P, w, E]), ALU.add))
                settle()
                link(nc.vector.tensor_tensor(taken[:, :], taken[:, :], px[:, w * E:w * E + E], ALU.add))
                link(nc.vector.tensor_tensor(eq_, place_, one[:, 0, at, :], ALU.mult))
                link(nc.vector.tensor_tensor(lg2[:, 0:w, :], place_, one[:, 1, at, :], ALU.mult))
                settle()
                link(nc.vector.tensor_reduce(slot[:, 0, at], eq_, AX.X, ALU.add))
                link(nc.vector.tensor_reduce(slot[:, 1, at], lg2[:, 0:w, :], AX.X, ALU.add))
                settle()
                if ffn == 0:
                    wait_some(dve, scattered[u], scattered_by(0, m, u))
                nc.vector.tensor_scalar(slot_i[:, u, :, 0:w], slot[:, :, at], 0.0, None, ALU.add).then_inc(slot_done, 1)
                dve.wait_ge(e2_done, n + 1)
                link(nc.vector.tensor_scalar(den[:, 0:w], e2[:, u, 0:w], 1.0, 2.0 * WSCALE, ALU.add, ALU.mult))
                settle()
                link(nc.vector.reciprocal(gate[:, 0, at], den[:, 0:w]))
                settle()
                link(nc.vector.tensor_tensor(gate[:, 1, at], gate[:, 0, at], e2[:, u, 0:w], ALU.mult))

            def route_beat(k, u):
                if there(k - 2):
                    assign(0, k - 2, u, banks[4 + u])
                if there(k - 1):
                    choose(0, k - 1, 1 - u, banks[3 - u][:, 0:W[0] * E])
                if k >= 1 and there(k + 1):
                    first_norm(k + 1)
                if k == RING:
                    split_b2()

            def tile_table(ffn):
                k = [ffn * TABLE_LINKS]

                def link(ins):
                    ins.then_inc(table_chain, 1)
                    k[0] = k[0] + 1
                    dve.wait_ge(table_chain, k[0])

                V = nc.vector
                link(V.tensor_tensor(cnt[:, :], taken[:, :], region0[:, :], ALU.subtract))
                link(V.tensor_scalar(cnt_f[:, :], cnt[:, :], float(SLOT_T - 1), None, ALU.add))
                link(V.tensor_copy(cnt_i[:, :], cnt_f[:, :]))
                link(V.tensor_scalar(cnt_i[:, :], cnt_i[:, :], SLOT_T.bit_length() - 1, None, ALU.logical_shift_right))
                link(V.tensor_copy(cnt[:, :], cnt_i[:, :]))
                link(V.tensor_tensor(tri_w[:, :, :], tri_e[:, :, :], cnt[:, None, :].broadcast_to([P, E, E]), ALU.mult))
                link(V.tensor_reduce(cum[:, :], tri_w[:, :, :], AX.X, ALU.add))
                link(V.tensor_tensor(past[:, :, :], tile_no[:, :, None].broadcast_to([P, TILES, E]),
                                     cum[:, None, :].broadcast_to([P, TILES, E]), ALU.is_ge))
                link(V.tensor_tensor(past_w[:, :, :], past[:, :, :], cnt[:, None, :].broadcast_to([P, TILES, E]),
                                     ALU.mult))
                link(V.tensor_reduce(t_e[:, :], past[:, :, :], AX.X, ALU.add))
                link(V.tensor_reduce(t_sum[:, :], past_w[:, :, :], AX.X, ALU.add))
                link(V.tensor_scalar(t_ok[:, :], past[:, :, E - 1], -1.0, 1.0, ALU.mult, ALU.add))
                link(V.tensor_tensor(t_sum[:, :], tile_no[:, :], t_sum[:, :], ALU.subtract))
                link(V.tensor_scalar(t_sum[:, :], t_sum[:, :], float(SLOT_T), None, ALU.mult))
                link(V.scalar_tensor_tensor(out=t_sum[:, :], in0=t_e[:, :], scalar=float(REGION), in1=t_sum[:, :],
                                            op0=ALU.mult, op1=ALU.add))
                link(V.tensor_tensor(t_sum[:, :], t_sum[:, :], t_ok[:, :], ALU.mult))
                link(V.scalar_tensor_tensor(out=tab_row[:, :], in0=past[0:1, :, E - 1], scalar=taken[0:1, 0:1],
                                            in1=t_sum[0:1, :], op0=ALU.mult, op1=ALU.add))
                link(V.scalar_tensor_tensor(out=t_off[:, :], in0=tile_no[:, :], scalar=float(SLOT_T),
                                            in1=past[:, :, E - 1], op0=ALU.mult, op1=ALU.mult))
                link(V.tensor_tensor(t_e[:, :], t_e[:, :], t_ok[:, :], ALU.mult))
                link(V.tensor_copy(t_pack[:, :], t_e[:, :]))
                for n in range(1, TURN + 1):
                    link(V.scalar_tensor_tensor(out=t_pack[:, 0:TILES - n], in0=t_e[:, n:TILES],
                                                scalar=float(1 << EB * n), in1=t_pack[:, 0:TILES - n],
                                                op0=ALU.mult, op1=ALU.add))
                V.tensor_copy(tab_e[:, :], t_pack[0:1, :])
                V.tensor_copy(pad_row[:, :], taken[0:1, :]).then_inc(table_done, 1)
                link(V.tensor_tensor(past[:, :, :], t_e[:, :, None].broadcast_to([P, TILES, E]),
                                     exp_no[:, None, :].broadcast_to([P, TILES, E]), ALU.is_equal))
                if ffn == 0:
                    dve.wait_ge(b1_done, 1)
                link(V.tensor_tensor(b1_w[:, :, :, :], past[:, :, None, :].broadcast_to([P, TILES, HC, E]),
                                     b1T[:, :].rearrange("p (e j) -> p j e", e=E)[:, None, :, :]
                                     .broadcast_to([P, TILES, HC, E]), ALU.mult))
                V.tensor_reduce(b1_t[:, :, :], b1_w[:, :, :, :], AX.X, ALU.add).then_inc(b1t_done, 1)
                if ffn == 0:
                    prepare_weights()
                low_g(ffn * TILES, 0)
                low_g(ffn * TILES + 1, 1)
                V.tensor_copy(taken[:, :], region0[:, :]).then_inc(taken_reset, 1)
                dve.wait_ge(taken_reset, ffn + 1)
                assert k[0] == (ffn + 1) * TABLE_LINKS

            def low_g(step, u):
                dve.wait_ge(gh_done, step + 1)
                nc.vector.tensor_tensor(gl[:, u, :], gT[u][:, 0:SLOT_T], gh[:, u, :], ALU.subtract).then_inc(gl_done, 1)

            def split_r(step, u):
                for h in range(2):
                    dve.wait_ge(r_done, 2 * step + h + 1)
                    nc.vector.tensor_copy(rh[:, u, 2 * h:2 * h + 2, :], r[:, u, 2 * h:2 * h + 2, :]
                                              ).then_inc(rh_done, 1)
                for h, done in enumerate((rl0_done, rl1_done)):
                    dve.wait_ge(rh_done, 2 * step + h + 1)
                    nc.vector.tensor_tensor(rl[:, u, 2 * h:2 * h + 2, :], r[:, u, 2 * h:2 * h + 2, :],
                                            rh[:, u, 2 * h:2 * h + 2, :], ALU.subtract).then_inc(done, 1)

            def result(t, u):
                step = now[0] * TILES + t
                dve.wait_ge(y_full, step + 1)
                wait_some(dve, stored[u], stored_before(t, u))
                nc.vector.tensor_scalar(y_row[:, u:u + 1, :], meta[:, bass.ds(t, 1), :, 0],
                                        t_off[:, bass.ds(t, 1)], None, ALU.add)
                for h in range(SH):
                    last = nc.vector.tensor_scalar(ysb[:, u, h, :], y[u][:, h * D:(h + 1) * D],
                                                   meta[:, bass.ds(t, 1), h, 1], None, ALU.mult)
                last.then_inc(y_done, 1)

            def stored_before(t, u):
                return 32 * (now[0] * ((TILES + 1 - u) // 2)) + (t - u) * 16

            def tile_step(t, u, left, lead):
                if left >= 2:
                    low_g(now[0] * TILES + t + 2, u)
                if left >= 1:
                    split_r(now[0] * TILES + t + 1, 1 - u)
                result(t, u)

            def add_rows(ffn, m, u, other=None):
                n = ffn * B + m
                if other is not None:
                    dve.wait_ge(res_done, other + 1)
                if ffn == 0:
                    rows = yg[:, u, :, :, :]
                    dve.wait_ge(fetched[u], 8 * TOPK * (n - u) + 16 * TOPK)
                else:
                    rows = y_last[:, m % LAST_U, :, :, :]
                    dve.wait_ge(fetched_last[m % LAST_U], 16 * TOPK * (m // LAST_U + 1))
                xr = xres[:, bass.ds(m * UT, UT), :]
                for h in range(TOPK):
                    last = nc.vector.tensor_tensor(xr, xr, rows[:, h, :, :], ALU.add)
                    if h == 0:
                        last.then_inc(add_chain, 1)
                        if other is not None:
                            batch_stats(other, NT_B).then_inc(beside_done, 1)
                        dve.wait_ge(add_chain, n + 1)
                last.then_inc(added, 1)
                dve.wait_ge(added, n + 1)

            first_stats()
            for k in range(2):
                first_norm(k)
            dve.wait_ge(router_loaded, 16 * 3)
            dve.wait_ge(const_done, N_CONSTS)
            nc.vector.tensor_copy(taken[:, :], region0[:, :]).then_inc(taken_done, 1)
            dve.wait_ge(taken_done, 1)
            now = [0]
            route_beats(route_beat)
            row_signs()
            for ffn in range(2):
                now[0] = ffn
                tile_table(ffn)
                split_r(ffn * TILES, 0)
                tiles(dve, tile_step)
                if ffn == 0:
                    batches(dve, attention_step)

            for m in range(B):
                add_rows(1, m, 0)

        @block.tensor
        def _(pe):
            def turn_weights():
                pe.wait_ge(weights_loaded, 16 * N_WEIGHT_LOADS)
                nc.tensor.transpose(gT[1][:, 0:E * HC], b1n[:, :], ident[0:E * HC, 0:E * HC]).then_inc(b1_full, 1)
                pe.wait_ge(b1_done, 1)
                for k in range(4):
                    last = nc.tensor.transpose(z[0][:, k * D:(k + 1) * D], wnat[:, k, :], ident[:, :])
                last.then_inc(wT_full, 1)
                pe.wait_ge(wT_done, 4)

            def slot_free(b, k, middle, route):
                if k == 2:
                    if not (isinstance(b, int) and b < 3):
                        pe.wait_ge(res_done, b - 2)
                elif k == 3:
                    if middle:
                        pe.wait_ge(sub_done, 2 * b)
                elif k == 6:
                    if route:
                        pe.wait_ge(xT_done, BASE[1] + b - 2)
                elif k >= 7:
                    pe.wait_ge(qk_done, 6 * b + k - 6)

            def attention_step(i, odd, fetch, project, middle, finish, route):
                b = i + 1
                if middle:
                    scores(i, par(i, odd))
                if finish:
                    weigh(i - 1, 1 - par(i, odd))
                if project:
                    pe.wait_ge(aln_done, b + 1)
                    if not (isinstance(b, int) and b == 0):
                        pe.wait_ge(vb_done, 3 * b - 1)
                    if not (isinstance(b, int) and b < 3):
                        pe.wait_ge(atT_done, b - 2)
                    for t in range(NT_B):
                        last = nc.tensor.transpose(pj[0][:, t * P:(t + 1) * P], axn[:, t, :], ident[:, :])
                    last.then_inc(aT_full, 1)
                    project_slots(b, (1, 2), middle, route)
                if route:
                    pe.wait_ge(sub_done, 2 * (i + 1) if middle else 2 * B)
                    route_t(1, i - 2, par(i, odd), banks[3])
                if project:
                    project_slots(b, range(3, 7), middle, route)
                if route:
                    if finish:
                        pe.wait_ge(ob_done, i)
                    route_l(1, i - 2, par(i, odd), ob[:, LG_AT:LG_AT + W[1] * E])
                if project:
                    project_slots(b, range(7, 10), middle, route)
                if finish:
                    pe.wait_ge(att_done, i)
                    pe.wait_ge(gm_done, i)
                    if project:
                        pe.wait_ge(vb_done, 3 * b + 1)
                    elif not (isinstance(i, int) and i < 2):
                        pe.wait_ge(atT_done, i - 1)
                    for t in range(NT_B):
                        nc.tensor.transpose(pj[0][:, t * P:(t + 1) * P], att[:, t, :], ident[:, :])
                    nc.tensor.matmul(pj[0][:, S:S + 1], g_out[:, :], ones[0:NH, :], start=True, stop=True
                                     ).then_inc(atT_full, 1)
                if middle:
                    u = par(i, odd)
                    pe.wait_ge(bd_done, 2 * i + 2)
                    if finish:
                        pe.wait_ge(gm_done, i)
                    for g in range(HG):
                        last = nc.tensor.matmul(gb[0:NH, 0:S], q0[:, u, g, :], krow[:, u, g, WIN:WIN + S],
                                                start=(g == 0), stop=(g == HG - 1))
                    last.then_inc(gs_full, 1)
                if route:
                    route_p(1, i - 2, par(i, odd), ob[:, PX_AT:PX_AT + (W[1] + 1) * E])
                if finish:
                    pe.wait_ge(atT_done, i)
                    if project:
                        pe.wait_ge(vb_done, 3 * b + 2)
                    elif not (isinstance(i, int) and i < 2):
                        pe.wait_ge(res_done, i - 1)
                    for t in range(NT_B):
                        last = nc.tensor.matmul(pj[1][:, t * D:(t + 1) * D], atT[:, t * P:(t + 1) * P], woT[:, :],
                                                start=True, stop=True)
                    last.then_inc(wo_full, 1)

            def scores(b, u):
                pe.wait_ge(qk_done, 6 * b + 6)
                pe.wait_ge(vp_done, b + 1)
                if not (isinstance(b, int) and b == 0):
                    pe.wait_ge(sub_done, 2 * b)
                if not (isinstance(b, int) and b < 3):
                    pe.wait_ge(xT_done, BASE[1] + b - 2)
                for g in range(HG):
                    nc.tensor.matmul(sc[:, g, :], identb[:, :], maskb[:, :, :], start=True, stop=False,
                                     skip_group_check=True)
                for q in range(NQ):
                    for turn in range(HG):
                        for h in range(HP):
                            g = (turn + h) % HG
                            sh = slice(QB * h, QB * h + QB)
                            last = nc.tensor.matmul(sc[sh, g, 2 * QB * q:2 * QB * (q + 1)],
                                                    qrow[sh, u, g, QB * q:QB * (q + 1)],
                                                    krow[sh, u, g, QB * q:QB * (q + 2)], start=False,
                                                    stop=(q == NQ - 1), skip_group_check=True)
                last.then_inc(sc_full, 1)

            def weigh(b, u):
                pe.wait_ge(p0_done, b + 1)
                pe.wait_ge(mxd_done, b + 1)
                pe.wait_ge(bd_done, 2 * b + 2)
                if not (isinstance(b, int) and b == 0):
                    pe.wait_ge(ob_done, b)
                if not (isinstance(b, int) and b < 2):
                    pe.wait_ge(slot_done, BASE[1] + b - 1)
                for t in range(NT_B):
                    for g in range(HG):
                        at = S0_AT + t * NH + g * HP
                        nc.tensor.matmul(ob[:, at:at + HP], qrow[:, u, g, t * P:(t + 1) * P], k0[:, u, g, :],
                                         start=True, stop=True)
                for t in range(NT_B):
                    last = nc.tensor.transpose(gb[:, 256 + t * NH:256 + (t + 1) * NH], g_prob[:, t * P:(t + 1) * P],
                                               ident[0:NH, 0:NH])
                last.then_inc(p0T_full, 1)
                for j in range(P // QB):
                    nc.tensor.matmul(ob[QB * j:QB * (j + 1), MT_AT:MT_AT + NM], fold[:, :], mxd[:, j:NQ:P // QB, :, :],
                                     start=True, stop=True)
                pe.wait_ge(pt_done, 2 * b + 2)
                for q in range(NQ):
                    for g in range(HG):
                        j, t = q % (P // QB), q // (P // QB)
                        at = (t * HG + g) * HP * (HD + 1)
                        for part in range(2):
                            last = nc.tensor.matmul(
                                ob[QB * j:QB * (j + 1), at:at + HP * (HD + 1)], probT[:, g * NQ + q, part, :],
                                vbd[:, u, q + part, g, :, :].rearrange("p h e -> p (h e)"),
                                start=(part == 0), stop=(part == 1))
                last.then_inc(o_full, 1)
                pe.wait_ge(p0T_done, b + 1)
                for t in range(NT_B):
                    last = nc.tensor.matmul(gb[0:NH, 288:288 + D], g_pT[:, t, :], vp[:, u, t, :],
                                            start=(t == 0), stop=(t == NT_B - 1))
                last.then_inc(go_full, 1)

            def project_slots(b, which, middle, route):
                pe.wait_ge(aT_done, b + 1)
                for k in which:
                    slot_free(b, k, middle, route)
                    o = slots[k]
                    if k < 3:
                        for n in range(2):
                            last = nc.tensor.matmul(o[:, n * S:(n + 1) * S], wqr[:, 2 * k - 2 + n, :],
                                                    aT[:, WIN:WIN + S], start=True, stop=True)
                    elif k < 7:
                        last = nc.tensor.matmul(o[:, 0:PADS], wkr[:, k - 3, :], aT[:, :], start=True, stop=True)
                    else:
                        if k == 7:
                            pe.wait_ge(aTr_done, b + 1)
                        for n in range(4 if k < 9 else 1):
                            q = 4 * (k - 7) + n
                            last = nc.tensor.matmul(
                                o[:, n * D:(n + 1) * D],
                                aTr[:, q, :, :].rearrange("p h k -> p (h k)"), wvT[:, :],
                                start=True, stop=True)
                        if k == 9:
                            for t in range(NT_B):
                                nc.tensor.matmul(o[:, (t + 1) * D:(t + 2) * D], aT[:, WIN + t * P:WIN + (t + 1) * P],
                                                 wvT[:, :], start=True, stop=True)
                            last = nc.tensor.matmul(o[:, 3 * D:4 * D], aT[:, WIN:WIN + 1].broadcast_to([P, P]),
                                                    wvT[:, :], start=True, stop=True)
                    last.then_inc(pj_full, 1)

            def route_t(ffn, m, u, bank):
                pe.wait_ge(ln_done, BASE[ffn] + m + 1)
                for t in range(W[ffn]):
                    last = nc.tensor.transpose(bank[:, t * P:(t + 1) * P], xn[:, place_of(ffn, m, u, t), 0, 0:D],
                                               ident[:, :])
                last.then_inc(pT_full, 1)

            def route_l(ffn, m, u, logits):
                pe.wait_ge(xT_done, BASE[ffn] + m + 1)
                for t in range(W[ffn]):
                    last = nc.tensor.matmul(logits[:, t * E:(t + 1) * E], xT[:, u, t * P:(t + 1) * P], wr[:, :],
                                            start=True, stop=True)
                last.then_inc(lg_full, 1)

            def route_p(ffn, m, u, px):
                w = W[ffn]
                pe.wait_ge(delta_done, BASE[ffn] + m + 1)
                wait_some(pe, slot_done, BASE[ffn] + m)
                for t in range(w):
                    o = px[:, t * E:(t + 1) * E]
                    nc.tensor.matmul(o, before[:, :], both[:, u, t, :], start=True, stop=(t == 0))
                    for earlier in range(t):
                        nc.tensor.matmul(o, ones16[:, :], both[:, u, earlier, :], start=False,
                                         stop=(earlier == t - 1))
                for t in range(w):
                    last = nc.tensor.matmul(px[:, w * E:w * E + E], ones16[:, :], both[:, u, t, :],
                                            start=(t == 0), stop=(t == w - 1))
                last.then_inc(px_full, 1)

            def route_beat(k, u):
                if there(k - 1):
                    route_l(0, k - 1, 1 - u, banks[3 - u][:, 0:W[0] * E])
                if there(k):
                    route_t(0, k, u, banks[u])
                if there(k - 1):
                    route_p(0, k - 1, 1 - u, banks[5 - u])

            def g_transposes(t, u):
                step = now[0] * TILES + t
                pe.wait_ge(loaded[u], 16 * (now[0] * ((TILES + 1 - u) // 2) + 1) + (t - u) * 8)
                wait_some(pe, gl_done, step - 1)
                for h in range(SH):
                    last = nc.tensor.transpose(gT[u][:, h * P:(h + 1) * P], xg[:, u, h, 0:D], ident[:, :])
                last.then_inc(gT_full, 1)

            def up(t, u, e):
                step = now[0] * TILES + t
                pe.wait_ge(gl_done, step + 1)
                for j in range(HC):
                    if j % 2 == 0:
                        wait_some(pe, r_done, 2 * (step - 2) + j // 2 + 1)
                    o = z[2 * u + j // 2][:, (j % 2) * SLOT_T:(j % 2 + 1) * SLOT_T]
                    wh, wl = (w[:, bass.ds(e, 1), j * P:(j + 1) * P] for w in (w1h, w1l))
                    nc.tensor.matmul(o, wh, gh[:, u, :], start=True, stop=False)
                    nc.tensor.matmul(o, wh, gl[:, u, :], start=False, stop=False)
                    last = nc.tensor.matmul(o, wl, gh[:, u, :], start=False, stop=True)
                    if j % 2:
                        last.then_inc(z_full, 1)

            def down(t, u, e):
                step = now[0] * TILES + t
                wait_some(pe, y_done, step - 1)
                for h in range(SH):
                    o = y[u][:, h * D:(h + 1) * D]
                    nc.tensor.matmul(o, ones16[0:2, :], b2hl[:, bass.ds(e, 1), :], start=True, stop=False)
                    for j in range(HC):
                        if h == 0 and j == 0:
                            pe.wait_ge(rl0_done, step + 1)
                        if h == 0 and j == 2:
                            pe.wait_ge(rl1_done, step + 1)
                        wh, wl = (w[:, bass.ds(e, 1), j, :] for w in (w2h, w2l))
                        a = slice(h * P, (h + 1) * P)
                        nc.tensor.matmul(o, rh[:, u, j, a], wh, start=False, stop=False)
                        nc.tensor.matmul(o, rh[:, u, j, a], wl, start=False, stop=False)
                        last = nc.tensor.matmul(o, rl[:, u, j, a], wh, start=False, stop=(j == HC - 1))
                last.then_inc(y_full, 1)

            def experts(t):
                v = pe.value_load(tab_e[0:1, bass.ds(t, 1)], min_val=0, max_val=(1 << (TURN + 1) * EB) - 1)
                return tuple((v >> EB * k) & ((1 << EB) - 1) for k in range(TURN + 1))

            e_of = [()]

            def tile_step(t, u, left, lead):
                if lead == 0:
                    e_of[0] = experts(t)
                if left >= 2:
                    g_transposes(t + 2, u)
                if left >= 1:
                    up(t + 1, 1 - u, e_of[0][lead + 1])
                down(t, u, e_of[0][lead])

            now = [0]
            pe.wait_ge(const_done, N_CONSTS)
            pe.wait_ge(router_loaded, 16 * 3)
            route_beats(route_beat)
            turn_weights()
            for ffn in range(2):
                now[0] = ffn
                pe.wait_ge(table_done, ffn + 1)
                first = experts(0)[0]
                g_transposes(0, 0)
                g_transposes(1, 1)
                if ffn == 0:
                    pe.wait_ge(low_weights_done, 3)
                up(0, 0, first)
                tiles(pe, tile_step)
                if ffn == 0:
                    pe.wait_ge(y_done, TILES)
                    batches(pe, attention_step)


_INS = ['L0_attn_x', 'L0_attn_Wq', 'L0_attn_Wk', 'L0_attn_Wv', 'L0_attn_Wo', 'L0_ffn_Wr', 'L0_ffn_br', 'L0_ffn_W1',
        'L0_ffn_b1', 'L0_ffn_W2', 'L0_ffn_b2']
_OUTS = [((16, 256, 128), 'float32')]


def kernel(**inputs):
    import numpy as _np
    import concourse.bacc as _bacc
    from concourse import mybir as _mybir
    from concourse.bass_utils import run_bass_kernel_spmd as _run

    nc = _bacc.Bacc("TRN2", target_bir_lowering=False, num_devices=1)
    arrays, args = {}, []
    for name in _INS:
        a = _np.ascontiguousarray(inputs[name])
        arrays[f"in_{name}_dram"] = a
        args.append(nc.dram_tensor(f"in_{name}_dram", a.shape, _mybir.dt.from_np(a.dtype), kind="ExternalInput").ap())
    for i, (shape, dtype) in enumerate(_OUTS):
        dt = _mybir.dt.from_np(_np.dtype(dtype))
        args.append(nc.dram_tensor(f"out_{i}_dram", shape, dt, kind="ExternalOutput").ap())
    macaron_kernel(nc, *args)
    r = _run(nc, [arrays], core_ids=[0])
    got = tuple(r.results[0][f"out_{i}_dram"] for i in range(len(_OUTS)))
    return got[0]
```
